# Optimizing a Trainium2 kernel written in Bass

```python
import numpy as np
import jax
import jax.numpy as jnp

def _softmax(x, axis=-1):
    return jax.nn.softmax(x, axis=axis)

def _gelu(x):
    return jax.nn.gelu(x, approximate=True)

def _silu(x):
    return jax.nn.silu(x)

def _sigmoid(x):
    return jax.nn.sigmoid(x)

def _layernorm(x, axis=-1, eps=1e-05):
    m = jnp.mean(x, axis=axis, keepdims=True)
    v = jnp.var(x, axis=axis, keepdims=True)
    return (x - m) / jnp.sqrt(v + eps)

def _scatter_add(tgt, idx, src, axis=0):
    return tgt.at[idx].add(src)

def _segment_sum(src, seg, n):
    return jax.ops.segment_sum(src, seg, n)
kernel_name = 'mk_xattn_ffn_d2_seqx_r2_a0cdf3'

def setup_inputs(seed: int=0):
    np.random.seed(seed)
    _w = jnp.asarray

    def _rec_inputs():
        import jax
        import jax.numpy as jnp
        _rk = jax.random.key(seed)
        x = -0.0002928 + 1 * jax.random.normal(jax.random.fold_in(_rk, 1), (2, 2048, 512), jnp.float32)
        _lenS = 2048 - jax.random.randint(jax.random.fold_in(_rk, 7), (2,), 0, max(1, 2048 // 4) + 1, jnp.int32)
        _lenS2 = 128 - jax.random.randint(jax.random.fold_in(_rk, 8), (2,), 0, max(1, 128 // 4) + 1, jnp.int32)
        _ctx_1024P = jax.random.normal(jax.random.fold_in(_rk, 11), (2, 16, 512), jnp.float32)
        _ctx_1024c = jax.random.dirichlet(jax.random.fold_in(_rk, 511), 0.3 * jnp.ones((16,), jnp.float32), (2, 128))
        _ctx_1024t = jnp.einsum('bsk,bkd->bsd', _ctx_1024c, _ctx_1024P)
        _ctx_1024t = _ctx_1024t * jax.lax.rsqrt(jnp.mean(jnp.square(_ctx_1024t)) + 1e-12) * 0.953939
        ctx_1024 = -1.39393e-06 + 0.999914 * (_ctx_1024t + 0.3 * jax.random.normal(jax.random.fold_in(_rk, 611), (2, 128, 512), jnp.float32))
        _validS = jnp.arange(2048)[None, :] < _lenS[:, None]
        _validS2 = jnp.arange(128)[None, :] < _lenS2[:, None]
        _causal = jnp.tril(jnp.ones((2048, 2048), dtype=bool))
        mask_BxS2_bf0 = jnp.logical_not(jnp.ones((2, 128), dtype=bool))
        mask_1x1xSxS2_bk0 = jnp.logical_not(jnp.broadcast_to(_validS2[0:1, None, None, :], (1, 1, 2048, 128)))
        return (x, ctx_1024, mask_BxS2_bf0, mask_1x1xSxS2_bk0)
    x, ctx_1024, mask_BxS2_bf0, mask_1x1xSxS2_bk0 = _rec_inputs()

    def _L0_xattn_setup():
        import jax, jax.numpy as jnp
        import numpy as np
        D_MODEL = 512
        N_HEADS = 16
        D_HEAD = 64
        EPS = 1e-05
        GROK_SCALE = 30.0
        ROPE_BASE = 10000.0

        def layer_norm(x, g, b):
            m = jnp.mean(x, axis=-1, keepdims=True)
            v = jnp.var(x, axis=-1, keepdims=True)
            return (x - m) * jax.lax.rsqrt(v + EPS) * g + b

        def rope(x):
            T, D = (x.shape[-2], x.shape[-1])
            inv_freq = 1.0 / ROPE_BASE ** (jnp.arange(0, D, 2, dtype=jnp.float32) / D)
            freqs = jnp.arange(T, dtype=jnp.float32)[:, None] * inv_freq[None, :]
            emb = jnp.repeat(freqs, 2, axis=-1)
            cos, sin = (jnp.cos(emb), jnp.sin(emb))
            xp = x.reshape(x.shape[:-1] + (D // 2, 2))
            rot = jnp.stack([-xp[..., 1], xp[..., 0]], axis=-1).reshape(x.shape)
            return x * cos + rot * sin
        key = jax.random.key(seed)
        ks = jax.random.split(key, 7)
        N, T = (2, 1024)
        f = lambda k, sh: jax.random.normal(k, sh, dtype=jnp.float32)
        return {'query_sequences': f(ks[0], (N, T, D_MODEL)), 'key_sequences': f(ks[1], (N, T, D_MODEL)), 'value_sequences': f(ks[2], (N, T, D_MODEL)), 'attention_mask': jnp.zeros((N, T), dtype=bool), 'Wq': f(ks[3], (D_MODEL, N_HEADS * D_HEAD)) * 0.02, 'Wk': f(ks[4], (D_MODEL, N_HEADS * D_HEAD)) * 0.02, 'Wv': f(ks[5], (D_MODEL, N_HEADS * D_HEAD)) * 0.02, 'Wo': f(ks[6], (N_HEADS * D_HEAD, D_MODEL)) * 0.02, 'ln_g': jnp.ones((D_MODEL,), dtype=jnp.float32), 'ln_b': jnp.zeros((D_MODEL,), dtype=jnp.float32)}
    _L0_xattn_all = _L0_xattn_setup()
    _L0_xattn_in = {k: v for k, v in _L0_xattn_all.items() if k in ('Wq', 'Wk', 'Wv', 'Wo', 'ln_g', 'ln_b')}
    del _L0_xattn_all

    def _L0_ffn_setup():
        import jax, jax.numpy as jnp
        import numpy as np
        QMAX = 127.0

        def _ste_round(v):
            return v + jax.lax.stop_gradient(jnp.round(v) - v)

        def _act_fake_quant(x, clip_factor):
            scale = jax.nn.sigmoid(clip_factor) * jnp.max(jnp.abs(x)) / QMAX
            return jnp.clip(_ste_round(x / scale), -QMAX - 1.0, QMAX) * scale

        def _weight_fake_quant(w):
            scale = jnp.max(jnp.abs(w), axis=1, keepdims=True) / QMAX
            return jnp.clip(_ste_round(w / scale), -QMAX - 1.0, QMAX) * scale
        key = jax.random.key(seed)
        k1, k2, k3, k4 = jax.random.split(key, 4)
        B, S, H, I = (8, 4096, 512, 1408)
        return {'x': jax.random.normal(k1, (B, S, H), dtype=jnp.float32), 'clip_x': jnp.full((1,), 4.0, dtype=jnp.float32), 'clip_down': jnp.full((1,), 4.0, dtype=jnp.float32), 'w_gate': jax.random.normal(k2, (I, H), dtype=jnp.float32) * 0.02, 'w_up': jax.random.normal(k3, (I, H), dtype=jnp.float32) * 0.02, 'w_down': jax.random.normal(k4, (H, I), dtype=jnp.float32) * 0.02}
    _L0_ffn_all = _L0_ffn_setup()
    _L0_ffn_in = {k: v for k, v in _L0_ffn_all.items() if k in ('clip_x', 'clip_down', 'w_gate', 'w_up', 'w_down')}
    del _L0_ffn_all

    def _L1_xattn_setup():
        import jax, jax.numpy as jnp
        import numpy as np
        import math
        B, S, D, H = (4, 1024, 512, 16)
        DV = D // H

        def _split_heads(x):
            b, s, _ = x.shape
            return x.reshape(b, s, H, DV).transpose(0, 2, 1, 3)
        key = jax.random.key(seed)
        ks = jax.random.split(key, 13)
        s = 1.0 / math.sqrt(D)
        inp = {'q': jax.random.normal(ks[0], (B, S, D), jnp.float32), 'k': jax.random.normal(ks[1], (B, S, D), jnp.float32), 'v': jax.random.normal(ks[2], (B, S, D), jnp.float32), 'mask': jax.random.bernoulli(ks[3], 0.1, (1, 1, S, S)), 'Wq': jax.random.normal(ks[4], (D, D), jnp.float32) * s, 'bq': jnp.zeros((D,), jnp.float32), 'Wk': jax.random.normal(ks[5], (D, D), jnp.float32) * s, 'bk': jnp.zeros((D,), jnp.float32), 'Wv': jax.random.normal(ks[6], (D, D), jnp.float32) * s, 'bv': jnp.zeros((D,), jnp.float32), 'Wo': jax.random.normal(ks[7], (D, D), jnp.float32) * s, 'bo': jnp.zeros((D,), jnp.float32)}
        return inp
    _L1_xattn_all = _L1_xattn_setup()
    _L1_xattn_in = {k: v for k, v in _L1_xattn_all.items() if k in ('Wq', 'bq', 'Wk', 'bk', 'Wv', 'bv', 'Wo', 'bo')}
    del _L1_xattn_all

    def _L1_ffn_setup():
        import jax, jax.numpy as jnp
        import numpy as np
        B, S, D, E = (4, 2048, 512, 8)
        key = jax.random.key(seed)
        k1, k2, k3, k4, k5 = jax.random.split(key, 5)
        scale = 1.0 / np.sqrt(D)
        return {'x': jax.random.normal(k1, (B, S, D), dtype=jnp.float32), 'Wg': jax.random.normal(k2, (D, D), dtype=jnp.float32) * scale, 'bg': jnp.zeros((D,), dtype=jnp.float32), 'We': jax.random.normal(k3, (E, D, D), dtype=jnp.float32) * scale, 'be': jnp.zeros((E, D), dtype=jnp.float32)}
    _L1_ffn_all = _L1_ffn_setup()
    _L1_ffn_in = {k: v for k, v in _L1_ffn_all.items() if k in ('Wg', 'bg', 'We', 'be')}
    del _L1_ffn_all
    return {'x': x, 'ctx_1024': ctx_1024, 'mask_BxS2_bf0': mask_BxS2_bf0, 'mask_1x1xSxS2_bk0': mask_1x1xSxS2_bk0, 'L0_xattn_Wq': _L0_xattn_in['Wq'], 'L0_xattn_Wk': _L0_xattn_in['Wk'], 'L0_xattn_Wv': _L0_xattn_in['Wv'], 'L0_xattn_Wo': _L0_xattn_in['Wo'], 'L0_xattn_ln_g': _L0_xattn_in['ln_g'], 'L0_xattn_ln_b': _L0_xattn_in['ln_b'], 'L0_ffn_clip_x': _L0_ffn_in['clip_x'], 'L0_ffn_clip_down': _L0_ffn_in['clip_down'], 'L0_ffn_w_gate': _L0_ffn_in['w_gate'], 'L0_ffn_w_up': _L0_ffn_in['w_up'], 'L0_ffn_w_down': _L0_ffn_in['w_down'], 'L1_xattn_Wq': _L1_xattn_in['Wq'], 'L1_xattn_bq': _L1_xattn_in['bq'], 'L1_xattn_Wk': _L1_xattn_in['Wk'], 'L1_xattn_bk': _L1_xattn_in['bk'], 'L1_xattn_Wv': _L1_xattn_in['Wv'], 'L1_xattn_bv': _L1_xattn_in['bv'], 'L1_xattn_Wo': _L1_xattn_in['Wo'], 'L1_xattn_bo': _L1_xattn_in['bo'], 'L1_ffn_Wg': _L1_ffn_in['Wg'], 'L1_ffn_bg': _L1_ffn_in['bg'], 'L1_ffn_We': _L1_ffn_in['We'], 'L1_ffn_be': _L1_ffn_in['be']}

def reference(x, ctx_1024, mask_BxS2_bf0, mask_1x1xSxS2_bk0, L0_xattn_Wq, L0_xattn_Wk, L0_xattn_Wv, L0_xattn_Wo, L0_xattn_ln_g, L0_xattn_ln_b, L0_ffn_clip_x, L0_ffn_clip_down, L0_ffn_w_gate, L0_ffn_w_up, L0_ffn_w_down, L1_xattn_Wq, L1_xattn_bq, L1_xattn_Wk, L1_xattn_bk, L1_xattn_Wv, L1_xattn_bv, L1_xattn_Wo, L1_xattn_bo, L1_ffn_Wg, L1_ffn_bg, L1_ffn_We, L1_ffn_be):
    import jax
    import jax.numpy as jnp

    def _L0_xattn_ref(query_sequences, key_sequences, value_sequences, attention_mask, Wq, Wk, Wv, Wo, ln_g, ln_b):
        import jax, jax.numpy as jnp
        import numpy as np
        D_MODEL = 512
        N_HEADS = 16
        D_HEAD = 64
        EPS = 1e-05
        GROK_SCALE = 30.0
        ROPE_BASE = 10000.0

        def layer_norm(x, g, b):
            m = jnp.mean(x, axis=-1, keepdims=True)
            v = jnp.var(x, axis=-1, keepdims=True)
            return (x - m) * jax.lax.rsqrt(v + EPS) * g + b

        def rope(x):
            T, D = (x.shape[-2], x.shape[-1])
            inv_freq = 1.0 / ROPE_BASE ** (jnp.arange(0, D, 2, dtype=jnp.float32) / D)
            freqs = jnp.arange(T, dtype=jnp.float32)[:, None] * inv_freq[None, :]
            emb = jnp.repeat(freqs, 2, axis=-1)
            cos, sin = (jnp.cos(emb), jnp.sin(emb))
            xp = x.reshape(x.shape[:-1] + (D // 2, 2))
            rot = jnp.stack([-xp[..., 1], xp[..., 0]], axis=-1).reshape(x.shape)
            return x * cos + rot * sin
        q = layer_norm(query_sequences, ln_g, ln_b)
        k = layer_norm(key_sequences, ln_g, ln_b)
        v = layer_norm(value_sequences, ln_g, ln_b)
        N, t, _ = q.shape
        T = k.shape[1]
        qh = (q @ Wq).reshape(N, t, N_HEADS, D_HEAD).transpose(0, 2, 1, 3)
        kh = (k @ Wk).reshape(N, T, N_HEADS, D_HEAD).transpose(0, 2, 1, 3)
        vh = (v @ Wv).reshape(N, T, N_HEADS, D_HEAD).transpose(0, 2, 1, 3)
        qh = rope(qh)
        kh = rope(kh)
        aw = jnp.einsum('nhtd,nhTd->nhtT', qh, kh)
        aw = aw * (1.0 / jnp.sqrt(jnp.float32(D_HEAD)))
        aw = GROK_SCALE * jnp.tanh(aw / GROK_SCALE)
        pad = attention_mask[:, None, None, :]
        causal = ~jnp.tril(jnp.ones((t, T), dtype=bool))
        aw = jnp.where(pad | causal, -jnp.inf, aw)
        p = jax.nn.softmax(aw, axis=-1)
        out = jnp.einsum('nhtT,nhTd->nhtd', p, vh)
        out = out.transpose(0, 2, 1, 3).reshape(N, t, N_HEADS * D_HEAD)
        return out @ Wo

    def _L0_ffn_ref(x, clip_x, clip_down, w_gate, w_up, w_down):
        import jax, jax.numpy as jnp
        import numpy as np
        QMAX = 127.0

        def _ste_round(v):
            return v + jax.lax.stop_gradient(jnp.round(v) - v)

        def _act_fake_quant(x, clip_factor):
            scale = jax.nn.sigmoid(clip_factor) * jnp.max(jnp.abs(x)) / QMAX
            return jnp.clip(_ste_round(x / scale), -QMAX - 1.0, QMAX) * scale

        def _weight_fake_quant(w):
            scale = jnp.max(jnp.abs(w), axis=1, keepdims=True) / QMAX
            return jnp.clip(_ste_round(w / scale), -QMAX - 1.0, QMAX) * scale
        xq = _act_fake_quant(x, clip_x[0])
        gate = jnp.einsum('bsh,ih->bsi', xq, _weight_fake_quant(w_gate))
        up = jnp.einsum('bsh,ih->bsi', xq, _weight_fake_quant(w_up))
        h = _act_fake_quant(jax.nn.silu(gate) * up, clip_down[0])
        return jnp.einsum('bsi,hi->bsh', h, _weight_fake_quant(w_down))

    def _L1_xattn_ref(q, k, v, mask, Wq, bq, Wk, bk, Wv, bv, Wo, bo):
        import jax, jax.numpy as jnp
        import numpy as np
        import math
        B, S, D, H = (4, 1024, 512, 16)
        DV = D // H

        def _split_heads(x):
            b, s, _ = x.shape
            return x.reshape(b, s, H, DV).transpose(0, 2, 1, 3)
        Q = _split_heads(q @ Wq.T + bq)
        K = _split_heads(k @ Wk.T + bk)
        V = _split_heads(v @ Wv.T + bv)
        scores = jnp.einsum('bhqd,bhkd->bhqk', Q, K) / math.sqrt(DV)
        scores = jnp.where(mask, jnp.asarray(1e-09, scores.dtype), scores)
        attn = jax.nn.softmax(scores, axis=-1)
        ctx = jnp.einsum('bhqk,bhkd->bhqd', attn, V)
        b = ctx.shape[0]
        ctx = ctx.transpose(0, 2, 1, 3).reshape(b, -1, H * DV)
        return ctx @ Wo.T + bo

    def _L1_ffn_ref(x, Wg, bg, We, be):
        import jax, jax.numpy as jnp
        import numpy as np
        B, S, D, E = (4, 2048, 512, 8)
        probs = jax.nn.softmax(x @ Wg + bg, axis=-1)
        idx = jnp.argmax(probs, axis=-1)
        p = jnp.take_along_axis(probs, idx[..., None], axis=-1)[..., 0]
        e_idx = idx % We.shape[0]
        h = jax.nn.relu(jnp.einsum('bsd,edf->besf', x, We) + be[None, :, None, :])
        onehot = jax.nn.one_hot(e_idx, We.shape[0], dtype=x.dtype)
        out = jnp.einsum('besf,bse->bsf', h, onehot) * p[..., None]
        return out
    x = x + _L0_xattn_ref(_layernorm(x, axis=-1), ctx_1024, ctx_1024, mask_BxS2_bf0, L0_xattn_Wq, L0_xattn_Wk, L0_xattn_Wv, L0_xattn_Wo, L0_xattn_ln_g, L0_xattn_ln_b)
    x = x + _L0_ffn_ref(_layernorm(x, axis=-1), L0_ffn_clip_x, L0_ffn_clip_down, L0_ffn_w_gate, L0_ffn_w_up, L0_ffn_w_down)
    x = x + _L1_xattn_ref(_layernorm(x, axis=-1), ctx_1024, ctx_1024, mask_1x1xSxS2_bk0, L1_xattn_Wq, L1_xattn_bq, L1_xattn_Wk, L1_xattn_bk, L1_xattn_Wv, L1_xattn_bv, L1_xattn_Wo, L1_xattn_bo)
    x = x + _L1_ffn_ref(_layernorm(x, axis=-1), L1_ffn_Wg, L1_ffn_bg, L1_ffn_We, L1_ffn_be)
    return x

_drawn_inputs = setup_inputs


def setup_inputs(seed=0):
    import zlib

    import numpy as np

    out = dict(_drawn_inputs(seed))
    spreads = {'L0_xattn_ln_g': (1.0, 0.563),
     'L0_xattn_ln_b': (0.0, 0.279),
     'L1_xattn_bq': (0.0, 0.451),
     'L1_xattn_bk': (0.0, 0.8),
     'L1_xattn_bv': (0.0, 0.1),
     'L1_xattn_bo': (0.0, 0.1),
     'L1_ffn_bg': (0.0, 0.8),
     'L1_ffn_be': (0.0, 0.8)}
    factors = {'L0_xattn_Wq': 4.993, 'L0_xattn_Wk': 5.012, 'L1_ffn_Wg': 4.06, 'L1_ffn_We': 4.019}
    for name, (base, spread) in spreads.items():
        noise = np.random.default_rng([zlib.crc32(name.encode()), seed]).standard_normal(out[name].shape)
        drawn = base * np.exp(spread * noise) if base else spread * noise
        out[name] = jnp.asarray(drawn.astype(out[name].dtype))
    for name, factor in factors.items():
        out[name] = (out[name] * factor).astype(out[name].dtype)
    return out
```

```python
import concourse.bass as bass
from concourse import mybir
from contextlib import ExitStack

F32 = mybir.dt.float32
BF16 = mybir.dt.bfloat16
I32 = mybir.dt.int32
U32 = mybir.dt.uint32
U8 = mybir.dt.uint8
ALU = mybir.AluOpType
ACT = mybir.ActivationFunctionType
AX = mybir.AxisListType

P = 128
B, S, D = 2, 2048, 512
KEYS = 128
TOK = B * S
TILES = TOK // P
CHUNK = 512
TPC = CHUNK // P
CHUNKS = TOK // CHUNK
CPB = CHUNKS // B
KB = D // P
LN_EPS = 1e-5
ROW = D + 4
COL_P, COL_MEAN, COL_RSTD = D, D + 1, D + 2

H0, DH0 = 16, 64
HD0 = H0 * DH0
PAIRS = H0 // 2
GROK = 30.0


class Chain:

    def __init__(self, eng, sem, base=0):
        self.eng, self.sem, self.base, self.k = eng, sem, base, 0

    def step(self, ins):
        ins.then_inc(self.sem, 1)
        self.k += 1

    def wait(self):
        self.eng.wait_ge(self.sem, self.base + self.k)


class Ring:

    def __init__(self, prefix, body):
        self.prefix, self.body = prefix, body
        assert len(prefix) % 2 == 0 and len(body) % 2 == 0 and prefix[-2:] == body[-2:]

    def full(self, n, pos):
        return len(self.prefix) + len(self.body) * n + pos + 1

    def emptied(self, n, seq, pos):
        who = seq[pos]
        return who, self.prefix.count(who) + self.body.count(who) * n + seq[:pos + 1].count(who)

    def reuse(self, n, seq, pos):
        if pos >= 2:
            return self.emptied(n, seq, pos - 2)
        last = self.prefix[-2:]
        who = last[pos]
        return who, self.prefix.count(who) + self.body.count(who) * n - last[pos + 1:].count(who)

    def prefix_full(self, pos):
        return pos + 1

    def prefix_emptied(self, pos):
        who = self.prefix[pos]
        return who, self.prefix[:pos + 1].count(who)


def rope_attention_stage(nc, io, xres, ident):
    SWAP = [i ^ 1 for i in range(32)]
    VW = DH0 + 1
    with ExitStack() as stage:
        def sb(name, shape, dt=F32):
            return stage.enter_context(nc.sbuf_tensor("a_" + name, shape, dt))

        def pb(name, shape, dt=F32):
            return stage.enter_context(nc.psum_tensor("a_" + name, shape, dt))

        def sem(name):
            return stage.enter_context(nc.semaphore("a_" + name))

        keysT = sb("keysT", [P, HD0 // P, B * KEYS])
        vals = sb("vals", [P, B, H0, VW])
        gain = sb("gain", [P, KB])
        shift = sb("shift", [P, KB])
        pad_u8 = sb("pad_u8", [P, B], U8)
        pad_bias = sb("pad_bias", [P, B])
        causal = sb("causal", [P, CPB, KEYS])
        rot = sb("rot", [P, 2, CHUNK])
        wq = sb("wq", [P, KB, HD0])
        wo = sb("wo", [P, HD0 // P, D])
        xn = sb("xn", [P, TPC, D])
        qT = sb("qT", [P, KB, CHUNK])
        stats = sb("stats", [P, TPC, 6])
        mv = sb("mv", [P, TPC, 2])
        var = sb("var", [P, TPC])
        rstd = sb("rstd", [P, TPC])
        minus_half = sb("minus_half", [P, TPC])
        swapped = sb("swapped", [P, CHUNK])
        turned = sb("turned", [P, CHUNK])
        recip = sb("recip", [P, 2, 4])
        held = sb("held", [P, 1])

        score_ps = pb("score_ps", [P, 2, 2, CHUNK])
        bank = [pb(f"bank{i}", [P, CHUNK]) for i in range(2)]
        pv_ps = [pb(f"pv_ps{i}", [P, CHUNK]) for i in range(2)]

        ld_small, ld_ctx, ld_wk, ld_wv = sem("ld_small"), sem("ld_ctx"), sem("ld_wk"), sem("ld_wv")
        ld_wq, ld_wo, ld_x = sem("ld_wq"), sem("ld_wo"), sem("ld_x")
        ld_rot, rot_used = sem("ld_rot"), sem("rot_used")
        prep = sem("prep")
        bank_full = sem("bank_full")
        freed = {"dve": sem("freed_by_dve"), "act": sem("freed_by_act")}
        var_ready, rstd_ready, xn_ready = sem("var_ready"), sem("rstd_ready"), sem("xn_ready")
        half_ready = sem("half_ready")
        keys_ready, vals_ready = sem("keys_ready"), sem("vals_ready")
        q_ready, score_full, capped, exped = sem("q_ready"), sem("score_full"), sem("capped"), sem("exped")
        masked, pv_full, normed = sem("masked"), sem("pv_full"), sem("normed")
        dve_step, act_step = sem("dve_step"), sem("act_step")
        k_done = sem("k_done")

        PRE = ["act"] * KB + ["dve"] * (HD0 // P) + ["act"] * (2 * B) + ["act"] * KB + ["dve"] * 2
        BODY = ["dve"] * 6 + ["act"] * KB + ["dve"] * 2 + ["act"] * (HD0 // P) + ["dve"] * TPC
        LAST = ["dve"] * 6 + ["act"] * (HD0 // P) + ["dve"] * TPC
        ring = Ring(PRE, BODY)
        PRE_T, PRE_K, PRE_V = 0, KB, KB + HD0 // P
        PRE_T0, PRE_Q0 = PRE_V + 2 * B, PRE_V + 2 * B + KB

        with ExitStack() as early:
            wk = early.enter_context(nc.sbuf_tensor("a_wk", [P, KB, HD0], F32))
            wv = early.enter_context(nc.sbuf_tensor("a_wv", [P, KB, HD0], F32))
            ctx_t = early.enter_context(nc.sbuf_tensor("a_ctx", [P, B, D], F32))
            ctxT = early.enter_context(nc.sbuf_tensor("a_ctxT", [P, KB, B * KEYS], F32))

            with nc.Block() as block:
                @block.sync
                def _(sp):
                    sp.dma_start(ctx_t[:], io["ctx"].rearrange("(b p) f -> p b f", p=P)).then_inc(ld_ctx, 16)
                    sp.dma_start(ident[:], io["ident"]).then_inc(ld_small, 16)
                    sp.dma_start(gain[:], io["ln_g"]).then_inc(ld_small, 16)
                    sp.dma_start(shift[:], io["ln_b"]).then_inc(ld_small, 16)
                    sp.dma_start(pad_u8[:], io["pad"]).then_inc(ld_small, 16)
                    sp.dma_start(causal[:], io["causal"]).then_inc(ld_small, 16)
                    sp.dma_start(rot[:], io["rot"][:, :, 0:CHUNK]).then_inc(ld_small, 16)
                    sp.dma_start(wk[:], io["wk0"].rearrange("(k p) n -> p k n", p=P)).then_inc(ld_wk, 16)
                    sp.dma_start(wv[:], io["wv0"].rearrange("(k p) n -> p k n", p=P)).then_inc(ld_wv, 16)
                    sp.dma_start(wq[:], io["wq0"].rearrange("(k p) n -> p k n", p=P)).then_inc(ld_wq, 16)
                    sp.dma_start(wo[:], io["wo0"].rearrange("(k p) n -> p k n", p=P)).then_inc(ld_wo, 16)
                    for c in range(CHUNKS):
                        sp.dma_start(xres[:, c * TPC:(c + 1) * TPC, 0:D],
                                     io["x"][c * CHUNK:(c + 1) * CHUNK, :].rearrange("(t p) f -> p t f", p=P)
                                     ).then_inc(ld_x, 16)

                @block.gpsimd
                def _(pool):
                    nc.gpsimd.memset(minus_half[:], -0.5).then_inc(half_ready, 1)
                    pool.wait_ge(half_ready, 1)
                    pool.wait_ge(var_ready, 1)
                    nc.gpsimd.tensor_tensor(rstd[:, 0:B], var[:, 0:B], minus_half[:, 0:B], ALU.pow).then_inc(rstd_ready, 1)

                @block.scalar
                def _(act):
                    act.wait_ge(ld_small, 96)
                    for k in range(KB):
                        act.wait_ge(bank_full, ring.prefix_full(PRE_T + k))
                        nc.scalar.activation(ctxT[:, k, :], bank[k % 2][:, 0:B * KEYS], ACT.Identity,
                                             bias=shift[:, k:k + 1], scale=gain[:, k:k + 1]).then_inc(freed["act"], 1)
                    for u in range(2 * B):
                        b, half = u // 2, u % 2
                        act.wait_ge(bank_full, ring.prefix_full(PRE_V + u))
                        nc.scalar.copy(vals[:, b, half * 8:(half + 1) * 8, 0:DH0],
                                       bank[(PRE_V + u) % 2][:].rearrange("p (h d) -> p h d", d=DH0)
                                       ).then_inc(freed["act"], 1)

                @block.vector
                def _(dve):
                    ch = Chain(dve, dve_step)
                    nc.vector.memset(vals[:, :, :, DH0:VW], 1.0).then_inc(vals_ready, 1)
                    dve.wait_ge(ld_ctx, 16)
                    for b in range(B):
                        ch.step(nc.vector.bn_stats(stats[:, b, :], ctx_t[:, b, :]))
                    ch.wait()
                    for b in range(B):
                        ch.step(nc.vector.bn_aggr(mv[:, b, :], stats[:, b, :]))
                    ch.wait()
                    nc.vector.tensor_scalar(var[:, 0:B], mv[:, 0:B, 1], LN_EPS, None, ALU.add).then_inc(var_ready, 1)
                    dve.wait_ge(rstd_ready, 1)
                    for b in range(B):
                        last = nc.vector.tensor_scalar(ctx_t[:, b, :], ctx_t[:, b, :], mv[:, b, 0:1],
                                                       rstd[:, b:b + 1], ALU.subtract, ALU.mult)
                    last.then_inc(xn_ready, 1)
                    dve.wait_ge(ld_small, 96)
                    ch.step(nc.vector.tensor_scalar(pad_bias[:], pad_u8[:], -1e30, None, ALU.mult))
                    cos_k = rot[:, 0, 0:KEYS].unsqueeze(1).to_broadcast([P, B, KEYS])
                    sin_k = rot[:, 1, 0:KEYS].unsqueeze(1).to_broadcast([P, B, KEYS])
                    for m in range(HD0 // P):
                        dve.wait_ge(bank_full, ring.prefix_full(PRE_K + m))
                        src = bank[(PRE_K + m) % 2][:, 0:B * KEYS]
                        src3 = src.rearrange("p (b k) -> p b k", b=B)
                        sw3 = swapped[:, 0:B * KEYS].rearrange("p (b k) -> p b k", b=B)
                        tu3 = turned[:, 0:B * KEYS].rearrange("p (b k) -> p b k", b=B)
                        ch.wait()
                        ch.step(nc.vector.stream_shuffle(swapped[:, 0:B * KEYS], src, SWAP))
                        nc.vector.tensor_tensor(tu3, src3, cos_k, ALU.mult).then_inc(freed["dve"], 1)
                        ch.wait()
                        ch.step(nc.vector.tensor_tensor(sw3, sw3, sin_k, ALU.mult))
                        ch.wait()
                        ch.step(nc.vector.tensor_tensor(keysT[:, m, :], turned[:, 0:B * KEYS], swapped[:, 0:B * KEYS], ALU.add))
                    ch.wait()

                @block.tensor
                def _(pe):
                    pe.wait_ge(ld_small, 96)
                    pe.wait_ge(xn_ready, 1)

                    def begin(u):
                        if u >= 2:
                            who, count = ring.prefix_emptied(u - 2)
                            pe.wait_ge(freed[who], count)
                        return bank[u % 2]

                    for k in range(KB):
                        out = begin(PRE_T + k)
                        for b in range(B):
                            last = nc.tensor.transpose(out[:, b * KEYS:(b + 1) * KEYS], ctx_t[:, b, k * P:(k + 1) * P], ident[:])
                        last.then_inc(bank_full, 1)
                    pe.wait_ge(freed["act"], KB)
                    pe.wait_ge(ld_wk, 16)
                    for m in range(HD0 // P):
                        out = begin(PRE_K + m)
                        for k in range(KB):
                            last = nc.tensor.matmul(out[:, 0:B * KEYS], wk[:, k, m * P:(m + 1) * P], ctxT[:, k, :],
                                                    start=(k == 0), stop=(k == KB - 1))
                        last.then_inc(bank_full, 1)
                    pe.wait_ge(ld_wv, 16)
                    for u in range(2 * B):
                        b, half = u // 2, u % 2
                        out = begin(PRE_V + u)
                        for k in range(KB):
                            last = nc.tensor.matmul(out[:], ctxT[:, k, b * KEYS:(b + 1) * KEYS],
                                                    wv[:, k, half * D:(half + 1) * D], start=(k == 0), stop=(k == KB - 1))
                        last.then_inc(bank_full, 1)

        probs = sb("probs", [P, 2, 2, CHUNK])
        q = sb("q", [P, PAIRS, CHUNK])
        attn = sb("attn", [P, TPC, HD0])
        attnT = sb("attnT", [P, HD0 // P, CHUNK])
        VAR0, ROT0 = 1, 96
        DVE_STEPS = 2 * TPC + 3 * PAIRS - 1
        with nc.Block() as block:
            @block.sync
            def _(sp):
                def load_rot(n, c):
                    sp.wait_ge(rot_used, n)
                    sp.dma_start(rot[:], io["rot"][:, :, bass.ds(c * CHUNK, CHUNK)]).then_inc(ld_rot, 16)
                with sp.Fori(1, CPB) as c:
                    load_rot(c, c)
                with sp.Fori(0, CPB) as c:
                    load_rot(c + CPB, c)

            @block.gpsimd
            def _(pool):
                with pool.Fori(0, CHUNKS) as n:
                    pool.wait_ge(var_ready, VAR0 + 1 + n)
                    nc.gpsimd.tensor_tensor(rstd[:], var[:], minus_half[:], ALU.pow).then_inc(rstd_ready, 1)

            @block.scalar
            def _(act):
                def to_qT(k, src):
                    nc.scalar.activation(qT[:, k, :], src[:], ACT.Identity, bias=shift[:, k:k + 1],
                                         scale=gain[:, k:k + 1]).then_inc(freed["act"], 1)

                for k in range(KB):
                    act.wait_ge(bank_full, ring.prefix_full(PRE_T0 + k))
                    to_qT(k, bank[k % 2])

                def body(n, b, last):
                    seq = LAST if last else BODY
                    for p in range(PAIRS):
                        pair = n * PAIRS + p
                        buf = probs[:, p % 2]
                        act.wait_ge(score_full, pair + 1)
                        if p >= 2:
                            act.wait_ge(pv_full, 2 * (pair - 1))
                        nc.scalar.activation(buf, score_ps[:, p % 2], ACT.Tanh, scale=1.0 / (DH0 ** 0.5 * GROK)).then_inc(capped, 1)
                        act.wait_ge(capped, pair + 1)
                        nc.scalar.activation(buf, buf, ACT.Exp, bias=pad_bias[:, b:b + 1], scale=GROK).then_inc(exped, 1)
                        if p == 6 and not last:
                            for k in range(KB):
                                act.wait_ge(bank_full, ring.full(n, 6 + k))
                                to_qT(k, bank[k % 2])
                    at = seq.index("act", 6 if last else 12)
                    for k in range(HD0 // P):
                        act.wait_ge(bank_full, ring.full(n, at + k))
                        nc.scalar.copy(attnT[:, k, :], bank[k % 2][:]).then_inc(freed["act"], 1)

                with act.Fori(0, CPB) as c:
                    body(c, 0, False)
                with act.Fori(0, CPB - 1) as c:
                    body(c + CPB, 1, False)
                body(CHUNKS - 1, 1, True)

            @block.vector
            def _(dve):
                ch = Chain(dve, dve_step)
                ch.base = 2 * B + 1 + 3 * (HD0 // P)

                def norm_stats(n, before):
                    dve.wait_ge(xn_ready, before)
                    for t in range(TPC):
                        ch.step(nc.vector.bn_stats(stats[:, t, :], xres[:, n * TPC + t, 0:D]))
                    ch.wait()
                    nc.vector.memset(held[:], 0.0)
                    for t in range(TPC):
                        ch.step(nc.vector.bn_aggr(mv[:, t, :], stats[:, t, :]))
                    ch.wait()
                    nc.vector.tensor_scalar(var[:], mv[:, :, 1], 1.0 + LN_EPS, LN_EPS * LN_EPS,
                                            ALU.mult, ALU.add).then_inc(var_ready, 1)

                def norm_rows(n):
                    dve.wait_ge(rstd_ready, VAR0 + 1 + n)
                    for t in range(TPC):
                        nc.vector.tensor_scalar(xn[:, t, :], xres[:, n * TPC + t, 0:D], mv[:, t, 0:1], rstd[:, t:t + 1],
                                                ALU.subtract, ALU.mult).then_inc(xn_ready, 1)

                def rotate(full, emptied, pos, before, last_of_chunk=False):
                    src = bank[pos % 2]
                    dve.wait_ge(bank_full, full)
                    if before is not None:
                        dve.wait_ge(q_ready, before)
                    nc.vector.tensor_tensor(turned[:], src[:], rot[:, 0, :], ALU.mult)
                    nc.vector.stream_shuffle(swapped[:], src[:], SWAP).then_inc(freed["dve"], 1)
                    dve.wait_ge(freed["dve"], emptied)
                    if last_of_chunk:
                        nc.vector.tensor_tensor(swapped[:], swapped[:], rot[:, 1, :], ALU.mult).then_inc(rot_used, 1)
                    else:
                        ch.step(nc.vector.tensor_tensor(swapped[:], swapped[:], rot[:, 1, :], ALU.mult))

                def rotated(n, p, last_of_chunk=False):
                    if last_of_chunk:
                        dve.wait_ge(rot_used, n + 1)
                    else:
                        ch.wait()
                    nc.vector.tensor_tensor(q[:, p, :], turned[:], swapped[:], ALU.add).then_inc(q_ready, 1)

                def mask(n, c, p):
                    dve.wait_ge(exped, n * PAIRS + p + 1)
                    first = probs[:, p % 2, :, 0:P]
                    nc.vector.tensor_tensor(first, first, causal[:, bass.ds(c, 1), :].to_broadcast([P, 2, KEYS]),
                                            ALU.mult).then_inc(masked, 1)

                def normalise(n, p):
                    for half in range(2):
                        got = pv_ps[half][:, 0:4 * VW].rearrange("p (t h d) -> p t h d", t=2, d=VW)
                        flat = pv_ps[half][:, 0:4 * VW].rearrange("p (a d) -> p a d", d=VW)
                        dve.wait_ge(pv_full, 2 * (n * PAIRS + p) + half + 1)
                        ch.step(nc.vector.reciprocal(recip[:, half, :], flat[:, :, DH0]))
                        ch.wait()
                        out = attn[:, 2 * half:2 * half + 2, p * P:(p + 1) * P].rearrange("p t (h d) -> p t h d", d=DH0)
                        scale = recip[:, half, :].rearrange("p (t h) -> p t h", h=2).unsqueeze(3).to_broadcast([P, 2, 2, DH0])
                        nc.vector.tensor_tensor(out, got[:, :, :, 0:DH0], scale, ALU.mult).then_inc(normed, 1)

                dve.wait_ge(ld_x, 16 * CHUNKS)
                norm_stats(0, 1)
                norm_rows(0)
                for p in range(2):
                    rotate(ring.prefix_full(PRE_Q0 + p), ring.prefix_emptied(PRE_Q0 + p)[1], PRE_Q0 + p, p or None)
                    rotated(0, p)
                start = ch.base + ch.k

                def body(n, c, last):
                    seq = LAST if last else BODY
                    ch.base, ch.k = start + n * DVE_STEPS, 0
                    for p in range(PAIRS):
                        mask(n, c, p)
                        if p >= 1:
                            normalise(n, p - 1)
                        if p == 0 and not last:
                            norm_stats(n + 1, 1 + TPC * (n + 1))
                        if p == 2 and not last:
                            norm_rows(n + 1)
                        if p < 6:
                            rotate(ring.full(n, p), ring.emptied(n, seq, p)[1], p, n * PAIRS + p + 2, p == 5)
                            rotated(n, p + 2, p == 5)
                        elif p == 7 and not last:
                            dve.wait_ge(ld_rot, 16 * (n + 1))
                            rotate(ring.full(n, 10), ring.emptied(n, seq, 10)[1], 10, (n + 1) * PAIRS)
                            rotated(n + 1, 0)
                    normalise(n, PAIRS - 1)
                    if not last:
                        rotate(ring.full(n, 11), ring.emptied(n, seq, 11)[1], 11, (n + 1) * PAIRS + 1)
                        rotated(n + 1, 1)
                    for t in range(TPC):
                        pos = len(seq) - TPC + t
                        dve.wait_ge(bank_full, ring.full(n, pos))
                        row = xres[:, n * TPC + t, 0:D]
                        nc.vector.tensor_tensor(row, bank[pos % 2][:], row, ALU.add).then_inc(freed["dve"], 1)
                    if not last:
                        assert ch.k == DVE_STEPS, ch.k

                with dve.Fori(0, CPB) as c:
                    body(c, c, False)
                with dve.Fori(0, CPB - 1) as c:
                    body(c + CPB, c, False)
                body(CHUNKS - 1, CPB - 1, True)

            @block.tensor
            def _(pe):
                def begin_prefix(u):
                    who, count = ring.prefix_emptied(u - 2)
                    pe.wait_ge(freed[who], count)
                    return bank[u % 2]

                def begin(n, seq, pos):
                    who, count = ring.reuse(n, seq, pos)
                    pe.wait_ge(freed[who], count)
                    return bank[pos % 2]

                def transposes(out, k):
                    for t in range(TPC):
                        last = nc.tensor.transpose(out[:, t * P:(t + 1) * P], xn[:, t, k * P:(k + 1) * P], ident[:])
                    last.then_inc(bank_full, 1)

                def project(out, p):
                    for k in range(KB):
                        last = nc.tensor.matmul(out[:], wq[:, k, p * P:(p + 1) * P], qT[:, k, :], start=(k == 0), stop=(k == KB - 1))
                    last.then_inc(bank_full, 1)

                def scores(n, b, p):
                    pair = n * PAIRS + p
                    pe.wait_ge(q_ready, pair + 1)
                    if p >= 2:
                        pe.wait_ge(capped, pair - 1)
                    for h in range(2):
                        rows = slice(h * DH0, (h + 1) * DH0)
                        last = nc.tensor.matmul(score_ps[:, p % 2, h, :], keysT[rows, p, b * KEYS:(b + 1) * KEYS], q[rows, p, :],
                                                start=True, stop=True)
                    last.then_inc(score_full, 1)

                def weigh(n, b, p):
                    pair = n * PAIRS + p
                    pe.wait_ge(masked, pair + 1)
                    for half in range(2):
                        if p >= 1:
                            pe.wait_ge(normed, 2 * (pair - 1) + half + 1)
                        for t in range(2):
                            for h in range(2):
                                at = (t * 2 + h) * VW
                                tok = (half * 2 + t) * P
                                last = nc.tensor.matmul(pv_ps[half][:, at:at + VW], probs[:, p % 2, h, tok:tok + P],
                                                        vals[:, b, 2 * p + h, :], start=True, stop=True)
                        last.then_inc(pv_full, 1)

                pe.wait_ge(xn_ready, 1 + TPC)
                for k in range(KB):
                    transposes(begin_prefix(PRE_T0 + k), k)
                pe.wait_ge(ld_wq, 16)
                pe.wait_ge(freed["act"], ring.prefix.count("act"))
                for p in range(2):
                    project(begin_prefix(PRE_Q0 + p), p)

                def body(n, b, last):
                    seq = LAST if last else BODY
                    for p in range(PAIRS):
                        scores(n, b, p)
                        if p >= 1:
                            weigh(n, b, p - 1)
                        if p < 6:
                            project(begin(n, seq, p), p + 2)
                        elif not last and p == 6:
                            pe.wait_ge(xn_ready, 1 + TPC * (n + 2))
                            for k in range(KB):
                                transposes(begin(n, seq, 6 + k), k)
                        elif not last:
                            pe.wait_ge(freed["act"], ring.emptied(n, seq, 9)[1])
                            project(begin(n, seq, 10), 0)
                    weigh(n, b, PAIRS - 1)
                    pos = 6
                    if not last:
                        project(begin(n, seq, 11), 1)
                        pos = 12
                    pe.wait_ge(normed, 2 * PAIRS * (n + 1))
                    for k in range(HD0 // P):
                        out = begin(n, seq, pos)
                        for t in range(TPC):
                            ins = nc.tensor.transpose(out[:, t * P:(t + 1) * P], attn[:, t, k * P:(k + 1) * P], ident[:])
                        ins.then_inc(bank_full, 1)
                        pos += 1
                    pe.wait_ge(freed["act"], ring.emptied(n, seq, pos - 1)[1])
                    pe.wait_ge(ld_wo, 16)
                    for t in range(TPC):
                        out = begin(n, seq, pos)
                        for k in range(HD0 // P):
                            ins = nc.tensor.matmul(out[:], attnT[:, k, t * P:(t + 1) * P], wo[:, k, :],
                                                   start=(k == 0), stop=(k == HD0 // P - 1))
                        ins.then_inc(bank_full, 1)
                        pos += 1

                with pe.Fori(0, CPB) as c:
                    body(c, 0, False)
                with pe.Fori(0, CPB - 1) as c:
                    body(c + CPB, 1, False)
                body(CHUNKS - 1, 1, True)


INNER = 1408
IT = INNER // P
QMAX = 127.0
MAGIC = 1.5 * 2.0 ** 23


def quantised_ffn_stage(nc, io, xres, ident):
    with ExitStack() as stage:
        def sb(name, shape, dt=F32):
            return stage.enter_context(nc.sbuf_tensor("b_" + name, shape, dt))

        def sem(name):
            return stage.enter_context(nc.semaphore("b_" + name))

        gateT = sb("gateT", [P, KB, INNER], BF16)
        upT = sb("upT", [P, KB, INNER], BF16)
        downT = sb("downT", [P, IT, D], BF16)
        gate_scale, up_scale, down_scale = sb("gate_scale", [P, IT]), sb("up_scale", [P, IT]), sb("down_scale", [P, KB])
        down_row = sb("down_row", [P, D])
        ident16 = sb("ident16", [P, P], BF16)
        clip = sb("clip", [P, 2])
        sigm = sb("sigm", [P, 2])
        mv = sb("mv", [P, TILES, 2])
        rstd = sb("rstd", [P, TILES])
        top = sb("top", [P, TILES])
        low = sb("low", [P, TILES])
        peak = sb("peak", [P, 1])
        peak_all = sb("peak_all", [P, 1])
        x_scale = sb("x_scale", [P, 1])
        inv_scale = sb("inv_scale", [P, 1])
        h_peak = sb("h_peak", [P, CHUNKS * IT])
        dve_step = sem("dve_step")
        tr_full, tr_freed = sem("tr_full"), sem("tr_freed")

        with ExitStack() as early:
            def esb(name, shape, dt=F32):
                return early.enter_context(nc.sbuf_tensor("b_" + name, shape, dt))

            raw = [esb("raw_gate", [P, IT, D]), esb("raw_up", [P, IT, D]), esb("raw_down", [P, KB, INNER])]
            ld_small, ld_w = sem("ld_small"), [sem(f"ld_w{i}") for i in range(3)]
            inv = [esb("inv_gate", [P, IT]), esb("inv_up", [P, IT]), esb("inv_down", [P, KB])]
            scale = [gate_scale, up_scale, down_scale]
            whole = [esb("whole_gate", [P, IT, D], BF16), esb("whole_up", [P, IT, D], BF16), esb("whole_down", [P, KB, INNER], BF16)]
            stats = esb("stats", [P, TILES, 6])
            half_minus = esb("half_minus", [P, TILES])
            ones = esb("ones", [P, P])
            diag = esb("diag", [P, P])
            tr_bank = [early.enter_context(nc.psum_tensor(f"b_tr{i}", [P, 4, P], BF16)) for i in range(2)]
            row_ps = early.enter_context(nc.psum_tensor("b_row", [P, D], F32))
            quantised, ident16_ready = sem("quantised"), sem("ident16_ready")
            var_ready, rstd_ready, half_ready = sem("var_ready"), sem("rstd_ready"), sem("half_ready")
            peak_ready, peak_all_ready, sig_exp = sem("peak_ready"), sem("peak_all_ready"), sem("sig_exp")
            diag_ready, diag_used = sem("diag_ready"), sem("diag_used")
            uses = [(w, r, range(KB)) for w in range(2) for r in range(IT)]
            uses += [(2, r, range(g, min(g + 4, IT))) for r in range(KB) for g in range(0, IT, 4)]
            rows_before = [0, IT, 2 * IT]

            with nc.Block() as block:
                @block.sync
                def _(sp):
                    sp.dma_start(clip[:], io["clip"].partition_broadcast(P)).then_inc(ld_small, 16)
                    sp.dma_start(raw[0][:], io["w_gate"].rearrange("(i p) f -> p i f", p=P)).then_inc(ld_w[0], 16)
                    sp.dma_start(raw[1][:], io["w_up"].rearrange("(i p) f -> p i f", p=P)).then_inc(ld_w[1], 16)
                    sp.dma_start(raw[2][:], io["w_down"].rearrange("(k p) i -> p k i", p=P)).then_inc(ld_w[2], 16)

                @block.gpsimd
                def _(pool):
                    nc.gpsimd.memset(half_minus[:], -0.5).then_inc(half_ready, 1)
                    pool.wait_ge(half_ready, 1)
                    pool.wait_ge(var_ready, 1)
                    nc.gpsimd.tensor_tensor(rstd[:], rstd[:], half_minus[:], ALU.pow).then_inc(rstd_ready, 1)
                    pool.wait_ge(peak_ready, 1)
                    nc.gpsimd.partition_all_reduce(peak_all[:], peak[:], P, bass.bass_isa.ReduceOp.max).then_inc(peak_all_ready, 1)

                @block.scalar
                def _(act):
                    act.wait_ge(ld_small, 16)
                    nc.scalar.activation(sigm[:], clip[:], ACT.Exp, scale=-1.0).then_inc(sig_exp, 1)
                    for u, (w, r, cols) in enumerate(uses):
                        act.wait_ge(tr_full, u + 1)
                        if w < 2:
                            out = (gateT, upT)[w][:, :, r * P:(r + 1) * P]
                        else:
                            out = downT[:, cols[0]:cols[-1] + 1, r * P:(r + 1) * P]
                        nc.scalar.copy(out, tr_bank[u % 2][:, 0:len(cols), :]).then_inc(tr_freed, 1)

                @block.vector
                def _(dve):
                    ch = Chain(dve, dve_step)
                    nc.vector.tensor_copy(ident16[:], ident[:]).then_inc(ident16_ready, 1)
                    ch.step(nc.vector.memset(ones[:], 1.0))
                    for w in range(3):
                        dve.wait_ge(ld_w[w], 16)
                        ch.step(nc.vector.tensor_reduce(inv[w][:], raw[w][:], AX.X, ALU.max, apply_absolute_value=True))
                        ch.wait()
                        ch.step(nc.vector.tensor_scalar(scale[w][:], inv[w][:], 1.0 / QMAX, None, ALU.mult))
                        ch.wait()
                        ch.step(nc.vector.reciprocal(inv[w][:], scale[w][:]))
                        ch.wait()
                        rows = raw[w].shape[1]
                        for r in range(rows):
                            ch.step(nc.vector.tensor_scalar(raw[w][:, r, :], raw[w][:, r, :], inv[w][:, r:r + 1], MAGIC, ALU.mult, ALU.add))
                        ch.wait()
                        for r in range(rows):
                            nc.vector.tensor_scalar(whole[w][:, r, :], raw[w][:, r, :], MAGIC, QMAX, ALU.subtract, ALU.min).then_inc(quantised, 1)
                    for k in range(KB):
                        if k:
                            dve.wait_ge(diag_used, k)
                        nc.vector.tensor_scalar(diag[:], ident[:], down_scale[:, k:k + 1], None, ALU.mult).then_inc(diag_ready, 1)
                    for n in range(CHUNKS):
                        rows = xres[:, n * TPC:(n + 1) * TPC, 0:D]
                        at = slice(n * TPC, (n + 1) * TPC)
                        for t in range(n * TPC, (n + 1) * TPC):
                            ch.step(nc.vector.bn_stats(stats[:, t, :], xres[:, t, 0:D]))
                        ch.step(nc.vector.tensor_reduce(top[:, at], rows, AX.X, ALU.max))
                        ch.step(nc.vector.tensor_reduce(low[:, at], rows, AX.X, ALU.min))
                    ch.wait()
                    for t in range(TILES):
                        ch.step(nc.vector.bn_aggr(mv[:, t, :], stats[:, t, :]))
                    ch.wait()
                    nc.vector.tensor_scalar(rstd[:], mv[:, :, 1], LN_EPS, None, ALU.add).then_inc(var_ready, 1)
                    ch.step(nc.vector.tensor_tensor(top[:], top[:], mv[:, :, 0], ALU.subtract))
                    ch.step(nc.vector.tensor_tensor(low[:], mv[:, :, 0], low[:], ALU.subtract))
                    ch.wait()
                    ch.step(nc.vector.tensor_tensor(top[:], top[:], low[:], ALU.max))
                    dve.wait_ge(rstd_ready, 1)
                    ch.wait()
                    ch.step(nc.vector.tensor_tensor(top[:], top[:], rstd[:], ALU.mult))
                    ch.wait()
                    nc.vector.tensor_reduce(peak[:], top[:], AX.X, ALU.max).then_inc(peak_ready, 1)
                    dve.wait_ge(sig_exp, 1)
                    ch.step(nc.vector.tensor_scalar(clip[:], sigm[:], 1.0, None, ALU.add))
                    ch.wait()
                    ch.step(nc.vector.reciprocal(sigm[:], clip[:]))
                    dve.wait_ge(peak_all_ready, 1)
                    ch.wait()
                    ch.step(nc.vector.tensor_scalar(x_scale[:], peak_all[:], sigm[:, 0:1], 1.0 / QMAX, ALU.mult, ALU.mult))
                    ch.wait()
                    ch.step(nc.vector.reciprocal(inv_scale[:], x_scale[:]))
                    ch.step(nc.vector.tensor_scalar(gate_scale[:], gate_scale[:], x_scale[:], None, ALU.mult))
                    ch.step(nc.vector.tensor_scalar(up_scale[:], up_scale[:], x_scale[:], None, ALU.mult))
                    ch.wait()
                    ch.step(nc.vector.tensor_scalar(rstd[:], rstd[:], inv_scale[:], None, ALU.mult))
                    dve.wait_ge(diag_used, KB)
                    ch.step(nc.vector.tensor_copy(down_row[:], row_ps[:]))

                @block.tensor
                def _(pe):
                    pe.wait_ge(ident16_ready, 1)
                    for u, (w, r, cols) in enumerate(uses):
                        pe.wait_ge(quantised, rows_before[w] + r + 1)
                        if u >= 2:
                            pe.wait_ge(tr_freed, u - 1)
                        for j, c in enumerate(cols):
                            last = nc.tensor.transpose(tr_bank[u % 2][:, j, :], whole[w][:, r, c * P:(c + 1) * P], ident16[:])
                        last.then_inc(tr_full, 1)
                    for k in range(KB):
                        pe.wait_ge(diag_ready, k + 1)
                        last = nc.tensor.matmul(row_ps[:, k * P:(k + 1) * P], ones[:], diag[:], start=True, stop=True)
                        last.then_inc(diag_used, 1)

        hidden = sb("hidden", [P, 2, IT, CHUNK])
        spilled = [sem("spilled0"), sem("spilled1")]
        with ExitStack() as mid:
            def msb(name, shape, dt=F32):
                return mid.enter_context(nc.sbuf_tensor("b_" + name, shape, dt))

            scaled = msb("scaled", [P, 2, D])
            whole_x = msb("whole_x", [P, TPC, D], BF16)
            xT = msb("xT", [P, 2, KB, CHUNK], BF16)
            silu = msb("silu", [P, 2, CHUNK])
            scratch = msb("scratch", [P, 6])
            bank = [mid.enter_context(nc.psum_tensor(f"b_bank{i}", [P, CHUNK], BF16)) for i in range(2)]
            gate_ps = mid.enter_context(nc.psum_tensor("b_gate", [P, 2, CHUNK], F32))
            up_ps = mid.enter_context(nc.psum_tensor("b_up", [P, 2, CHUNK], F32))
            x_full, x_freed, x_quant = sem("x_full"), sem("x_freed"), sem("x_quant")
            gate_full, up_full = sem("gate_full"), sem("up_full")
            gate_used, up_used = sem("gate_used"), sem("up_used")
            dve_q = sem("dve_q")
            h_seen = sem("h_seen")
            Q_STEPS = 2 * TPC

            def all_chunks(eng, body):
                with eng.Fori(0, CHUNKS // 2 - 1) as i:
                    for j in range(2):
                        body(2 * i + j, j, False)
                body(CHUNKS - 2, 0, False)
                body(CHUNKS - 1, 1, True)

            with nc.Block() as block:
                @block.sync
                def _(sp):
                    with sp.Fori(0, CHUNKS // 2 - 1) as i:
                        for j in range(2):
                            n = 2 * i + j
                            sp.wait_ge(up_used, 2 + IT * (n + 1))
                            sp.dma_start(io["hidden"][bass.ds(n, 1)].rearrange("o p f -> (o p) f"),
                                         hidden[:, j].rearrange("p i t -> p (i t)")).then_inc(spilled[j], 16)
                    for j in range(2):
                        sp.wait_ge(spilled[j], 16 * (CHUNKS // 2))

                @block.scalar
                def _(act):
                    nc.scalar.copy(scratch[:, 0:1], clip[:, 0:1]).then_inc(gate_used, 1)
                    nc.scalar.copy(scratch[:, 1:2], clip[:, 0:1]).then_inc(gate_used, 1)
                    for k in range(KB):
                        act.wait_ge(x_full, k + 1)
                        nc.scalar.copy(xT[:, 0, k, :], bank[k % 2][:]).then_inc(x_freed, 1)

                    def body(n, j, last):
                        for i in range(IT):
                            k = n * IT + i
                            b = (j * IT + i) % 2
                            act.wait_ge(gate_full, k + 1)
                            act.wait_ge(up_used, k + 1)
                            nc.scalar.activation(silu[:, b, :], gate_ps[:, b, :], ACT.Silu, scale=gate_scale[:, i:i + 1]).then_inc(gate_used, 1)
                            if i >= 7 and not last:
                                act.wait_ge(x_full, KB * (n + 1) + i - 6)
                                nc.scalar.copy(xT[:, 1 - j, i - 7, :], bank[(i - 7) % 2][:]).then_inc(x_freed, 1)

                    all_chunks(act, body)

                @block.vector
                def _(dve):
                    ch = Chain(dve, dve_q)
                    nc.vector.memset(scratch[:, 2:3], 0.0).then_inc(up_used, 1)
                    nc.vector.memset(scratch[:, 3:4], 0.0).then_inc(up_used, 1)
                    nc.vector.memset(scratch[:, 4:5], 0.0).then_inc(spilled[0], 16)
                    nc.vector.memset(scratch[:, 5:6], 0.0).then_inc(spilled[1], 16)

                    def quantise(n, t, done):
                        buf = scaled[:, t % 2, :]
                        if done is not None:
                            dve.wait_ge(x_quant, done)
                        at = n * TPC + t
                        ch.step(nc.vector.tensor_scalar(buf, xres[:, at, 0:D], mv[:, at, 0:1], rstd[:, bass.ds(at, 1)], ALU.subtract, ALU.mult))
                        ch.wait()
                        ch.step(nc.vector.tensor_scalar(buf, buf, MAGIC, MAGIC + QMAX, ALU.add, ALU.min))
                        ch.wait()
                        nc.vector.tensor_scalar(whole_x[:, t, :], buf, MAGIC - QMAX - 1.0, MAGIC, ALU.max, ALU.subtract).then_inc(x_quant, 1)

                    for t in range(TPC):
                        quantise(0, t, t - 1 if t >= 2 else None)

                    def body(n, j, last):
                        ch.base, ch.k = Q_STEPS * (n + 1), 0

                        def greatest(i):
                            dve.wait_ge(up_used, n * IT + i + 3)
                            nc.vector.tensor_reduce(h_peak[:, bass.ds(n * IT + i, 1)], hidden[:, j, i, :], AX.X, ALU.max,
                                                    apply_absolute_value=True).then_inc(h_seen, 1)

                        dve.wait_ge(spilled[j], 16 * ((n + 2 - j) // 2) if isinstance(n, int) else 8 * (n + 2 - j))
                        for i in range(IT):
                            k = n * IT + i
                            b = (j * IT + i) % 2
                            dve.wait_ge(up_full, k + 1)
                            dve.wait_ge(gate_used, k + 3)
                            nc.vector.scalar_tensor_tensor(hidden[:, j, i, :], up_ps[:, b, :], up_scale[:, i:i + 1], silu[:, b, :],
                                                           ALU.mult, ALU.mult).then_inc(up_used, 1)
                            if i >= 1:
                                greatest(i - 1)
                            if i < TPC and not last:
                                quantise(n + 1, i, TPC * (n + 1) + i - 1)
                        greatest(IT - 1)

                    all_chunks(dve, body)

                @block.tensor
                def _(pe):
                    def turn(n, k, count):
                        if count is not None:
                            pe.wait_ge(x_freed, count)
                        for t in range(TPC):
                            last = nc.tensor.transpose(bank[k % 2][:, t * P:(t + 1) * P], whole_x[:, t, k * P:(k + 1) * P], ident16[:])
                        last.then_inc(x_full, 1)

                    pe.wait_ge(x_quant, TPC)
                    for k in range(KB):
                        turn(0, k, k - 1 if k >= 2 else None)

                    def body(n, j, last):
                        pe.wait_ge(x_freed, KB * (n + 1))
                        for i in range(IT):
                            b = (j * IT + i) % 2
                            for ps, w, full, used in ((gate_ps, gateT, gate_full, gate_used), (up_ps, upT, up_full, up_used)):
                                pe.wait_ge(used, n * IT + i + 1)
                                for k in range(KB):
                                    ins = nc.tensor.matmul(ps[:, b, :], w[:, k, i * P:(i + 1) * P], xT[:, j, k, :],
                                                           start=(k == 0), stop=(k == KB - 1))
                                ins.then_inc(full, 1)
                            if i == 6 and not last:
                                pe.wait_ge(x_quant, TPC * (n + 2))
                            if i >= 6 and i < 6 + KB and not last:
                                turn(n + 1, i - 6, KB * (n + 1) + i - 7)

                    all_chunks(pe, body)

        with ExitStack() as late:
            def lsb(name, shape, dt=F32):
                return late.enter_context(nc.sbuf_tensor("b_" + name, shape, dt))

            whole_h = lsb("whole_h", [P, 2, IT, CHUNK], BF16)
            h_scale, h_inv = lsb("h_scale", [P, 1]), lsb("h_inv", [P, 1])
            minus_magic = lsb("minus_magic", [P, 1])
            delta = lsb("delta", [P, 2, D])
            out_ps = late.enter_context(nc.psum_tensor("b_out", [P, 2, D], F32))
            h_peak_ready, h_all_ready = sem("h_peak_ready"), sem("h_all_ready")
            rounded, whole_ready = sem("rounded"), sem("whole_ready")
            out_full, out_freed, added = sem("out_full"), sem("out_freed"), sem("added")
            reloaded = [sem("reloaded0"), sem("reloaded1")]
            h_step = sem("h_step")
            magic_set = sem("magic_set")
            LOOPS = CHUNKS // 2 - 1

            def order(eng, body):
                body(0, 0, CHUNKS - 2, None, True)
                body(1, 1, CHUNKS - 1, 0, True)
                with eng.Fori(0, LOOPS - 1) as i:
                    body(2 * i + 2, 0, 2 * i, i, True)
                    body(2 * i + 3, 1, 2 * i + 1, i + 1, True)
                body(CHUNKS - 2, 0, CHUNKS - 4, LOOPS - 1, True)
                body(CHUNKS - 1, 1, CHUNKS - 3, None, False)

            with nc.Block() as block:
                @block.sync
                def _(sp):
                    with sp.Fori(0, LOOPS) as i:
                        for j in range(2):
                            sp.wait_ge(whole_ready, 2 * i + j + 1)
                            sp.dma_start(hidden[:, j].rearrange("p i t -> p (i t)"),
                                         io["hidden"][bass.ds(2 * i + j, 1)].rearrange("o p f -> (o p) f")).then_inc(reloaded[j], 16)

                @block.gpsimd
                def _(pool):
                    pool.wait_ge(h_peak_ready, 1)
                    nc.gpsimd.partition_all_reduce(peak_all[:], peak[:], P, bass.bass_isa.ReduceOp.max).then_inc(h_all_ready, 1)

                    def body(q, j, n, load, more):
                        for t in range(TPC):
                            pool.wait_ge(out_freed, q * TPC + t + 1)
                            row = xres[:, n * TPC + t, 0:D]
                            nc.gpsimd.tensor_tensor(row, row, delta[:, t % 2, :], ALU.add).then_inc(added, 1)

                    order(pool, body)

                @block.scalar
                def _(act):
                    act.wait_ge(magic_set, 1)

                    def body(q, j, n, load, more):
                        act.wait_ge(rounded, q + 1)
                        if not isinstance(q, int) or q >= 2:
                            act.wait_ge(out_full, TPC * (q - 1))
                        nc.scalar.activation(whole_h[:, j], hidden[:, j], ACT.Identity, bias=minus_magic[:]).then_inc(whole_ready, 1)

                    order(act, body)

                @block.vector
                def _(dve):
                    ch = Chain(dve, h_step)
                    nc.vector.memset(minus_magic[:], -MAGIC).then_inc(magic_set, 1)
                    dve.wait_ge(h_seen, CHUNKS * IT)
                    nc.vector.tensor_reduce(peak[:], h_peak[:], AX.X, ALU.max).then_inc(h_peak_ready, 1)
                    dve.wait_ge(h_all_ready, 1)
                    ch.step(nc.vector.tensor_scalar(h_scale[:], peak_all[:], sigm[:, 1:2], 1.0 / QMAX, ALU.mult, ALU.mult))
                    ch.wait()
                    ch.step(nc.vector.reciprocal(h_inv[:], h_scale[:]))
                    ch.step(nc.vector.tensor_scalar(down_row[:], down_row[:], h_scale[:], None, ALU.mult))
                    ch.wait()

                    def round_chunk(j):
                        ch.step(nc.vector.tensor_scalar(hidden[:, j], hidden[:, j], h_inv[:], QMAX, ALU.mult, ALU.min))
                        ch.wait()
                        nc.vector.tensor_scalar(hidden[:, j], hidden[:, j], -QMAX - 1.0, MAGIC, ALU.max, ALU.add).then_inc(rounded, 1)

                    round_chunk(0)
                    base = ch.k

                    def body(q, j, n, load, more):
                        ch.base, ch.k = q + base, 0
                        if more:
                            if load is not None:
                                dve.wait_ge(reloaded[1 - j], 16 * (load + 1))
                            round_chunk(1 - j)
                        for t in range(TPC):
                            dve.wait_ge(out_full, q * TPC + t + 1)
                            if not isinstance(q, int) or q or t >= 2:
                                dve.wait_ge(added, q * TPC + t - 1)
                            nc.vector.tensor_tensor(delta[:, t % 2, :], out_ps[:, t % 2, :], down_row[:], ALU.mult).then_inc(out_freed, 1)

                    order(dve, body)

                @block.tensor
                def _(pe):
                    def body(q, j, n, load, more):
                        pe.wait_ge(whole_ready, q + 1)
                        for t in range(TPC):
                            if not isinstance(q, int) or q or t >= 2:
                                pe.wait_ge(out_freed, q * TPC + t - 1)
                            for i in range(IT):
                                ins = nc.tensor.matmul(out_ps[:, t % 2, :], whole_h[:, j, i, t * P:(t + 1) * P], downT[:, i, :],
                                                       start=(i == 0), stop=(i == IT - 1))
                            ins.then_inc(out_full, 1)

                    order(pe, body)


H1, DH1 = 16, 32
VW1 = DH1 + 1
QUADS = H1 // 4


def masked_attention_stage(nc, io, xres, ident):
    with ExitStack() as stage:
        def sb(name, shape, dt=F32):
            return stage.enter_context(nc.sbuf_tensor("c_" + name, shape, dt))

        def pb(name, shape, dt=F32):
            return stage.enter_context(nc.psum_tensor("c_" + name, shape, dt))

        def sem(name):
            return stage.enter_context(nc.semaphore("c_" + name))

        keys = sb("keys", [P, B, QUADS, 4 * KEYS])
        vals = sb("vals", [P, B, H1, VW1])
        bias = sb("bias", [P, 2, KB])
        rows = sb("rows", [P, 2, D])
        wk, wv = sb("wk", [P, KB, D]), sb("wv", [P, KB, D])
        wq, wo = sb("wq", [P, KB, D]), sb("wo", [P, KB, D])
        ctx_t = sb("ctx", [P, B, D])
        ctxT = sb("ctxT", [P, KB, B * KEYS])
        masks = sb("masks", [P, 2, TPC, KEYS], U8)
        tiny = sb("tiny", [P, 1])
        xn = sb("xn", [P, TPC, D])
        xT = sb("xT", [P, KB, CHUNK])
        q = sb("q", [P, 2, KB, CHUNK])
        stats = sb("stats", [P, TPC, 6])
        mv = sb("mv", [P, TPC, 2])
        var, rstd, minus_half = sb("var", [P, TPC]), sb("rstd", [P, TPC]), sb("minus_half", [P, TPC])
        top = sb("top", [P, H1])
        held = sb("held", [P, 1])
        probs = sb("probs", [P, 2, H1, KEYS])
        probsT = sb("probsT", [P, H1, P])
        recip = sb("recip", [P, 2, H1 // 2])
        attn = sb("attn", [P, D])
        attnT = sb("attnT", [P, KB, P])

        score_ps = pb("score", [P, H1, KEYS])
        bank = [pb(f"bank{i}", [P, CHUNK]) for i in range(2)]
        pv_ps = [pb(f"pv{i}", [P, CHUNK]) for i in range(2)]

        ld_ctx, ld_small, ld_wk, ld_wv, ld_wq, ld_wo = (sem("ld_" + x) for x in ("ctx", "small", "wk", "wv", "wq", "wo"))
        ld_mask, mask_used = sem("ld_mask"), sem("mask_used")
        bank_full = sem("bank_full")
        freed = {"dve": sem("freed_by_dve"), "act": sem("freed_by_act")}
        set_up, half_ready = sem("set_up"), sem("half_ready")
        var_ready, rstd_ready, xn_ready, bo_added = sem("var_ready"), sem("rstd_ready"), sem("xn_ready"), sem("bo_added")
        score_full, shifted, exped = sem("score_full"), sem("shifted"), sem("exped")
        pv_full, normed = sem("pv_full"), sem("normed")
        dve_step, prep_step = sem("dve_step"), sem("prep_step")

        W_USES = ["act", "act", "act", "act", "act", "dve"]
        PRE = ["act"] * KB + ["dve"] * KB + ["dve"] * B + ["act"] * KB + ["dve"] * KB
        FIRST = ["act"] * 4 + ["act"] * KB + W_USES + W_USES + ["dve"] * KB
        BODY = W_USES * 2 + ["act"] * KB + W_USES + W_USES + ["dve"] * KB
        LAST = W_USES * 4 + W_USES + ["act", "dve"]
        ring = Ring(PRE + FIRST, BODY)
        PRE_K, PRE_V, PRE_T, PRE_Q = KB, 2 * KB, 2 * KB + B, 3 * KB + B
        DVE_STEPS, DVE_HEAD = TPC + 2 * TPC + 2 * TPC, 2

        def plan(n, first, last):
            out, pos = [], 0
            for t in range(TPC):
                step = {}
                if t == 2 and not last:
                    step["T"] = pos
                    pos += KB
                if not (first and t == 0):
                    if first and t == 1:
                        step["PT"] = [pos, pos + 1, pos + 2, pos + 3]
                        pos += 4
                    else:
                        step["PT"] = [pos, pos + 1, pos + 3, pos + 4]
                        step["OT"], step["O"] = pos + 2, pos + 5
                        pos += 6
                if t == TPC - 1 and not last:
                    step["Q"] = pos
                    pos += KB
                out.append(step)
            if last:
                out.append({"PT": [pos, pos + 1, pos + 3, pos + 4], "OT": pos + 2, "O": pos + 5})
                out.append({"OT": pos + 6, "O": pos + 7})
            return out

        class Uses:

            def __init__(self, n, first, last):
                self.first, self.n = first, 0 if first else n - 1
                self.seq = FIRST if first else LAST if last else BODY

            def bank(self, pos):
                return bank[pos % 2]

            def full(self, pos):
                return len(PRE) + pos + 1 if self.first else ring.full(self.n, pos)

            def emptied(self, pos):
                return ring.prefix_emptied(len(PRE) + pos) if self.first else ring.emptied(self.n, self.seq, pos)

            def reuse(self, pos):
                return ring.prefix_emptied(len(PRE) + pos - 2) if self.first else ring.reuse(self.n, self.seq, pos)

        def all_chunks(eng, body):
            body(0, 0, True, False)
            with eng.Fori(0, CHUNKS // 2 - 1) as i:
                body(2 * i + 1, 1, False, False)
                body(2 * i + 2, 0, False, False)
            body(CHUNKS - 1, 1, False, True)

        def batch(n):
            return n // CPB

        with nc.Block() as block:
            @block.sync
            def _(sp):
                sp.dma_start(ctx_t[:], io["ctx"].rearrange("(b p) f -> p b f", p=P)).then_inc(ld_ctx, 16)
                sp.dma_start(bias[:], io["qk_bias"]).then_inc(ld_small, 16)
                sp.dma_start(rows[:, 0, :], io["bv"].partition_broadcast(P)).then_inc(ld_small, 16)
                sp.dma_start(rows[:, 1, :], io["bo"].partition_broadcast(P)).then_inc(ld_small, 16)
                for w, name, s in ((wk, "wk1", ld_wk), (wv, "wv1", ld_wv), (wq, "wq1", ld_wq), (wo, "wo1", ld_wo)):
                    sp.dma_start(w[:], io[name].rearrange("(k p) n -> p k n", p=P)).then_inc(s, 16)

                def body(n, j, first, last):
                    if not first:
                        sp.wait_ge(mask_used, TPC * (n - 1) + 1)
                    c = n % CPB
                    sp.dma_start(masks[:, j], io["mask"][bass.ds(c * CHUNK, CHUNK), :].rearrange("(t p) k -> p t k", p=P)).then_inc(ld_mask, 16)

                all_chunks(sp, body)

            @block.gpsimd
            def _(pool):
                nc.gpsimd.memset(minus_half[:], -0.5).then_inc(half_ready, 1)
                pool.wait_ge(half_ready, 1)
                pool.wait_ge(ld_small, 48)
                with pool.Fori(0, CHUNKS) as n:
                    pool.wait_ge(var_ready, n + 1)
                    nc.gpsimd.tensor_tensor(rstd[:], var[:], minus_half[:], ALU.pow).then_inc(rstd_ready, 1)
                    pool.wait_ge(xn_ready, TPC * (n + 1))
                    for t in range(TPC):
                        row = xres[:, n * TPC + t, 0:D]
                        nc.gpsimd.tensor_tensor(row, row, rows[:, 1, :], ALU.add).then_inc(bo_added, 1)

            @block.scalar
            def _(act):
                def copy(out, full, pos):
                    act.wait_ge(bank_full, full)
                    nc.scalar.copy(out, bank[pos % 2][:]).then_inc(freed["act"], 1)

                for k in range(KB):
                    act.wait_ge(bank_full, ring.prefix_full(k))
                    nc.scalar.copy(ctxT[:, k, :], bank[k % 2][:, 0:B * KEYS]).then_inc(freed["act"], 1)
                for k in range(KB):
                    copy(xT[:, k, :], ring.prefix_full(PRE_T + k), PRE_T + k)

                def step(u, s):
                    for g in range(QUADS):
                        if "PT" in s:
                            pos = s["PT"][g]
                            out = probsT[:, 4 * g:4 * g + 4, :].rearrange("p h t -> p (h t)")
                            copy(out, u.full(pos), pos)
                        if g == 1 and "OT" in s:
                            copy(attnT[:].rearrange("p k t -> p (k t)"), u.full(s["OT"]), s["OT"])

                def body(n, j, first, last):
                    u = Uses(n, first, last)
                    steps = plan(n, first, last)
                    for t in range(TPC):
                        s = steps[t]
                        tile = n * TPC + t
                        if "T" in s:
                            for k in range(KB):
                                copy(xT[:, k, :], u.full(s["T"] + k), s["T"] + k)
                        step(u, s)
                        act.wait_ge(shifted, tile + 1)
                        nc.scalar.activation(probs[:, t % 2], probs[:, t % 2], ACT.Exp).then_inc(exped, 1)
                    for s in steps[TPC:]:
                        step(u, s)

                all_chunks(act, body)

            @block.vector
            def _(dve):
                ch = Chain(dve, prep_step)
                nc.vector.memset(tiny[:], 1e-9).then_inc(set_up, 1)
                nc.vector.memset(vals[:, :, :, DH1:VW1], 1.0).then_inc(set_up, 1)
                nc.vector.memset(keys[:], 0.0).then_inc(set_up, 1)

                def norm_stats(n, before):
                    if before is not None:
                        dve.wait_ge(xn_ready, before)
                    for t in range(TPC):
                        ch.step(nc.vector.bn_stats(stats[:, t, :], xres[:, n * TPC + t, 0:D]))
                    ch.wait()
                    nc.vector.memset(held[:], 0.0)
                    for t in range(TPC):
                        ch.step(nc.vector.bn_aggr(mv[:, t, :], stats[:, t, :]))
                    ch.wait()
                    nc.vector.tensor_scalar(var[:], mv[:, :, 1], LN_EPS, None, ALU.add).then_inc(var_ready, 1)

                def norm_rows(n):
                    dve.wait_ge(rstd_ready, n + 1)
                    for t in range(TPC):
                        nc.vector.tensor_scalar(xn[:, t, :], xres[:, n * TPC + t, 0:D], mv[:, t, 0:1], rstd[:, t:t + 1],
                                                ALU.subtract, ALU.mult).then_inc(xn_ready, 1)

                def queries(j, k, full, pos):
                    dve.wait_ge(bank_full, full)
                    nc.vector.tensor_scalar(q[:, j, k, :], bank[pos % 2][:], bias[:, 0, k:k + 1], DH1 ** -0.5,
                                            ALU.add, ALU.mult).then_inc(freed["dve"], 1)

                norm_stats(0, None)
                norm_rows(0)
                dve.wait_ge(ld_small, 48)
                dve.wait_ge(set_up, 3)
                for g in range(QUADS):
                    dve.wait_ge(bank_full, ring.prefix_full(PRE_K + g))
                    src = bank[(PRE_K + g) % 2]
                    for h in range(4):
                        part = slice(h * DH1, (h + 1) * DH1)
                        last = nc.vector.tensor_scalar(keys[part, :, g, h * KEYS:(h + 1) * KEYS],
                                                       src[part, 0:B * KEYS].rearrange("p (b k) -> p b k", b=B),
                                                       bias[part, 1, g:g + 1], None, ALU.add)
                    last.then_inc(freed["dve"], 1)
                for b in range(B):
                    dve.wait_ge(bank_full, ring.prefix_full(PRE_V + b))
                    nc.vector.tensor_tensor(vals[:, b, :, 0:DH1], bank[(PRE_V + b) % 2][:].rearrange("p (h d) -> p h d", d=DH1),
                                            rows[:, 0, :].rearrange("p (h d) -> p h d", d=DH1), ALU.add).then_inc(freed["dve"], 1)
                for k in range(KB):
                    queries(0, k, ring.prefix_full(PRE_Q + k), PRE_Q + k)
                ch = Chain(dve, dve_step)

                def shift(n, j, t):
                    tile = n * TPC + t
                    dve.wait_ge(score_full, tile + 1)
                    nc.vector.memset(held[:], 0.0)
                    ch.step(nc.vector.copy_predicated(score_ps[:], masks[:, j, t, :].unsqueeze(1).to_broadcast([P, H1, KEYS]),
                                                      tiny[:].unsqueeze(2).to_broadcast([P, H1, KEYS])))
                    ch.wait()
                    nc.vector.tensor_reduce(top[:], score_ps[:], AX.X, ALU.max).then_inc(mask_used, 1)
                    dve.wait_ge(mask_used, tile + 1)
                    nc.vector.tensor_tensor(probs[:, t % 2], score_ps[:], top[:].unsqueeze(2).to_broadcast([P, H1, KEYS]),
                                            ALU.subtract).then_inc(shifted, 1)

                def normalise(tile):
                    for half in range(2):
                        got = pv_ps[half][:, 0:8 * VW1].rearrange("p (h d) -> p h d", d=VW1)
                        dve.wait_ge(pv_full, 2 * tile + half + 1)
                        ch.step(nc.vector.reciprocal(recip[:, half, :], got[:, :, DH1]))
                        ch.wait()
                        nc.vector.tensor_tensor(attn[:, half * 256:(half + 1) * 256].rearrange("p (h d) -> p h d", d=DH1),
                                                got[:, :, 0:DH1], recip[:, half, :].unsqueeze(2).to_broadcast([P, 8, DH1]),
                                                ALU.mult).then_inc(normed, 1)

                def add_out(u, pos, tile):
                    dve.wait_ge(bank_full, u.full(pos))
                    dve.wait_ge(bo_added, tile + 1)
                    row = xres[:, tile, 0:D]
                    nc.vector.tensor_tensor(row, bank[pos % 2][:], row, ALU.add).then_inc(freed["dve"], 1)

                def body(n, j, first, last):
                    u = Uses(n, first, last)
                    steps = plan(n, first, last)
                    ch.base, ch.k = (0, 0) if first else (n * DVE_STEPS - DVE_HEAD, 0)
                    dve.wait_ge(ld_mask, 16 * (n + 1))
                    for t, s in enumerate(steps):
                        tile = n * TPC + t
                        if t < TPC:
                            shift(n, j, t)
                        if "PT" in s:
                            normalise(tile - 1)
                        if "O" in s:
                            add_out(u, s["O"], tile - 2)
                        if t == 0 and not last:
                            norm_stats(n + 1, TPC * (n + 1))
                        if t == 1 and not last:
                            norm_rows(n + 1)
                        if "Q" in s:
                            for k in range(KB):
                                queries(1 - j, k, u.full(s["Q"] + k), s["Q"] + k)
                    assert last or ch.k == DVE_STEPS - (DVE_HEAD if first else 0), ch.k

                all_chunks(dve, body)

            @block.tensor
            def _(pe):
                def begin(reuse, pos):
                    if reuse is not None:
                        pe.wait_ge(freed[reuse[0]], reuse[1])
                    return bank[pos % 2]

                def prefix(pos):
                    return begin(ring.prefix_emptied(pos - 2) if pos >= 2 else None, pos)

                def transposes(out, k):
                    for t in range(TPC):
                        last = nc.tensor.transpose(out[:, t * P:(t + 1) * P], xn[:, t, k * P:(k + 1) * P], ident[:])
                    last.then_inc(bank_full, 1)

                def project(out, m):
                    for k in range(KB):
                        last = nc.tensor.matmul(out[:], wq[:, k, m * P:(m + 1) * P], xT[:, k, :], start=(k == 0), stop=(k == KB - 1))
                    last.then_inc(bank_full, 1)

                pe.wait_ge(ld_ctx, 16)
                for k in range(KB):
                    out = prefix(k)
                    for b in range(B):
                        last = nc.tensor.transpose(out[:, b * KEYS:(b + 1) * KEYS], ctx_t[:, b, k * P:(k + 1) * P], ident[:])
                    last.then_inc(bank_full, 1)
                pe.wait_ge(freed["act"], KB)
                pe.wait_ge(ld_wk, 16)
                for m in range(KB):
                    out = prefix(PRE_K + m)
                    for k in range(KB):
                        last = nc.tensor.matmul(out[:, 0:B * KEYS], wk[:, k, m * P:(m + 1) * P], ctxT[:, k, :], start=(k == 0), stop=(k == KB - 1))
                    last.then_inc(bank_full, 1)
                pe.wait_ge(ld_wv, 16)
                for b in range(B):
                    out = prefix(PRE_V + b)
                    for k in range(KB):
                        last = nc.tensor.matmul(out[:], ctxT[:, k, b * KEYS:(b + 1) * KEYS], wv[:, k, :], start=(k == 0), stop=(k == KB - 1))
                    last.then_inc(bank_full, 1)
                pe.wait_ge(xn_ready, TPC)
                for k in range(KB):
                    transposes(prefix(PRE_T + k), k)
                pe.wait_ge(ld_wq, 16)
                pe.wait_ge(freed["act"], 2 * KB)
                for m in range(KB):
                    project(prefix(PRE_Q + m), m)
                pe.wait_ge(ld_wo, 16)
                pe.wait_ge(freed["dve"], PRE.count("dve"))

                def scores(n, j, t):
                    tile = n * TPC + t
                    if not (isinstance(n, int) and tile == 0):
                        pe.wait_ge(shifted, tile)
                    for g in range(QUADS):
                        last = nc.tensor.matmul(score_ps[:, 4 * g:4 * g + 4, :].rearrange("p h k -> p (h k)"),
                                                q[:, j, g, t * P:(t + 1) * P], keys[:, batch(n), g, :], start=True, stop=True)
                    last.then_inc(score_full, 1)

                def turn_probs(u, s, t, g):
                    pos = s["PT"][g]
                    out = begin(u.reuse(pos), pos)
                    for h in range(4):
                        last = nc.tensor.transpose(out[:, h * P:(h + 1) * P], probs[:, (t - 1) % 2, 4 * g + h, :], ident[:])
                    last.then_inc(bank_full, 1)

                def turn_attn(u, s, tile):
                    pe.wait_ge(normed, 2 * (tile + 1))
                    out = begin(u.reuse(s["OT"]), s["OT"])
                    for k in range(KB):
                        last = nc.tensor.transpose(out[:, k * P:(k + 1) * P], attn[:, k * P:(k + 1) * P], ident[:])
                    last.then_inc(bank_full, 1)

                def output(u, s):
                    pe.wait_ge(freed["act"], u.emptied(s["OT"])[1])
                    out = begin(u.reuse(s["O"]), s["O"])
                    for k in range(KB):
                        last = nc.tensor.matmul(out[:], attnT[:, k, :], wo[:, k, :], start=(k == 0), stop=(k == KB - 1))
                    last.then_inc(bank_full, 1)

                def weigh(u, s, tile, b):
                    for half in range(2):
                        pe.wait_ge(freed["act"], u.emptied(s["PT"][2 * half + 1])[1])
                        if not (isinstance(tile, int) and tile == 0):
                            pe.wait_ge(normed, 2 * (tile - 1) + half + 1)
                        for h in range(8):
                            last = nc.tensor.matmul(pv_ps[half][:, h * VW1:(h + 1) * VW1], probsT[:, half * 8 + h, :],
                                                    vals[:, b, half * 8 + h, :], start=True, stop=True)
                        last.then_inc(pv_full, 1)

                def body(n, j, first, last):
                    u = Uses(n, first, last)
                    steps = plan(n, first, last)
                    for t, s in enumerate(steps):
                        tile = n * TPC + t
                        if t < TPC:
                            scores(n, j, t)
                        if "T" in s:
                            pe.wait_ge(xn_ready, TPC * (n + 2))
                            for k in range(KB):
                                transposes(begin(u.reuse(s["T"] + k), s["T"] + k), k)
                        if "PT" in s:
                            pe.wait_ge(exped, tile)
                            turn_probs(u, s, t, 0)
                            turn_probs(u, s, t, 1)
                        if "OT" in s:
                            turn_attn(u, s, tile - 2)
                        if "PT" in s:
                            turn_probs(u, s, t, 2)
                            turn_probs(u, s, t, 3)
                        if "O" in s:
                            output(u, s)
                        if "PT" in s:
                            weigh(u, s, tile - 1, batch(n) if t else batch(n - 1))
                        if "Q" in s:
                            pe.wait_ge(freed["act"], u.emptied(steps[2]["T"] + KB - 1)[1])
                            for m in range(KB):
                                project(begin(u.reuse(s["Q"] + m), s["Q"] + m), m)
                    if not last:
                        pe.wait_ge(freed["dve"], u.emptied(steps[TPC - 1]["Q"] + KB - 1)[1])

                all_chunks(pe, body)


EXPERTS = 8
SLOT_TILES = TILES + EXPERTS
SLOTS = SLOT_TILES * P


def expert_stage(nc, io, xres, ident):
    G = 8
    LAG = 3
    with ExitStack() as stage:
        def sb(name, shape, dt=F32):
            return stage.enter_context(nc.sbuf_tensor("d_" + name, shape, dt))

        def sem(name):
            return stage.enter_context(nc.semaphore("d_" + name))

        we = sb("we", [P, EXPERTS, KB, D])
        be = sb("be", [P, EXPERTS, D])
        token_of = sb("token_of", [P, SLOT_TILES], U32)
        tile_expert = sb("tile_expert", [P, SLOT_TILES], U32)
        ld_we, ld_be = sem("ld_we"), sem("ld_be")
        dve_step = sem("dve_step")
        rows_out = sem("rows_out")

        with ExitStack() as early:
            def esb(name, shape, dt=F32):
                return early.enter_context(nc.sbuf_tensor("d_" + name, shape, dt))

            def epb(name, shape, dt=F32):
                return early.enter_context(nc.psum_tensor("d_" + name, shape, dt))

            wg = esb("wg", [P, KB, D])
            bg = esb("bg", [P, D])
            upper_f, upper, ones = esb("upper_f", [P, P]), esb("upper", [P, P], BF16), esb("ones", [P, P], BF16)
            tile_start = esb("tile_start", [P, SLOT_TILES])
            token_id = esb("token_id", [P, TILES])
            nobody = esb("nobody", [SLOT_TILES, P])
            stats = esb("stats", [P, TPC, 6])
            mv = esb("mv", [P, TPC, 2])
            minus_half = esb("minus_half", [P, TPC])
            xn = esb("xn", [P, TPC, D])
            xT = esb("xT", [P, KB, CHUNK])
            logits = esb("logits", [P, 2, D])
            best = esb("best", [P, TPC, 8])
            where = esb("where", [P, TPC, 8], U32)
            minus_best = esb("minus_best", [P, TPC])
            total = esb("total", [P, TPC])
            held = esb("held", [P, 1])
            index = esb("index", [P, TILES], U32)
            expert_i, expert = esb("expert_i", [P, TILES], U32), esb("expert", [P, TILES])
            onehot = esb("onehot", [P, TILES, EXPERTS], BF16)
            rank = esb("rank", [P, TILES, EXPERTS])
            counts, running = esb("counts", [P, EXPERTS, TILES]), esb("running", [P, EXPERTS, TILES])
            ones_f = esb("ones_f", [P, TILES])
            padded, padded_i = esb("padded", [P, EXPERTS]), esb("padded_i", [P, EXPERTS], I32)
            end = esb("end", [P, EXPERTS])
            slot, slot_u = esb("slot", [P, TILES]), esb("slot_u", [P, TILES], U32)
            expert_at = esb("expert_at", [P, SLOT_TILES])
            owner = esb("owner", [SLOT_TILES, P])
            bank = [epb(f"bank{i}", [P, CHUNK]) for i in range(2)]
            logit_ps = epb("logit", [P, 2, D])
            rank_ps, count_ps = epb("rank_ps", [P, TILES * EXPERTS]), epb("count_ps", [P, TILES * EXPERTS])
            owner_ps = epb("owner_ps", [P, SLOT_TILES])
            ld_small, ld_wg = sem("ld_small"), sem("ld_wg")
            half_ready, pad_set = sem("half_ready"), sem("pad_set")
            var_ready, rstd_ready, xn_ready = sem("var_ready"), sem("rstd_ready"), sem("xn_ready")
            turned, turned_used = sem("turned"), sem("turned_used")
            logit_full, logit_used, best_ready, summed, row_ready = (sem(x) for x in ("logit_full", "logit_used", "best_ready", "summed", "row_ready"))
            map_cleared, hot_ready, ranked, slots_ready, scattered = (sem(x) for x in ("map_cleared", "hot_ready", "ranked", "slots_ready", "scattered"))
            owner_loaded, owner_turned = sem("owner_loaded"), sem("owner_turned")
            gate_step = sem("gate_step")

            with nc.Block() as block:
                @block.sync
                def _(sp):
                    sp.dma_start(nobody[:], io["nobody"]).then_inc(ld_small, 16)
                    sp.dma_start(bg[:], io["bg"].partition_broadcast(P)).then_inc(ld_small, 16)
                    sp.dma_start(upper_f[:], io["upper"]).then_inc(ld_small, 16)
                    sp.dma_start(tile_start[:], io["tile_start"].partition_broadcast(P)).then_inc(ld_small, 16)
                    sp.dma_start(token_id[:], io["token_id"]).then_inc(ld_small, 16)
                    sp.dma_start(wg[:], io["wg"].rearrange("(k p) n -> p k n", p=P)).then_inc(ld_wg, 16)
                    sp.wait_ge(ld_small, 80)
                    sp.dma_start(io["owner"].rearrange("(j p) o -> j (p o)", p=P), nobody[:]).then_inc(map_cleared, 16)
                    for e in range(EXPERTS):
                        sp.dma_start(we[:, e], io["we"][e].rearrange("(k p) n -> p k n", p=P)).then_inc(ld_we, 16)
                    sp.dma_start(be[:].rearrange("p e n -> p (e n)"), io["be"].partition_broadcast(P)).then_inc(ld_be, 16)
                    with sp.Fori(0, CHUNKS) as n:
                        sp.wait_ge(row_ready, n + 1)
                        sp.dma_start(io["rows"][bass.ds(n * CHUNK, CHUNK), :].rearrange("(t p) f -> p t f", p=P),
                                     xres[:, bass.ds(n * TPC, TPC), :]).then_inc(rows_out, 16)
                    sp.wait_ge(scattered, 16 * TILES)
                    sp.dma_start(owner[:], io["owner"].rearrange("(j p) o -> j (p o)", p=P)).then_inc(owner_loaded, 16)
                    sp.wait_ge(rows_out, 16 * CHUNKS)

                @block.gpsimd
                def _(pool):
                    nc.gpsimd.memset(minus_half[:], -0.5).then_inc(half_ready, 1)
                    pool.wait_ge(half_ready, 1)
                    with pool.Fori(0, CHUNKS) as n:
                        pool.wait_ge(var_ready, n + 1)
                        spread = xres[:, bass.ds(n * TPC, TPC), COL_RSTD]
                        nc.gpsimd.tensor_tensor(spread, spread, minus_half[:], ALU.pow).then_inc(rstd_ready, 1)
                    pool.wait_ge(map_cleared, 16)
                    pool.wait_ge(slots_ready, 1)
                    for t in range(TILES):
                        nc.gpsimd.indirect_dma_start(out=io["owner"], out_offset=bass.IndirectOffsetOnAxis(ap=slot_u[:, t:t + 1], axis=0),
                                                     in_=token_id[:, t:t + 1], in_offset=None).then_inc(scattered, 16)

                @block.scalar
                def _(act):
                    def body(n):
                        for k in range(KB):
                            act.wait_ge(turned, KB * n + k + 1)
                            nc.scalar.copy(xT[:, k, :], bank[k % 2][:]).then_inc(turned_used, 1)
                        for t in range(TPC):
                            tile = n * TPC + t
                            act.wait_ge(best_ready, tile + 1)
                            nc.scalar.activation(logits[:, t % 2, :], logits[:, t % 2, :], ACT.Exp, bias=minus_best[:, t:t + 1],
                                                 accum_out=total[:, t:t + 1]).then_inc(summed, 1)

                    with act.Fori(0, CHUNKS) as n:
                        body(n)

                @block.vector
                def _(dve):
                    ch = Chain(dve, gate_step)
                    nc.vector.memset(ones[:], 1.0).then_inc(pad_set, 1)
                    nc.vector.memset(ones_f[:], 1.0).then_inc(pad_set, 1)
                    nc.vector.memset(xres[:, :, COL_RSTD + 1:ROW], 0.0).then_inc(pad_set, 1)

                    def norm_stats(n):
                        for t in range(TPC):
                            ch.step(nc.vector.bn_stats(stats[:, t, :], xres[:, n * TPC + t, 0:D]))
                        ch.wait()
                        nc.vector.memset(held[:], 0.0)
                        for t in range(TPC):
                            ch.step(nc.vector.bn_aggr(mv[:, t, :], stats[:, t, :]))
                        ch.wait()
                        ch.step(nc.vector.tensor_copy(xres[:, bass.ds(n * TPC, TPC), COL_MEAN:COL_RSTD + 1], mv[:]))
                        ch.wait()
                        spread = xres[:, bass.ds(n * TPC, TPC), COL_RSTD]
                        nc.vector.tensor_scalar(spread, spread, LN_EPS, None, ALU.add).then_inc(var_ready, 1)

                    def norm_rows(n):
                        dve.wait_ge(rstd_ready, n + 1)
                        for t in range(TPC):
                            at = n * TPC + t
                            nc.vector.tensor_scalar(xn[:, t, :], xres[:, at, 0:D], xres[:, at, COL_MEAN:COL_MEAN + 1],
                                                    xres[:, at, COL_RSTD:COL_RSTD + 1], ALU.subtract, ALU.mult).then_inc(xn_ready, 1)

                    norm_stats(0)
                    norm_rows(0)
                    dve.wait_ge(ld_small, 80)
                    nc.vector.tensor_copy(upper[:], upper_f[:]).then_inc(pad_set, 1)
                    start = ch.k
                    STEPS = 2 * TPC + 1 + 3 * TPC + 1

                    def body(n, last):
                        ch.base, ch.k = start + STEPS * n, 0
                        for t in range(TPC):
                            tile = n * TPC + t
                            dve.wait_ge(logit_full, tile + 1)
                            if t >= 2:
                                dve.wait_ge(summed, tile - 1)
                            nc.vector.tensor_tensor(logits[:, t % 2, :], logit_ps[:, t % 2, :], bg[:], ALU.add).then_inc(logit_used, 1)
                            dve.wait_ge(logit_used, tile + 1)
                            nc.vector.memset(held[:], 0.0)
                            ch.step(nc.vector.max(best[:, t, :], logits[:, t % 2, :]))
                            ch.wait()
                            nc.vector.memset(held[:], 0.0)
                            ch.step(nc.vector.max_index(where[:, t, :], best[:, t, :], logits[:, t % 2, :]))
                            ch.step(nc.vector.tensor_scalar(minus_best[:, t:t + 1], best[:, t, 0:1], -1.0, None, ALU.mult))
                            ch.wait()
                            nc.vector.tensor_copy(index[:, bass.ds(tile, 1)], where[:, t, 0:1]).then_inc(best_ready, 1)
                            if t == 0 and not last:
                                norm_stats(n + 1)
                            if t == 2 and not last:
                                norm_rows(n + 1)
                        dve.wait_ge(summed, TPC * (n + 1))
                        ch.step(nc.vector.reciprocal(stats[:, :, 0], total[:]))
                        ch.wait()
                        nc.vector.tensor_copy(xres[:, bass.ds(n * TPC, TPC), COL_P], stats[:, :, 0]).then_inc(row_ready, 1)
                        dve.wait_ge(row_ready, n + 1)
                        assert last or ch.k == STEPS, ch.k

                    with dve.Fori(0, CHUNKS - 1) as n:
                        body(n, False)
                    body(CHUNKS - 1, True)

                    ch = Chain(dve, dve_step)
                    dve.wait_ge(best_ready, TILES)
                    ch.step(nc.vector.tensor_scalar(expert_i[:], index[:], EXPERTS - 1, None, ALU.bitwise_and))
                    ch.wait()
                    ch.step(nc.vector.tensor_copy(expert[:], expert_i[:]))
                    ch.wait()
                    for e in range(EXPERTS):
                        last = nc.vector.tensor_scalar(onehot[:, :, e], expert[:], float(e), None, ALU.is_equal)
                    last.then_inc(hot_ready, 1)
                    dve.wait_ge(ranked, 2)
                    ch.step(nc.vector.tensor_copy(counts[:], count_ps[:].rearrange("p (t e) -> p e t", e=EXPERTS)))
                    ch.wait()
                    for e in range(EXPERTS):
                        ch.step(nc.vector.tensor_tensor_scan(running[:, e, :], ones_f[:], counts[:, e, :], 0.0, ALU.mult, ALU.add))
                    ch.wait()
                    ch.step(nc.vector.tensor_scalar(padded[:], running[:, :, TILES - 1], float(P - 1), None, ALU.add))
                    ch.step(nc.vector.tensor_tensor(counts[:], running[:], counts[:], ALU.subtract))
                    ch.wait()
                    ch.step(nc.vector.tensor_copy(padded_i[:], padded[:]))
                    ch.wait()
                    ch.step(nc.vector.tensor_scalar(padded_i[:], padded_i[:], 7, 7, ALU.arith_shift_right, ALU.logical_shift_left))
                    ch.wait()
                    ch.step(nc.vector.tensor_copy(padded[:], padded_i[:]))
                    ch.wait()
                    ch.step(nc.vector.tensor_tensor_scan(end[:], ones_f[:, 0:EXPERTS], padded[:], 0.0, ALU.mult, ALU.add))
                    ch.wait()
                    ch.step(nc.vector.tensor_tensor(padded[:], end[:], padded[:], ALU.subtract))
                    ch.step(nc.vector.tensor_scalar(expert_at[:], tile_start[:], end[:, 0:1], None, ALU.is_ge))
                    ch.wait()
                    for e in range(1, EXPERTS - 1):
                        ch.step(nc.vector.scalar_tensor_tensor(expert_at[:], tile_start[:], end[:, e:e + 1], expert_at[:], ALU.is_ge, ALU.add))
                        ch.wait()
                    ch.step(nc.vector.tensor_copy(tile_expert[:], expert_at[:]))
                    ch.step(nc.vector.tensor_tensor(counts[:], counts[:], padded[:].unsqueeze(2).to_broadcast([P, EXPERTS, TILES]), ALU.add))
                    ch.wait()
                    ch.step(nc.vector.tensor_tensor(rank[:], rank_ps[:].rearrange("p (t e) -> p t e", e=EXPERTS),
                                                    counts[:].rearrange("p e t -> p t e"), ALU.add))
                    ch.wait()
                    ch.step(nc.vector.tensor_tensor(rank[:], rank[:], onehot[:], ALU.mult))
                    ch.wait()
                    ch.step(nc.vector.tensor_reduce(slot[:], rank[:], AX.X, ALU.add))
                    ch.wait()
                    nc.vector.tensor_copy(slot_u[:], slot[:]).then_inc(slots_ready, 1)
                    dve.wait_ge(owner_turned, 1)
                    ch.step(nc.vector.tensor_copy(token_of[:], owner_ps[:]))

                @block.tensor
                def _(pe):
                    def turn(n, k, count):
                        if count is not None:
                            pe.wait_ge(turned_used, count)
                        for t in range(TPC):
                            last = nc.tensor.transpose(bank[k % 2][:, t * P:(t + 1) * P], xn[:, t, k * P:(k + 1) * P], ident[:])
                        last.then_inc(turned, 1)

                    pe.wait_ge(xn_ready, TPC)
                    for k in range(KB):
                        turn(0, k, k - 1 if k >= 2 else None)
                    pe.wait_ge(ld_wg, 16)

                    def body(n, last, first):
                        pe.wait_ge(turned_used, KB * (n + 1))
                        for t in range(TPC):
                            tile = n * TPC + t
                            if not first or t >= 2:
                                pe.wait_ge(logit_used, tile - 1)
                            for k in range(KB):
                                ins = nc.tensor.matmul(logit_ps[:, t % 2, :], xT[:, k, t * P:(t + 1) * P], wg[:, k, :],
                                                       start=(k == 0), stop=(k == KB - 1))
                            ins.then_inc(logit_full, 1)
                        if not last:
                            pe.wait_ge(xn_ready, TPC * (n + 2))
                            for k in range(KB):
                                turn(n + 1, k, KB * (n + 1) + k - 1)

                    body(0, False, True)
                    with pe.Fori(1, CHUNKS - 1) as n:
                        body(n, False, False)
                    body(CHUNKS - 1, True, False)
                    pe.wait_ge(pad_set, 4)
                    pe.wait_ge(hot_ready, 1)
                    hot = onehot[:].rearrange("p t e -> p (t e)")
                    nc.tensor.matmul(rank_ps[:], upper[:], hot, start=True, stop=True).then_inc(ranked, 1)
                    nc.tensor.matmul(count_ps[:], ones[:], hot, start=True, stop=True).then_inc(ranked, 1)
                    pe.wait_ge(owner_loaded, 16)
                    nc.tensor.transpose(owner_ps[:], owner[:], ident[0:SLOT_TILES, 0:SLOT_TILES]).then_inc(owner_turned, 1)

        with ExitStack() as late:
            def lsb(name, shape, dt=F32):
                return late.enter_context(nc.sbuf_tensor("d_" + name, shape, dt))

            held = lsb("pool_held", [P, 3])
            got = [lsb(f"got{i}", [P, ROW]) for i in range(G)]
            token = [lsb(f"token{i}", [P, 1], U32) for i in range(G)]
            xn = lsb("slot_xn", [P, 2, D])
            xT = lsb("slot_xT", [P, 2, KB, P])
            y = [lsb(f"y{i}", [P, D]) for i in range(G)]
            turn_ps = late.enter_context(nc.psum_tensor("d_turn", [P, 2, D], F32))
            y_ps = late.enter_context(nc.psum_tensor("d_y", [P, 2, D], F32))
            got_clear, token_ready, held_set = sem("got_clear"), sem("token_ready"), sem("held_set")
            gathered = [sem(f"gathered{i}") for i in range(G)]
            stored = [sem(f"stored{i}") for i in range(G)]
            xn_ready, turned, xT_ready, y_full, y_used, y_ready = (sem("slot_" + x) for x in ("xn", "turned", "xT", "y_full", "y_used", "y_ready"))
            y_step = sem("y_step")
            ROUNDS = SLOT_TILES // G

            def rounds(eng, body):
                for u in range(G):
                    body(u, 0, u, True, False)
                with eng.Fori(1, ROUNDS - 1) as i:
                    for u in range(G):
                        body(G * i + u, i, u, False, False)
                for u in range(G):
                    body(SLOT_TILES - G + u, ROUNDS - 1, u, False, True)

            with nc.Block() as block:
                @block.gpsimd
                def _(pool):
                    nc.gpsimd.memset(held[:], 0.0).then_inc(held_set, 1)

                    def hold(before):
                        pool.wait_ge(held_set, 1 + before)
                        nc.gpsimd.tensor_tensor(held[:, 2:3], held[:, 0:1], held[:, 1:2], ALU.add).then_inc(held_set, 1)

                    def gather(i, u, before):
                        pool.wait_ge(token_ready, G * i + u + 1)
                        hold(before)
                        nc.gpsimd.indirect_dma_start(out=got[u][:], out_offset=None, in_=io["rows"],
                                                     in_offset=bass.IndirectOffsetOnAxis(ap=token[u][:], axis=0),
                                                     bounds_check=TOK - 1, oob_is_err=False).then_inc(gathered[u], 16)

                    def scatter(j, u, before):
                        pool.wait_ge(y_ready, j + 1)
                        hold(before)
                        nc.gpsimd.indirect_dma_start(out=io["out"], out_offset=bass.IndirectOffsetOnAxis(ap=token[u][:], axis=0),
                                                     in_=y[u][:], in_offset=None, bounds_check=TOK - 1,
                                                     oob_is_err=False).then_inc(stored[u], 16)

                    pool.wait_ge(got_clear, G)
                    for u in range(G):
                        gather(0, u, u)

                    def body(j, i, u, first, last):
                        more = SLOT_TILES - G if last and u >= LAG else 0 if first and u < LAG else j - LAG
                        scatter(j, u, G + j + more)
                        if u >= LAG and not last:
                            gather(i + 1, u - LAG, G + j + 1 + more)
                        elif u < LAG and not first:
                            gather(i, u - LAG + G, G + j + 1 + more)

                    rounds(pool, body)
                    for u in range(G):
                        pool.wait_ge(stored[u], 16 * ROUNDS)

                @block.scalar
                def _(act):
                    def body(j, i, u, first, last):
                        act.wait_ge(turned, j + 1)
                        if not first or u >= 2:
                            act.wait_ge(y_full, j - 1)
                        nc.scalar.copy(xT[:, u % 2].rearrange("p k t -> p (k t)"), turn_ps[:, u % 2, :]).then_inc(xT_ready, 1)

                    rounds(act, body)

                @block.vector
                def _(dve):
                    ch = Chain(dve, y_step)
                    for u in range(G):
                        nc.vector.memset(got[u][:], 0.0).then_inc(got_clear, 1)
                    for u in range(G):
                        nc.vector.tensor_copy(token[u][:], token_of[:, u:u + 1]).then_inc(token_ready, 1)
                    dve.wait_ge(ld_be, 16)

                    def norm(j, i, u, first):
                        dve.wait_ge(gathered[u], 16 * (i + 1))
                        if not first or u >= 2:
                            dve.wait_ge(turned, j - 1)
                        nc.vector.tensor_scalar(xn[:, u % 2, :], got[u][:, 0:D], got[u][:, COL_MEAN:COL_MEAN + 1],
                                                got[u][:, COL_RSTD:COL_RSTD + 1], ALU.subtract, ALU.mult).then_inc(xn_ready, 1)

                    def finish(j, u):
                        expert = dve.value_load(tile_expert[0:1, bass.ds(j, 1)], min_val=0, max_val=EXPERTS - 1)
                        dve.wait_ge(y_full, j + 1)
                        nc.vector.tensor_tensor(y[u][:], y_ps[:, u % 2, :], be[:, expert, :], ALU.add).then_inc(y_used, 1)
                        dve.wait_ge(y_used, j + 1)
                        ch.base, ch.k = j, 0
                        ch.step(nc.vector.tensor_scalar(y[u][:], y[u][:], 0.0, got[u][:, COL_P:COL_P + 1], ALU.max, ALU.mult))
                        ch.wait()
                        nc.vector.tensor_tensor(y[u][:], y[u][:], got[u][:, 0:D], ALU.add).then_inc(y_ready, 1)

                    def next_token(j, i, u):
                        dve.wait_ge(stored[u], 16 * (i + 1))
                        nc.vector.tensor_copy(token[u][:], token_of[:, bass.ds(j + G, 1)]).then_inc(token_ready, 1)

                    def body(j, i, u, first, last):
                        norm(j, i, u, first)
                        if not (first and u == 0):
                            finish(j - 1, (u - 1) % G)
                        if u >= LAG and not last:
                            next_token(j - LAG, i, u - LAG)
                        elif u < LAG and not first:
                            next_token(j - LAG, i - 1, u - LAG + G)

                    rounds(dve, body)
                    finish(SLOT_TILES - 1, G - 1)

                @block.tensor
                def _(pe):
                    pe.wait_ge(ld_we, 16 * EXPERTS)

                    def turn(j, i, u, first):
                        pe.wait_ge(xn_ready, j + 1)
                        if not first or u >= 2:
                            pe.wait_ge(xT_ready, j - 1)
                        for k in range(KB):
                            last = nc.tensor.transpose(turn_ps[:, u % 2, k * P:(k + 1) * P], xn[:, u % 2, k * P:(k + 1) * P], ident[:])
                        last.then_inc(turned, 1)

                    def product(j, par):
                        expert = pe.value_load(tile_expert[0:1, bass.ds(j, 1)], min_val=0, max_val=EXPERTS - 1)
                        pe.wait_ge(xT_ready, j + 1)
                        if not (isinstance(j, int) and j < 2):
                            pe.wait_ge(y_used, j - 1)
                        for k in range(KB):
                            last = nc.tensor.matmul(y_ps[:, par, :], xT[:, par, k, :], we[:, expert, k, :], start=(k == 0), stop=(k == KB - 1))
                        last.then_inc(y_full, 1)

                    def body(j, i, u, first, last):
                        turn(j, i, u, first)
                        if not (first and u == 0):
                            product(j - 1, (u - 1) % 2)

                    rounds(pe, body)
                    product(SLOT_TILES - 1, (SLOT_TILES - 1) % 2)


def build_program(nc, io):
    with ExitStack() as whole:
        xres = whole.enter_context(nc.sbuf_tensor("xres", [P, TILES, ROW], F32))
        ident = whole.enter_context(nc.sbuf_tensor("ident", [P, P], F32))
        rope_attention_stage(nc, io, xres, ident)
        quantised_ffn_stage(nc, io, xres, ident)
        masked_attention_stage(nc, io, xres, ident)
        expert_stage(nc, io, xres, ident)


def shape_constants():
    import numpy as np

    freq = np.float32(1) / (10000.0 ** (np.arange(0, DH0, 2) / DH0)).astype(np.float32)
    angle = np.arange(S, dtype=np.float32)[:, None] * freq[None, :]
    cos = np.repeat(np.cos(angle), 2, axis=1).T
    sin = np.repeat(np.sin(angle), 2, axis=1).T * np.tile(np.array([-1, 1], np.float32), DH0 // 2)[:, None]
    rot = np.stack([np.tile(cos, (2, 1)), np.tile(sin, (2, 1))], axis=1)
    at = np.arange(P)
    causal = np.ones((P, CPB, KEYS), np.float32)
    causal[:, 0, :] = at[:, None] <= at[None, :]
    return {
        "ident": np.eye(P, dtype=np.float32),
        "rot": np.ascontiguousarray(rot, np.float32),
        "causal": causal,
        "upper": (at[:, None] < at[None, :]).astype(np.float32),
        "tile_start": (P * np.arange(SLOT_TILES, dtype=np.float32))[None, :],
        "token_id": (P * np.arange(TILES, dtype=np.float32)[None, :] + at[:, None].astype(np.float32)),
        "nobody": np.full((SLOT_TILES, P), TOK, np.float32),
    }


def kernel(x, ctx_1024, mask_BxS2_bf0, mask_1x1xSxS2_bk0, L0_xattn_Wq, L0_xattn_Wk, L0_xattn_Wv, L0_xattn_Wo, L0_xattn_ln_g,
           L0_xattn_ln_b, L0_ffn_clip_x, L0_ffn_clip_down, L0_ffn_w_gate, L0_ffn_w_up, L0_ffn_w_down, L1_xattn_Wq, L1_xattn_bq,
           L1_xattn_Wk, L1_xattn_bk, L1_xattn_Wv, L1_xattn_bv, L1_xattn_Wo, L1_xattn_bo, L1_ffn_Wg, L1_ffn_bg, L1_ffn_We,
           L1_ffn_be):
    import numpy as np
    import concourse.bacc as bacc
    from concourse.bass_utils import run_bass_kernel_spmd

    def columns(v):
        return np.asarray(v).reshape(KB, P).T

    def row(v):
        return np.asarray(v).reshape(1, -1)

    laid_out = {
        "x": np.asarray(x).reshape(TOK, D),
        "ctx": np.asarray(ctx_1024).reshape(B * KEYS, D),
        "pad": np.asarray(mask_BxS2_bf0).T,
        "mask": np.asarray(mask_1x1xSxS2_bk0).reshape(S, KEYS),
        "ln_g": columns(L0_xattn_ln_g), "ln_b": columns(L0_xattn_ln_b),
        "wq0": L0_xattn_Wq, "wk0": L0_xattn_Wk, "wv0": L0_xattn_Wv, "wo0": L0_xattn_Wo,
        "clip": np.concatenate([row(L0_ffn_clip_x), row(L0_ffn_clip_down)], axis=1),
        "w_gate": L0_ffn_w_gate, "w_up": L0_ffn_w_up, "w_down": L0_ffn_w_down,
        "wq1": np.asarray(L1_xattn_Wq).T, "wk1": np.asarray(L1_xattn_Wk).T,
        "wv1": np.asarray(L1_xattn_Wv).T, "wo1": np.asarray(L1_xattn_Wo).T,
        "qk_bias": np.stack([columns(L1_xattn_bq), columns(L1_xattn_bk)], axis=1),
        "bv": row(L1_xattn_bv), "bo": row(L1_xattn_bo),
        "wg": L1_ffn_Wg, "bg": row(L1_ffn_bg), "we": L1_ffn_We, "be": row(L1_ffn_be),
        **shape_constants(),
    }
    nc = bacc.Bacc("TRN2", target_bir_lowering=False, num_devices=1)
    arrays, io = {}, {}
    for name, value in laid_out.items():
        a = np.ascontiguousarray(value)
        arrays[f"in_{name}"] = a
        io[name] = nc.dram_tensor(f"in_{name}", a.shape, mybir.dt.from_np(a.dtype), kind="ExternalInput").ap()
    io["hidden"] = nc.dram_tensor("hidden", [CHUNKS, P, IT * CHUNK], F32).ap()
    io["rows"] = nc.dram_tensor("rows", [TOK, ROW], F32).ap()
    io["owner"] = nc.dram_tensor("owner", [SLOTS, 1], F32).ap()
    io["out"] = nc.dram_tensor("out", [TOK, D], F32, kind="ExternalOutput").ap()
    build_program(nc, io)
    got = run_bass_kernel_spmd(nc, [arrays], core_ids=[0])
    return got.results[0]["out"].reshape(B, S, D)
```

```python
import concourse.bass as bass
from concourse import mybir
from contextlib import ExitStack

F32 = mybir.dt.float32
F32R = mybir.dt.float32r
BF16 = mybir.dt.bfloat16
I32 = mybir.dt.int32
U32 = mybir.dt.uint32
U8 = mybir.dt.uint8
ALU = mybir.AluOpType
ACT = mybir.ActivationFunctionType
AX = mybir.AxisListType

P = 128
B, S, D = 2, 2048, 512
KEYS = 128
TOK = B * S
TILES = TOK // P
CHUNK = 512
TPC = CHUNK // P
CHUNKS = TOK // CHUNK
CPB = CHUNKS // B
KB = D // P
LN_EPS = 1e-5
ROW = D + 4
COL_P, COL_MEAN, COL_RSTD = D, D + 1, D + 2

H0, DH0 = 16, 64
HD0 = H0 * DH0
GROK = 30.0
ROPE_CHUNK = 256
ROPE_TILES = ROPE_CHUNK // P
ROPE_CHUNKS = TOK // ROPE_CHUNK
ROPE_CPB = ROPE_CHUNKS // B
UNITS = H0 // 4
BLOCKS = HD0 // P


class Chain:

    def __init__(self, eng, sem, base=0):
        self.eng, self.sem, self.base, self.k = eng, sem, base, 0

    def step(self, ins):
        ins.then_inc(self.sem, 1)
        self.k += 1

    def wait(self):
        self.eng.wait_ge(self.sem, self.base + self.k)


class Ring:

    def __init__(self, prefix, body):
        self.prefix, self.body = prefix, body
        assert len(prefix) % 2 == 0 and len(body) % 2 == 0 and prefix[-2:] == body[-2:]

    def full(self, n, pos):
        return len(self.prefix) + len(self.body) * n + pos + 1

    def emptied(self, n, seq, pos):
        who = seq[pos]
        return who, self.prefix.count(who) + self.body.count(who) * n + seq[:pos + 1].count(who)

    def reuse(self, n, seq, pos):
        if pos >= 2:
            return self.emptied(n, seq, pos - 2)
        last = self.prefix[-2:]
        who = last[pos]
        return who, self.prefix.count(who) + self.body.count(who) * n - last[pos + 1:].count(who)

    def prefix_full(self, pos):
        return pos + 1

    def prefix_emptied(self, pos):
        who = self.prefix[pos]
        return who, self.prefix[:pos + 1].count(who)


class Seen:

    def __init__(self, nc, stage):
        self.stats = stage.enter_context(nc.sbuf_tensor("seen_stats", [P, TILES, 6], F32))
        self.top = stage.enter_context(nc.sbuf_tensor("seen_top", [P, TILES], F32))
        self.low = stage.enter_context(nc.sbuf_tensor("seen_low", [P, TILES], F32))


def rope_attention_stage(nc, io, xres, ident, seen):
    SWAP = [i ^ 1 for i in range(32)]
    VW = DH0 + 1
    NT, NC, CPBA = ROPE_TILES, ROPE_CHUNKS, ROPE_CPB
    with ExitStack() as stage:
        def sb(name, shape, dt=F32):
            return stage.enter_context(nc.sbuf_tensor("a_" + name, shape, dt))

        def pb(name, shape, dt=F32):
            return stage.enter_context(nc.psum_tensor("a_" + name, shape, dt))

        def sem(name):
            return stage.enter_context(nc.semaphore("a_" + name))

        keysT = sb("keysT", [P, BLOCKS, B * KEYS])
        vals = sb("vals", [P, B, H0, VW])
        gain = sb("gain", [P, KB])
        shift = sb("shift", [P, KB])
        pad_u8 = sb("pad_u8", [P, B], U8)
        pad_bias = sb("pad_bias", [P, B])
        causal = sb("causal", [P, 2, KEYS])
        rot = sb("rot", [P, 2, ROPE_CHUNK])
        wq_hi, wq_lo = (sb("wq_" + x, [P, KB, HD0], F32R) for x in ("hi", "lo"))
        wo_hi, wo_lo = (sb("wo_" + x, [P, BLOCKS, D], F32R) for x in ("hi", "lo"))
        q_bias, q_bias_swapped = sb("q_bias", [P, BLOCKS]), sb("q_bias_swapped", [P, BLOCKS])
        stats = sb("stats", [P, NT, 6])
        mv = sb("mv", [P, NT, 2])
        var = sb("var", [P, NT])
        rstd = sb("rstd", [P, NT])
        minus_half = sb("minus_half", [P, NT])
        swapped = sb("swapped", [P, 2, ROPE_CHUNK])
        recip = sb("recip", [P, NT, 4])
        held = sb("held", [P, 1])

        score_ps = pb("score_ps", [P, 2, 4, ROPE_CHUNK])
        bank = [pb(f"bank{i}", [P, 2, ROPE_CHUNK]) for i in range(2)]
        pv_ps = [pb(f"pv_ps{i}", [P, D]) for i in range(NT)]

        ld_small, ld_ctx, ld_wk, ld_wv = sem("ld_small"), sem("ld_ctx"), sem("ld_wk"), sem("ld_wv")
        ld_wq, ld_wo, ld_x = sem("ld_wq"), sem("ld_wo"), sem("ld_x")
        ld_rot, rot_used = sem("ld_rot"), sem("rot_used")
        bank_full = sem("bank_full")
        freed = {"dve": sem("freed_by_dve"), "act": sem("freed_by_act")}
        var_ready, rstd_ready, xn_ready = sem("var_ready"), sem("rstd_ready"), sem("xn_ready")
        half_ready = sem("half_ready")
        weight_hi, weight_lo, bias_full = sem("weight_hi"), sem("weight_lo"), sem("bias_full")
        hi_ready, lo_ready = sem("hi_ready"), sem("lo_ready")
        q_ready, score_full, capped, exped = sem("q_ready"), sem("score_full"), sem("capped"), sem("exped")
        masked, pv_full, normed = sem("masked"), sem("pv_full"), sem("normed")
        dve_step = sem("dve_step")

        PRE = ["act"] * KB + ["dve"] * BLOCKS + ["act"] * (2 * B) + ["act"] * 2 + ["dve"] * 2
        BODY = ["dve"] * 2 + ["act"] * 4 + ["dve", "act"] * 2 + ["dve"] * 2
        LAST = ["dve"] * 2 + ["act"] * 4 + ["dve"] * 2
        AT_Q2, AT_Q3, AT_X = 0, 1, 2
        ring = Ring(PRE, BODY)
        PREP_STEPS = 1 + 2 * B + 1 + 3 * BLOCKS + 2
        PRE_K, PRE_V = KB, KB + BLOCKS
        PRE_T0, PRE_Q0 = PRE_V + 2 * B, PRE_V + 2 * B + 2

        def places(last):
            if last:
                return {"attn": [2, 3, 4, 5], "out": [6, 7]}
            return {"attn": [4, 5, 7, 9], "next": [6, 8], "out": [10, 11]}

        def splits(n, last):
            return 2 + 6 * n, 2 + 6 * n + (0 if last else 2)

        def chunks(eng, body):
            with eng.Fori(0, CPBA) as c:
                body(c, c, 0, False)
            with eng.Fori(0, CPBA - 1) as c:
                body(c + CPBA, c, 1, False)
            body(NC - 1, CPBA - 1, 1, True)

        with ExitStack() as early:
            def esb(name, shape):
                return early.enter_context(nc.sbuf_tensor("a_" + name, shape, F32))

            wk_or_wo = esb("wk_or_wo", [P, KB * HD0])
            wk, wo = wk_or_wo[:].rearrange("p (k n) -> p k n", k=KB), wk_or_wo[:].rearrange("p (k n) -> p k n", k=BLOCKS)
            wv, wq = esb("wv", [P, KB, HD0]), esb("wq", [P, KB, HD0])
            ctx_t, ctxT = esb("ctx", [P, B, D]), esb("ctxT", [P, KB, B * KEYS])
            turned = ctx_t[:, 0, 0:B * KEYS]

            with nc.Block() as block:
                @block.sync
                def _(sp):
                    sp.dma_start(ctx_t[:], io["ctx"].rearrange("(b p) f -> p b f", p=P)).then_inc(ld_ctx, 16)
                    sp.dma_start(ident[:], io["ident"]).then_inc(ld_small, 16)
                    sp.dma_start(gain[:], io["ln_g"]).then_inc(ld_small, 16)
                    sp.dma_start(shift[:], io["ln_b"]).then_inc(ld_small, 16)
                    sp.dma_start(pad_u8[:], io["pad"]).then_inc(ld_small, 16)
                    sp.dma_start(causal[:], io["causal"]).then_inc(ld_small, 16)
                    sp.dma_start(rot[:], io["rot"][:, :, 0:ROPE_CHUNK]).then_inc(ld_small, 16)
                    sp.dma_start(wk, io["wk0"].rearrange("(k p) n -> p k n", p=P)).then_inc(ld_wk, 16)
                    sp.dma_start(wq[:], io["wq0"].rearrange("(k p) n -> p k n", p=P)).then_inc(ld_wq, 16)
                    sp.dma_start(wv[:], io["wv0"].rearrange("(k p) n -> p k n", p=P)).then_inc(ld_wv, 16)
                    for c in range(CHUNKS):
                        sp.dma_start(xres[:, c * TPC:(c + 1) * TPC, 0:D],
                                     io["x"][c * CHUNK:(c + 1) * CHUNK, :].rearrange("(t p) f -> p t f", p=P)
                                     ).then_inc(ld_x, 16)
                        if c == 0:
                            sp.wait_ge(bank_full, ring.prefix_full(PRE_V - 1))
                            sp.dma_start(wo, io["wo0"].rearrange("(k p) n -> p k n", p=P)).then_inc(ld_wo, 16)

                @block.gpsimd
                def _(pool):
                    nc.gpsimd.memset(minus_half[:], -0.5).then_inc(half_ready, 1)
                    pool.wait_ge(half_ready, 1)
                    pool.wait_ge(var_ready, 1)
                    nc.gpsimd.tensor_tensor(rstd[:, 0:B], var[:, 0:B], minus_half[:, 0:B], ALU.pow).then_inc(rstd_ready, 1)

                @block.scalar
                def _(act):
                    act.wait_ge(ld_small, 96)
                    for k in range(KB):
                        act.wait_ge(bank_full, ring.prefix_full(k))
                        nc.scalar.activation(ctxT[:, k, :], bank[k % 2][:, 0, :], ACT.Identity,
                                             bias=shift[:, k:k + 1], scale=gain[:, k:k + 1]).then_inc(freed["act"], 1)
                    act.wait_ge(ld_wq, 16)
                    for k in range(KB):
                        nc.scalar.activation(wq_hi[:, k, :], wq[:, k, :], ACT.Copy, scale=gain[:, k:k + 1]).then_inc(weight_hi, 1)
                    for u in range(2 * B):
                        b, half = u // 2, u % 2
                        act.wait_ge(bank_full, ring.prefix_full(PRE_V + u))
                        nc.scalar.copy(vals[:, b, half * 8:(half + 1) * 8, 0:DH0],
                                       bank[(PRE_V + u) % 2][:].rearrange("p a c -> p (a c)").rearrange("p (h d) -> p h d", d=DH0)
                                       ).then_inc(freed["act"], 1)
                    act.wait_ge(ld_wo, 16)
                    nc.scalar.copy(wo_hi[:], wo).then_inc(weight_hi, 1)

                @block.vector
                def _(dve):
                    ch = Chain(dve, dve_step)
                    ch.step(nc.vector.memset(vals[:, :, :, DH0:VW], 1.0))
                    dve.wait_ge(ld_ctx, 16)
                    for b in range(B):
                        ch.step(nc.vector.bn_stats(stats[:, b, :], ctx_t[:, b, :]))
                    ch.wait()
                    for b in range(B):
                        ch.step(nc.vector.bn_aggr(mv[:, b, :], stats[:, b, :]))
                    ch.wait()
                    nc.vector.tensor_scalar(var[:, 0:B], mv[:, 0:B, 1], LN_EPS, None, ALU.add).then_inc(var_ready, 1)
                    dve.wait_ge(rstd_ready, 1)
                    for b in range(B):
                        last = nc.vector.tensor_scalar(ctx_t[:, b, :], ctx_t[:, b, :], mv[:, b, 0:1],
                                                       rstd[:, b:b + 1], ALU.subtract, ALU.mult)
                    last.then_inc(xn_ready, 1)
                    dve.wait_ge(ld_small, 96)
                    ch.step(nc.vector.tensor_scalar(pad_bias[:], pad_u8[:], -1e30, None, ALU.mult))
                    cos_k = rot[:, 0, 0:KEYS].unsqueeze(1).to_broadcast([P, B, KEYS])
                    sin_k = rot[:, 1, 0:KEYS].unsqueeze(1).to_broadcast([P, B, KEYS])
                    by_batch = lambda x: x.rearrange("p (b k) -> p b k", b=B)
                    for m in range(BLOCKS):
                        dve.wait_ge(bank_full, ring.prefix_full(PRE_K + m))
                        src = bank[(PRE_K + m) % 2][:, 0, :]
                        sw = swapped[:, 0, :]
                        ch.wait()
                        ch.step(nc.vector.stream_shuffle(sw, src, SWAP))
                        nc.vector.tensor_tensor(by_batch(turned), by_batch(src), cos_k, ALU.mult).then_inc(freed["dve"], 1)
                        ch.wait()
                        ch.step(nc.vector.tensor_tensor(by_batch(sw), by_batch(sw), sin_k, ALU.mult))
                        ch.wait()
                        ch.step(nc.vector.tensor_tensor(keysT[:, m, :], turned, sw, ALU.add))
                    dve.wait_ge(bias_full, 1)
                    ch.step(nc.vector.tensor_copy(q_bias[:], score_ps[:, 0, 0, 0:BLOCKS]))
                    ch.wait()
                    ch.step(nc.vector.stream_shuffle(q_bias_swapped[:], q_bias[:], SWAP))
                    for k in range(KB):
                        dve.wait_ge(weight_hi, k + 1)
                        nc.vector.scalar_tensor_tensor(wq_lo[:, k, :], wq[:, k, :], gain[:, k:k + 1], wq_hi[:, k, :],
                                                       ALU.mult, ALU.subtract).then_inc(weight_lo, 1)
                    dve.wait_ge(weight_hi, KB + 1)
                    nc.vector.tensor_tensor(wo_lo[:], wo, wo_hi[:], ALU.subtract).then_inc(weight_lo, 1)
                    ch.wait()
                    assert ch.k == PREP_STEPS, ch.k

                @block.tensor
                def _(pe):
                    pe.wait_ge(ld_small, 96)
                    pe.wait_ge(xn_ready, 1)

                    def begin(u):
                        if u >= 2:
                            who, count = ring.prefix_emptied(u - 2)
                            pe.wait_ge(freed[who], count)
                        return bank[u % 2]

                    for k in range(KB):
                        out = begin(k)
                        for b in range(B):
                            last = nc.tensor.transpose(out[:, 0, b * KEYS:(b + 1) * KEYS], ctx_t[:, b, k * P:(k + 1) * P], ident[:])
                        last.then_inc(bank_full, 1)
                    pe.wait_ge(freed["act"], KB)
                    pe.wait_ge(ld_wk, 16)
                    for m in range(BLOCKS):
                        out = begin(PRE_K + m)
                        for k in range(KB):
                            last = nc.tensor.matmul(out[:, 0, :], wk[:, k, m * P:(m + 1) * P], ctxT[:, k, :],
                                                    start=(k == 0), stop=(k == KB - 1))
                        last.then_inc(bank_full, 1)
                    pe.wait_ge(ld_wq, 16)
                    for m in range(BLOCKS):
                        for k in range(KB):
                            last = nc.tensor.matmul(score_ps[:, 0, 0, m:m + 1], wq[:, k, m * P:(m + 1) * P], shift[:, k:k + 1],
                                                    start=(k == 0), stop=(k == KB - 1))
                    last.then_inc(bias_full, 1)
                    pe.wait_ge(ld_wv, 16)
                    for u in range(2 * B):
                        b, half = u // 2, u % 2
                        out = begin(PRE_V + u)
                        for k in range(KB):
                            last = nc.tensor.matmul(out[:].rearrange("p a c -> p (a c)"), ctxT[:, k, b * KEYS:(b + 1) * KEYS],
                                                    wv[:, k, half * D:(half + 1) * D], start=(k == 0), stop=(k == KB - 1))
                        last.then_inc(bank_full, 1)

        xn = sb("xn", [P, NT, D])
        x_hi, x_lo = (sb("x_" + x, [P, KB, ROPE_CHUNK], F32R) for x in ("hi_parts", "lo_parts"))
        probs = sb("probs", [P, 2, 4, ROPE_CHUNK])
        q = sb("q", [P, BLOCKS, ROPE_CHUNK])
        attn = sb("attn", [P, NT, HD0])
        attn_hi, attn_lo = (sb("attn_" + x, [P, BLOCKS, ROPE_CHUNK], F32R) for x in ("hi_parts", "lo_parts"))
        full = sb("full", [P, 2, 2, ROPE_CHUNK])
        VAR0 = 1
        DVE_STEPS = 2 * NT + 4 - 1 + UNITS * NT + 3 * NT
        with nc.Block() as block:
            @block.sync
            def _(sp):
                def load_rot(n, c):
                    sp.wait_ge(rot_used, n)
                    sp.dma_start(rot[:], io["rot"][:, :, bass.ds(c * ROPE_CHUNK, ROPE_CHUNK)]).then_inc(ld_rot, 16)
                with sp.Fori(1, CPBA) as c:
                    load_rot(c, c)
                with sp.Fori(0, CPBA) as c:
                    load_rot(c + CPBA, c)

            @block.gpsimd
            def _(pool):
                def deviation(n):
                    pool.wait_ge(var_ready, VAR0 + 1 + n)
                    nc.gpsimd.tensor_tensor(rstd[:], var[:], minus_half[:], ALU.pow).then_inc(rstd_ready, 1)

                def low_parts(i, j, lo, hi, pair):
                    pool.wait_ge(hi_ready, i + 1)
                    at = slice(2 * pair, 2 * pair + 2)
                    nc.gpsimd.tensor_tensor(lo[:, at, :], full[:, j], hi[:, at, :], ALU.subtract).then_inc(lo_ready, 1)

                deviation(0)
                for k in range(2):
                    low_parts(k, k, x_lo, x_hi, k)

                def body(n, c, b, last):
                    x_at, attn_at = splits(n, last)
                    if not last:
                        deviation(n + 1)
                        for k in range(2):
                            low_parts(x_at + k, k, x_lo, x_hi, k)
                    for g in range(UNITS):
                        low_parts(attn_at + g, g % 2, attn_lo, attn_hi, g)

                chunks(pool, body)

            @block.scalar
            def _(act):
                def split(i, j, filled, emptied, pos, hi, pair):
                    if not isinstance(i, int) or i >= 2:
                        act.wait_ge(lo_ready, i - 1)
                    act.wait_ge(bank_full, filled)
                    nc.scalar.copy(full[:, j], bank[pos % 2][:]).then_inc(freed["act"], 1)
                    act.wait_ge(freed["act"], emptied)
                    nc.scalar.copy(hi[:, 2 * pair:2 * pair + 2, :], full[:, j]).then_inc(hi_ready, 1)

                for k in range(2):
                    pos = PRE_T0 + k
                    split(k, k, ring.prefix_full(pos), ring.prefix_emptied(pos)[1], pos, x_hi, k)

                def body(n, c, b, last):
                    seq, at = LAST if last else BODY, places(last)["attn"]
                    x_at, attn_at = splits(n, last)

                    def split_attn(g):
                        split(attn_at + g, g % 2, ring.full(n, at[g]), ring.emptied(n, seq, at[g])[1], at[g], attn_hi, g)

                    for p in range(UNITS):
                        unit = n * UNITS + p
                        buf = probs[:, p % 2]
                        act.wait_ge(score_full, unit + 1)
                        if p >= 2:
                            act.wait_ge(pv_full, NT * (unit - 1))
                        nc.scalar.activation(buf, score_ps[:, p % 2], ACT.Tanh, scale=1.0 / (DH0 ** 0.5 * GROK)).then_inc(capped, 1)
                        act.wait_ge(capped, unit + 1)
                        nc.scalar.activation(buf, buf, ACT.Exp, bias=pad_bias[:, b:b + 1], scale=GROK).then_inc(exped, 1)
                        if p == 2 and not last:
                            for k in range(2):
                                pos = AT_X + k
                                split(x_at + k, k, ring.full(n, pos), ring.emptied(n, seq, pos)[1], pos, x_hi, k)
                        if p >= 2:
                            split_attn(p - 2)
                    for g in range(2, UNITS):
                        split_attn(g)

                chunks(act, body)

            @block.vector
            def _(dve):
                ch = Chain(dve, dve_step)
                ch.base = PREP_STEPS

                def norm_stats(n, before):
                    dve.wait_ge(xn_ready, before)
                    for t in range(NT):
                        ch.step(nc.vector.bn_stats(stats[:, t, :], xres[:, n * NT + t, 0:D]))
                    ch.wait()
                    nc.vector.memset(held[:], 0.0)
                    for t in range(NT):
                        ch.step(nc.vector.bn_aggr(mv[:, t, :], stats[:, t, :]))
                    ch.wait()
                    nc.vector.tensor_scalar(var[:], mv[:, :, 1], 1.0 + LN_EPS, LN_EPS * LN_EPS,
                                            ALU.mult, ALU.add).then_inc(var_ready, 1)

                def norm_rows(n):
                    dve.wait_ge(rstd_ready, VAR0 + 1 + n)
                    for t in range(NT):
                        nc.vector.tensor_scalar(xn[:, t, :], xres[:, n * NT + t, 0:D], mv[:, t, 0:1], rstd[:, t:t + 1],
                                                ALU.subtract, ALU.mult).then_inc(xn_ready, 1)

                def rotate(n, g, full, emptied, pos, before):
                    src = bank[pos % 2]
                    dve.wait_ge(bank_full, full)
                    if before is not None:
                        dve.wait_ge(q_ready, before)
                    blocks = range(2 * g, 2 * g + 2)
                    for i, m in enumerate(blocks):
                        nc.vector.scalar_tensor_tensor(q[:, m, :], src[:, i, :], q_bias[:, m:m + 1], rot[:, 0, :], ALU.add, ALU.mult)
                    nc.vector.stream_shuffle(swapped[:], src[:], SWAP).then_inc(freed["dve"], 1)
                    dve.wait_ge(freed["dve"], emptied)
                    for i, m in enumerate(blocks):
                        turned = nc.vector.scalar_tensor_tensor(swapped[:, i, :], swapped[:, i, :], q_bias_swapped[:, m:m + 1],
                                                                rot[:, 1, :], ALU.add, ALU.mult)
                    if g == UNITS - 1:
                        turned.then_inc(rot_used, 1)
                        dve.wait_ge(rot_used, n + 1)
                    else:
                        ch.step(turned)
                        ch.wait()
                    unit = q[:, 2 * g:2 * g + 2, :]
                    nc.vector.tensor_tensor(unit, unit, swapped[:], ALU.add).then_inc(q_ready, 1)

                def mask(n, c, p):
                    dve.wait_ge(exped, n * UNITS + p + 1)
                    first = probs[:, p % 2, :, 0:P]
                    kind = (c + CPBA - 1) // CPBA
                    nc.vector.tensor_tensor(first, first, causal[:, bass.ds(kind, 1), :].to_broadcast([P, 4, KEYS]),
                                            ALU.mult).then_inc(masked, 1)

                def normalise(n, p):
                    for t in range(NT):
                        got = pv_ps[t][:, 0:4 * VW].rearrange("p (h d) -> p h d", d=VW)
                        dve.wait_ge(pv_full, NT * (n * UNITS + p) + t + 1)
                        ch.step(nc.vector.reciprocal(recip[:, t, :], got[:, :, DH0]))
                        ch.wait()
                        out = attn[:, t, p * 4 * DH0:(p + 1) * 4 * DH0].rearrange("p (h d) -> p h d", d=DH0)
                        nc.vector.tensor_tensor(out, got[:, :, 0:DH0], recip[:, t, :].unsqueeze(2).to_broadcast([P, 4, DH0]),
                                                ALU.mult).then_inc(normed, 1)

                dve.wait_ge(ld_x, 16 * CHUNKS)
                norm_stats(0, 1)
                norm_rows(0)
                for g in range(2):
                    rotate(0, g, ring.prefix_full(PRE_Q0 + g), ring.prefix_emptied(PRE_Q0 + g)[1], PRE_Q0 + g, g or None)
                start = ch.base + ch.k

                def body(n, c, b, last):
                    seq, at = LAST if last else BODY, places(last)
                    ch.base, ch.k = start + n * DVE_STEPS, 0

                    def queries(m, g, pos):
                        rotate(m, g, ring.full(n, pos), ring.emptied(n, seq, pos)[1], pos, m * UNITS + g)

                    for p in range(UNITS):
                        mask(n, c, p)
                        if p >= 1:
                            normalise(n, p - 1)
                        if p == 0 and not last:
                            norm_stats(n + 1, 1 + NT * (n + 1))
                        if p == 1 and not last:
                            norm_rows(n + 1)
                        if p < 2:
                            queries(n, p + 2, (AT_Q2, AT_Q3)[p])
                        if p == 3 and not last:
                            dve.wait_ge(ld_rot, 16 * (n + 1))
                            queries(n + 1, 0, at["next"][0])
                    normalise(n, UNITS - 1)
                    if not last:
                        queries(n + 1, 1, at["next"][1])
                    for t in range(NT):
                        pos = at["out"][t]
                        dve.wait_ge(bank_full, ring.full(n, pos))
                        tile = n * NT + t
                        row = xres[:, tile, 0:D]
                        nc.vector.tensor_tensor(row, bank[pos % 2][:].rearrange("p a c -> p (a c)"), row, ALU.add).then_inc(freed["dve"], 1)
                        dve.wait_ge(freed["dve"], ring.emptied(n, seq, pos)[1])
                        ch.step(nc.vector.bn_stats(seen.stats[:, tile, :], row))
                        ch.step(nc.vector.tensor_reduce(seen.top[:, bass.ds(tile, 1)], row, AX.X, ALU.max))
                        ch.step(nc.vector.tensor_reduce(seen.low[:, bass.ds(tile, 1)], row, AX.X, ALU.min))
                    if not last:
                        assert ch.k == DVE_STEPS, (ch.k, DVE_STEPS)

                chunks(dve, body)

            @block.tensor
            def _(pe):
                def begin_prefix(u):
                    who, count = ring.prefix_emptied(u - 2)
                    pe.wait_ge(freed[who], count)
                    return bank[u % 2]

                def begin(n, seq, pos):
                    who, count = ring.reuse(n, seq, pos)
                    pe.wait_ge(freed[who], count)
                    return bank[pos % 2]

                def parts(out, hi, lo, w_hi, w_lo, first, last):
                    nc.tensor.matmul(out, hi, w_hi, start=first, stop=False)
                    nc.tensor.matmul(out, hi, w_lo, start=False, stop=False)
                    return nc.tensor.matmul(out, lo, w_hi, start=False, stop=last)

                def turn(out, rows, first_block):
                    for i in range(2):
                        at = slice((first_block + i) * P, (first_block + i + 1) * P)
                        for t in range(NT):
                            last = nc.tensor.transpose(out[:, i, t * P:(t + 1) * P], rows[:, t, at], ident[:])
                    last.then_inc(bank_full, 1)

                def project(out, g):
                    products = [(w, x, k) for k in range(KB) for w, x in ((wq_hi, x_hi), (wq_hi, x_lo), (wq_lo, x_hi))]
                    for j, (w, x, k) in enumerate(products):
                        for i in range(2):
                            cols = slice((2 * g + i) * P, (2 * g + i + 1) * P)
                            last = nc.tensor.matmul(out[:, i, :], w[:, k, cols], x[:, k, :], start=(j == 0 and i == 0), stop=(j == len(products) - 1 and i == 1))
                    last.then_inc(bank_full, 1)

                def place(h):
                    return h % 2 * 2 + h // 2

                def scores(n, b, p):
                    unit = n * UNITS + p
                    pe.wait_ge(q_ready, unit + 1)
                    if p >= 2:
                        pe.wait_ge(capped, unit - 1)
                    for h in range(4):
                        rows, m = slice(h % 2 * DH0, (h % 2 + 1) * DH0), 2 * p + h // 2
                        last = nc.tensor.matmul(score_ps[:, p % 2, place(h), :], keysT[rows, m, b * KEYS:(b + 1) * KEYS], q[rows, m, :],
                                                start=True, stop=True)
                    last.then_inc(score_full, 1)

                def weigh(n, b, p):
                    unit = n * UNITS + p
                    pe.wait_ge(masked, unit + 1)
                    for t in range(NT):
                        if p >= 1:
                            pe.wait_ge(normed, NT * (unit - 1) + t + 1)
                        for h in range(4):
                            last = nc.tensor.matmul(pv_ps[t][:, h * VW:(h + 1) * VW], probs[:, p % 2, place(h), t * P:(t + 1) * P],
                                                    vals[:, b, 4 * p + h, :], start=True, stop=True)
                        last.then_inc(pv_full, 1)

                pe.wait_ge(xn_ready, 1 + NT)
                for k in range(2):
                    turn(begin_prefix(PRE_T0 + k), xn, 2 * k)
                pe.wait_ge(weight_lo, KB + 1)
                pe.wait_ge(lo_ready, 2)
                for g in range(2):
                    project(begin_prefix(PRE_Q0 + g), g)

                def body(n, c, b, last):
                    seq, at = LAST if last else BODY, places(last)

                    def turn_attn(g):
                        pe.wait_ge(normed, NT * (n * UNITS + g + 1))
                        turn(begin(n, seq, at["attn"][g]), attn, 2 * g)

                    for p in range(UNITS):
                        scores(n, b, p)
                        if p >= 1:
                            weigh(n, b, p - 1)
                        if p < 2:
                            pos = (AT_Q2, AT_Q3)[p]
                            project(begin(n, seq, pos), p + 2)
                        if p == 2 and not last:
                            pe.wait_ge(xn_ready, 1 + NT * (n + 2))
                            for k in range(2):
                                turn(begin(n, seq, AT_X + k), xn, 2 * k)
                        if p >= 2:
                            turn_attn(p - 2)
                        if p == 3 and not last:
                            pe.wait_ge(lo_ready, splits(n, last)[0] + 2)
                            project(begin(n, seq, at["next"][0]), 0)
                    weigh(n, b, UNITS - 1)
                    turn_attn(2)
                    if not last:
                        project(begin(n, seq, at["next"][1]), 1)
                    turn_attn(3)
                    for t in range(NT):
                        out = begin(n, seq, at["out"][t])
                        for k in range(BLOCKS):
                            if t == 0 and k % 2 == 0:
                                pe.wait_ge(lo_ready, splits(n, last)[1] + k // 2 + 1)
                            tokens = slice(t * P, (t + 1) * P)
                            ins = parts(out[:].rearrange("p a c -> p (a c)"), attn_hi[:, k, tokens], attn_lo[:, k, tokens],
                                        wo_hi[:, k, :], wo_lo[:, k, :], k == 0, k == BLOCKS - 1)
                        ins.then_inc(bank_full, 1)

                chunks(pe, body)


INNER = 1408
IT = INNER // P
QMAX = 127.0
MAGIC = 1.5 * 2.0 ** 23


def quantised_ffn_stage(nc, io, xres, ident, seen):
    with ExitStack() as stage:
        def sb(name, shape, dt=F32):
            return stage.enter_context(nc.sbuf_tensor("b_" + name, shape, dt))

        def sem(name):
            return stage.enter_context(nc.semaphore("b_" + name))

        gateT = sb("gateT", [P, KB, INNER], BF16)
        upT = sb("upT", [P, KB, INNER], BF16)
        downT = sb("downT", [P, IT, D], BF16)
        gate_scale, up_scale, down_scale = sb("gate_scale", [P, IT]), sb("up_scale", [P, IT]), sb("down_scale", [P, KB])
        down_row = sb("down_row", [P, D])
        ident16 = sb("ident16", [P, P], BF16)
        clip = sb("clip", [P, 2])
        sigm = sb("sigm", [P, 2])
        mv = sb("mv", [P, TILES, 2])
        rstd = sb("rstd", [P, TILES])
        peak = sb("peak", [P, 1])
        peak_all = sb("peak_all", [P, 1])
        x_scale = sb("x_scale", [P, 1])
        inv_scale = sb("inv_scale", [P, 1])
        h_peak = sb("h_peak", [P, CHUNKS * IT])
        dve_step = sem("dve_step")
        peak_ready, peak_all_ready = sem("peak_ready"), sem("peak_all_ready")
        tr_full, tr_freed = sem("tr_full"), {"act": sem("tr_freed_by_act"), "dve": sem("tr_freed_by_dve")}

        with ExitStack() as early:
            def esb(name, shape, dt=F32):
                return early.enter_context(nc.sbuf_tensor("b_" + name, shape, dt))

            raw = [esb("raw_gate", [P, IT, D]), esb("raw_up", [P, IT, D]), esb("raw_down", [P, KB, INNER])]
            ld_small, ld_w = sem("ld_small"), [sem(f"ld_w{i}") for i in range(3)]
            inv = [esb("inv_gate", [P, IT]), esb("inv_up", [P, IT]), esb("inv_down", [P, KB])]
            scale = [gate_scale, up_scale, down_scale]
            whole = [esb("whole_gate", [P, IT, D], BF16), esb("whole_up", [P, IT, D], BF16), esb("whole_down", [P, KB, INNER], BF16)]
            stats, top, low = seen.stats, seen.top, seen.low
            magic = esb("magic", [P, 1])
            half_minus = esb("half_minus", [P, TILES])
            ones = esb("ones", [P, P])
            diag = esb("diag", [P, KB, P])
            tr_bank = [early.enter_context(nc.psum_tensor(f"b_tr{i}", [P, 4, P], BF16)) for i in range(2)]
            row_ps = early.enter_context(nc.psum_tensor("b_row", [P, D], F32))
            quantised, ident16_ready = sem("quantised"), sem("ident16_ready")
            inv_ready, rounded = sem("inv_ready"), sem("early_rounded")
            var_ready, rstd_ready, half_ready = sem("var_ready"), sem("rstd_ready"), sem("half_ready")
            sig_exp = sem("sig_exp")
            diag_ready, row_full = sem("diag_ready"), sem("row_full")
            uses = [(w, r, range(KB)) for w in range(2) for r in range(IT)]
            uses += [(2, r, range(g, min(g + 4, IT))) for r in range(KB) for g in range(0, IT, 4)]
            rows_before = [0, IT, 2 * IT]

            def user(u):
                return "dve" if uses[u][0] == 2 else "act"

            def turned_weight(u):
                w, r, cols = uses[u]
                at = slice(r * P, (r + 1) * P)
                out = downT[:, cols[0]:cols[-1] + 1, at] if w == 2 else (gateT, upT)[w][:, :, at]
                return out, tr_bank[u % 2][:, 0:len(cols), :]

            with nc.Block() as block:
                @block.sync
                def _(sp):
                    sp.dma_start(clip[:], io["clip"].partition_broadcast(P)).then_inc(ld_small, 16)
                    sp.dma_start(raw[0][:], io["w_gate"].rearrange("(i p) f -> p i f", p=P)).then_inc(ld_w[0], 16)
                    sp.dma_start(raw[1][:], io["w_up"].rearrange("(i p) f -> p i f", p=P)).then_inc(ld_w[1], 16)
                    sp.dma_start(raw[2][:], io["w_down"].rearrange("(k p) i -> p k i", p=P)).then_inc(ld_w[2], 16)

                @block.gpsimd
                def _(pool):
                    nc.gpsimd.memset(half_minus[:], -0.5).then_inc(half_ready, 1)
                    pool.wait_ge(half_ready, 1)
                    pool.wait_ge(var_ready, 1)
                    nc.gpsimd.tensor_tensor(rstd[:], rstd[:], half_minus[:], ALU.pow).then_inc(rstd_ready, 1)
                    pool.wait_ge(peak_ready, 1)
                    nc.gpsimd.partition_all_reduce(peak_all[:], peak[:], P, bass.bass_isa.ReduceOp.max).then_inc(peak_all_ready, 1)

                @block.scalar
                def _(act):
                    def whole_rows(w):
                        act.wait_ge(inv_ready, w + 1)
                        for r in range(raw[w].shape[1]):
                            nc.scalar.activation(raw[w][:, r, :], raw[w][:, r, :], ACT.Identity, bias=magic[:],
                                                 scale=inv[w][:, r:r + 1]).then_inc(rounded, 1)

                    act.wait_ge(ld_small, 16)
                    nc.scalar.activation(sigm[:], clip[:], ACT.Exp, scale=-1.0).then_inc(sig_exp, 1)
                    whole_rows(0)
                    whole_rows(1)
                    for u in range(len(uses)):
                        if u == IT:
                            whole_rows(2)
                        if user(u) == "act":
                            act.wait_ge(tr_full, u + 1)
                            nc.scalar.copy(*turned_weight(u)).then_inc(tr_freed["act"], 1)

                @block.vector
                def _(dve):
                    ch = Chain(dve, dve_step)
                    nc.vector.tensor_copy(ident16[:], ident[:]).then_inc(ident16_ready, 1)
                    nc.vector.memset(magic[:], MAGIC)
                    ch.step(nc.vector.memset(ones[:], 1.0))
                    for t in range(TILES):
                        ch.step(nc.vector.bn_aggr(mv[:, t, :], stats[:, t, :]))
                    ch.wait()
                    nc.vector.tensor_scalar(rstd[:], mv[:, :, 1], LN_EPS, None, ALU.add).then_inc(var_ready, 1)
                    ch.step(nc.vector.tensor_tensor(top[:], top[:], mv[:, :, 0], ALU.subtract))
                    ch.step(nc.vector.tensor_tensor(low[:], mv[:, :, 0], low[:], ALU.subtract))
                    ch.wait()
                    ch.step(nc.vector.tensor_tensor(top[:], top[:], low[:], ALU.max))
                    dve.wait_ge(rstd_ready, 1)
                    ch.wait()
                    ch.step(nc.vector.tensor_tensor(top[:], top[:], rstd[:], ALU.mult))
                    ch.wait()
                    nc.vector.tensor_reduce(peak[:], top[:], AX.X, ALU.max).then_inc(peak_ready, 1)
                    dve.wait_ge(sig_exp, 1)
                    ch.step(nc.vector.tensor_scalar(clip[:], sigm[:], 1.0, None, ALU.add))
                    ch.wait()
                    ch.step(nc.vector.reciprocal(sigm[:], clip[:]))

                    def row_scales(w):
                        dve.wait_ge(ld_w[w], 16)
                        ch.step(nc.vector.tensor_reduce(inv[w][:], raw[w][:], AX.X, ALU.max, apply_absolute_value=True))
                        ch.wait()
                        ch.step(nc.vector.tensor_scalar(scale[w][:], inv[w][:], 1.0 / QMAX, None, ALU.mult))
                        ch.wait()
                        nc.vector.reciprocal(inv[w][:], scale[w][:]).then_inc(inv_ready, 1)

                    def whole_rows(w):
                        for r in range(raw[w].shape[1]):
                            dve.wait_ge(rounded, rows_before[w] + r + 1)
                            nc.vector.tensor_scalar(whole[w][:, r, :], raw[w][:, r, :], MAGIC, QMAX, ALU.subtract, ALU.min).then_inc(quantised, 1)

                    row_scales(0)
                    row_scales(1)
                    whole_rows(0)
                    row_scales(2)
                    for k in range(KB):
                        nc.vector.tensor_scalar(diag[:, k, :], ident[:], down_scale[:, k:k + 1], None, ALU.mult).then_inc(diag_ready, 1)
                    whole_rows(1)
                    dve.wait_ge(peak_all_ready, 1)
                    ch.wait()
                    ch.step(nc.vector.tensor_scalar(x_scale[:], peak_all[:], sigm[:, 0:1], 1.0 / QMAX, ALU.mult, ALU.mult))
                    ch.wait()
                    ch.step(nc.vector.reciprocal(inv_scale[:], x_scale[:]))
                    ch.step(nc.vector.tensor_scalar(gate_scale[:], gate_scale[:], x_scale[:], None, ALU.mult))
                    ch.step(nc.vector.tensor_scalar(up_scale[:], up_scale[:], x_scale[:], None, ALU.mult))
                    ch.wait()
                    ch.step(nc.vector.tensor_scalar(rstd[:], rstd[:], inv_scale[:], None, ALU.mult))
                    whole_rows(2)
                    for u in range(len(uses)):
                        if user(u) == "dve":
                            dve.wait_ge(tr_full, u + 1)
                            nc.vector.tensor_copy(*turned_weight(u)).then_inc(tr_freed["dve"], 1)
                    dve.wait_ge(row_full, 1)
                    ch.step(nc.vector.tensor_copy(down_row[:], row_ps[:]))

                @block.tensor
                def _(pe):
                    pe.wait_ge(ident16_ready, 1)
                    for u, (w, r, cols) in enumerate(uses):
                        pe.wait_ge(quantised, rows_before[w] + r + 1)
                        if u >= 2:
                            pe.wait_ge(tr_freed[user(u - 2)], sum(user(v) == user(u - 2) for v in range(u - 1)))
                        for j, c in enumerate(cols):
                            last = nc.tensor.transpose(tr_bank[u % 2][:, j, :], whole[w][:, r, c * P:(c + 1) * P], ident16[:])
                        last.then_inc(tr_full, 1)
                    pe.wait_ge(diag_ready, KB)
                    for k in range(KB):
                        last = nc.tensor.matmul(row_ps[:, k * P:(k + 1) * P], ones[:], diag[:, k, :], start=True, stop=True)
                    last.then_inc(row_full, 1)

        hidden = sb("hidden", [P, 2, IT, CHUNK])
        spilled = [sem("spilled0"), sem("spilled1")]
        with ExitStack() as mid:
            def msb(name, shape, dt=F32):
                return mid.enter_context(nc.sbuf_tensor("b_" + name, shape, dt))

            scaled = msb("scaled", [P, 2, D])
            whole_x = msb("whole_x", [P, TPC, D], BF16)
            xT = msb("xT", [P, 2, KB, CHUNK], BF16)
            silu = msb("silu", [P, 2, CHUNK])
            scratch = msb("scratch", [P, 6])
            bank = [mid.enter_context(nc.psum_tensor(f"b_bank{i}", [P, CHUNK], BF16)) for i in range(2)]
            gate_ps = mid.enter_context(nc.psum_tensor("b_gate", [P, 2, CHUNK], F32))
            up_ps = mid.enter_context(nc.psum_tensor("b_up", [P, 2, CHUNK], F32))
            x_full, x_freed, x_quant = sem("x_full"), sem("x_freed"), sem("x_quant")
            gate_full, up_full = sem("gate_full"), sem("up_full")
            gate_used, up_used = sem("gate_used"), sem("up_used")
            dve_q = sem("dve_q")
            h_seen = sem("h_seen")
            Q_STEPS = 2 * TPC

            def all_chunks(eng, body):
                with eng.Fori(0, CHUNKS // 2 - 1) as i:
                    for j in range(2):
                        body(2 * i + j, j, False)
                body(CHUNKS - 2, 0, False)
                body(CHUNKS - 1, 1, True)

            with nc.Block() as block:
                @block.sync
                def _(sp):
                    with sp.Fori(0, CHUNKS // 2 - 1) as i:
                        for j in range(2):
                            n = 2 * i + j
                            sp.wait_ge(up_used, 2 + IT * (n + 1))
                            sp.dma_start(io["hidden"][bass.ds(n, 1)].rearrange("o p f -> (o p) f"),
                                         hidden[:, j].rearrange("p i t -> p (i t)")).then_inc(spilled[j], 16)
                    for j in range(2):
                        sp.wait_ge(spilled[j], 16 * (CHUNKS // 2))

                @block.scalar
                def _(act):
                    nc.scalar.copy(scratch[:, 0:1], clip[:, 0:1]).then_inc(gate_used, 1)
                    nc.scalar.copy(scratch[:, 1:2], clip[:, 0:1]).then_inc(gate_used, 1)
                    for k in range(KB):
                        act.wait_ge(x_full, k + 1)
                        nc.scalar.copy(xT[:, 0, k, :], bank[k % 2][:]).then_inc(x_freed, 1)

                    def body(n, j, last):
                        for i in range(IT):
                            k = n * IT + i
                            b = (j * IT + i) % 2
                            act.wait_ge(gate_full, k + 1)
                            act.wait_ge(up_used, k + 1)
                            nc.scalar.activation(silu[:, b, :], gate_ps[:, b, :], ACT.Silu, scale=gate_scale[:, i:i + 1]).then_inc(gate_used, 1)
                            if i >= 7 and not last:
                                act.wait_ge(x_full, KB * (n + 1) + i - 6)
                                nc.scalar.copy(xT[:, 1 - j, i - 7, :], bank[(i - 7) % 2][:]).then_inc(x_freed, 1)

                    all_chunks(act, body)

                @block.vector
                def _(dve):
                    ch = Chain(dve, dve_q)
                    nc.vector.memset(scratch[:, 2:3], 0.0).then_inc(up_used, 1)
                    nc.vector.memset(scratch[:, 3:4], 0.0).then_inc(up_used, 1)
                    nc.vector.memset(scratch[:, 4:5], 0.0).then_inc(spilled[0], 16)
                    nc.vector.memset(scratch[:, 5:6], 0.0).then_inc(spilled[1], 16)

                    def quantise(n, t, done):
                        buf = scaled[:, t % 2, :]
                        if done is not None:
                            dve.wait_ge(x_quant, done)
                        at = n * TPC + t
                        ch.step(nc.vector.tensor_scalar(buf, xres[:, at, 0:D], mv[:, at, 0:1], rstd[:, bass.ds(at, 1)], ALU.subtract, ALU.mult))
                        ch.wait()
                        ch.step(nc.vector.tensor_scalar(buf, buf, MAGIC, MAGIC + QMAX, ALU.add, ALU.min))
                        ch.wait()
                        nc.vector.tensor_scalar(whole_x[:, t, :], buf, MAGIC - QMAX - 1.0, MAGIC, ALU.max, ALU.subtract).then_inc(x_quant, 1)

                    for t in range(TPC):
                        quantise(0, t, t - 1 if t >= 2 else None)

                    def body(n, j, last):
                        ch.base, ch.k = Q_STEPS * (n + 1), 0

                        def greatest(i):
                            dve.wait_ge(up_used, n * IT + i + 3)
                            nc.vector.tensor_reduce(h_peak[:, bass.ds(n * IT + i, 1)], hidden[:, j, i, :], AX.X, ALU.max,
                                                    apply_absolute_value=True).then_inc(h_seen, 1)

                        dve.wait_ge(spilled[j], 16 * ((n + 2 - j) // 2) if isinstance(n, int) else 8 * (n + 2 - j))
                        for i in range(IT):
                            k = n * IT + i
                            b = (j * IT + i) % 2
                            dve.wait_ge(up_full, k + 1)
                            dve.wait_ge(gate_used, k + 3)
                            nc.vector.scalar_tensor_tensor(hidden[:, j, i, :], up_ps[:, b, :], up_scale[:, i:i + 1], silu[:, b, :],
                                                           ALU.mult, ALU.mult).then_inc(up_used, 1)
                            if i >= 1:
                                greatest(i - 1)
                            if i < TPC and not last:
                                quantise(n + 1, i, TPC * (n + 1) + i - 1)
                        greatest(IT - 1)

                    all_chunks(dve, body)

                @block.tensor
                def _(pe):
                    def turn(n, k, count):
                        if count is not None:
                            pe.wait_ge(x_freed, count)
                        for t in range(TPC):
                            last = nc.tensor.transpose(bank[k % 2][:, t * P:(t + 1) * P], whole_x[:, t, k * P:(k + 1) * P], ident16[:])
                        last.then_inc(x_full, 1)

                    pe.wait_ge(x_quant, TPC)
                    for k in range(KB):
                        turn(0, k, k - 1 if k >= 2 else None)

                    def body(n, j, last):
                        pe.wait_ge(x_freed, KB * (n + 1))
                        for i in range(IT):
                            b = (j * IT + i) % 2
                            for ps, w, full, used in ((gate_ps, gateT, gate_full, gate_used), (up_ps, upT, up_full, up_used)):
                                pe.wait_ge(used, n * IT + i + 1)
                                for k in range(KB):
                                    ins = nc.tensor.matmul(ps[:, b, :], w[:, k, i * P:(i + 1) * P], xT[:, j, k, :],
                                                           start=(k == 0), stop=(k == KB - 1))
                                ins.then_inc(full, 1)
                            if i == 6 and not last:
                                pe.wait_ge(x_quant, TPC * (n + 2))
                            if i >= 6 and i < 6 + KB and not last:
                                turn(n + 1, i - 6, KB * (n + 1) + i - 7)

                    all_chunks(pe, body)

        with ExitStack() as late:
            def lsb(name, shape, dt=F32):
                return late.enter_context(nc.sbuf_tensor("b_" + name, shape, dt))

            whole_h = lsb("whole_h", [P, 2, IT, CHUNK], BF16)
            h_scale, h_inv = lsb("h_scale", [P, 1]), lsb("h_inv", [P, 1])
            minus_magic = lsb("minus_magic", [P, 1])
            delta = lsb("delta", [P, 2, D])
            out_ps = late.enter_context(nc.psum_tensor("b_out", [P, 2, D], F32))
            rounded, whole_ready = sem("rounded"), sem("whole_ready")
            out_full, out_freed, added = sem("out_full"), sem("out_freed"), sem("added")
            reloaded = [sem("reloaded0"), sem("reloaded1")]
            h_step = sem("h_step")
            magic_set = sem("magic_set")
            LOOPS = CHUNKS // 2 - 1

            def order(eng, body):
                body(0, 0, CHUNKS - 2, None, True)
                body(1, 1, CHUNKS - 1, 0, True)
                with eng.Fori(0, LOOPS - 1) as i:
                    body(2 * i + 2, 0, 2 * i, i, True)
                    body(2 * i + 3, 1, 2 * i + 1, i + 1, True)
                body(CHUNKS - 2, 0, CHUNKS - 4, LOOPS - 1, True)
                body(CHUNKS - 1, 1, CHUNKS - 3, None, False)

            with nc.Block() as block:
                @block.sync
                def _(sp):
                    with sp.Fori(0, LOOPS) as i:
                        for j in range(2):
                            sp.wait_ge(whole_ready, 2 * i + j + 1)
                            sp.dma_start(hidden[:, j].rearrange("p i t -> p (i t)"),
                                         io["hidden"][bass.ds(2 * i + j, 1)].rearrange("o p f -> (o p) f")).then_inc(reloaded[j], 16)

                @block.gpsimd
                def _(pool):
                    pool.wait_ge(peak_ready, 2)
                    nc.gpsimd.partition_all_reduce(peak_all[:], peak[:], P, bass.bass_isa.ReduceOp.max).then_inc(peak_all_ready, 1)

                    def body(q, j, n, load, more):
                        for t in range(TPC):
                            pool.wait_ge(out_freed, q * TPC + t + 1)
                            row = xres[:, n * TPC + t, 0:D]
                            nc.gpsimd.tensor_tensor(row, row, delta[:, t % 2, :], ALU.add).then_inc(added, 1)

                    order(pool, body)

                @block.scalar
                def _(act):
                    act.wait_ge(magic_set, 1)

                    def body(q, j, n, load, more):
                        act.wait_ge(rounded, q + 1)
                        if not isinstance(q, int) or q >= 2:
                            act.wait_ge(out_full, TPC * (q - 1))
                        nc.scalar.activation(whole_h[:, j], hidden[:, j], ACT.Identity, bias=minus_magic[:]).then_inc(whole_ready, 1)

                    order(act, body)

                @block.vector
                def _(dve):
                    ch = Chain(dve, h_step)
                    nc.vector.memset(minus_magic[:], -MAGIC).then_inc(magic_set, 1)
                    dve.wait_ge(h_seen, CHUNKS * IT)
                    nc.vector.tensor_reduce(peak[:], h_peak[:], AX.X, ALU.max).then_inc(peak_ready, 1)
                    dve.wait_ge(peak_all_ready, 2)
                    ch.step(nc.vector.tensor_scalar(h_scale[:], peak_all[:], sigm[:, 1:2], 1.0 / QMAX, ALU.mult, ALU.mult))
                    ch.wait()
                    ch.step(nc.vector.reciprocal(h_inv[:], h_scale[:]))
                    ch.step(nc.vector.tensor_scalar(down_row[:], down_row[:], h_scale[:], None, ALU.mult))
                    ch.wait()

                    def round_chunk(j):
                        ch.step(nc.vector.tensor_scalar(hidden[:, j], hidden[:, j], h_inv[:], QMAX, ALU.mult, ALU.min))
                        ch.wait()
                        nc.vector.tensor_scalar(hidden[:, j], hidden[:, j], -QMAX - 1.0, MAGIC, ALU.max, ALU.add).then_inc(rounded, 1)

                    round_chunk(0)
                    base = ch.k

                    def body(q, j, n, load, more):
                        ch.base, ch.k = q + base, 0
                        if more:
                            if load is not None:
                                dve.wait_ge(reloaded[1 - j], 16 * (load + 1))
                            round_chunk(1 - j)
                        for t in range(TPC):
                            dve.wait_ge(out_full, q * TPC + t + 1)
                            if not isinstance(q, int) or q or t >= 2:
                                dve.wait_ge(added, q * TPC + t - 1)
                            nc.vector.tensor_tensor(delta[:, t % 2, :], out_ps[:, t % 2, :], down_row[:], ALU.mult).then_inc(out_freed, 1)

                    order(dve, body)

                @block.tensor
                def _(pe):
                    def body(q, j, n, load, more):
                        pe.wait_ge(whole_ready, q + 1)
                        for t in range(TPC):
                            if not isinstance(q, int) or q or t >= 2:
                                pe.wait_ge(out_freed, q * TPC + t - 1)
                            for i in range(IT):
                                ins = nc.tensor.matmul(out_ps[:, t % 2, :], whole_h[:, j, i, t * P:(t + 1) * P], downT[:, i, :],
                                                       start=(i == 0), stop=(i == IT - 1))
                            ins.then_inc(out_full, 1)

                    order(pe, body)


H1, DH1 = 16, 32
VW1 = DH1 + 1
QUADS = H1 // 4
HALF_HEADS = H1 // 2


def masked_attention_stage(nc, io, xres, ident):
    with ExitStack() as stage:
        def sb(name, shape, dt=F32):
            return stage.enter_context(nc.sbuf_tensor("c_" + name, shape, dt))

        def pb(name, shape, dt=F32):
            return stage.enter_context(nc.psum_tensor("c_" + name, shape, dt))

        def sem(name):
            return stage.enter_context(nc.semaphore("c_" + name))

        keys_hi, keys_lo = (sb("keys_" + x, [P, B, QUADS, 4 * KEYS], F32R) for x in ("hi", "lo"))
        vals = sb("vals", [P, B, H1, VW1])
        bias = sb("bias", [P, 2, KB])
        tiny = sb("tiny", [P, 1])
        bo = sb("bo", [P, D])
        wq_hi, wq_lo = (sb("wq_" + x, [P, KB, D], F32R) for x in ("hi", "lo"))
        wo_hi, wo_lo = (sb("wo_" + x, [P, KB, D], F32R) for x in ("hi", "lo"))

        score_ps = pb("score", [P, H1, KEYS])
        bank = [pb(f"bank{i}", [P, CHUNK]) for i in range(2)]
        pv_ps = [pb(f"pv{i}", [P, CHUNK]) for i in range(2)]

        ld_ctx, ld_small, ld_wk, ld_wv, ld_wq, ld_wo = (sem("ld_" + x) for x in ("ctx", "small", "wk", "wv", "wq", "wo"))
        ld_mask, mask_used = sem("ld_mask"), sem("mask_used")
        bank_full = sem("bank_full")
        freed = {"dve": sem("freed_by_dve"), "act": sem("freed_by_act")}
        early_hi, x_hi_ready, q_hi_ready, attn_hi_ready = (sem(x) for x in ("early_hi", "x_hi", "q_hi", "attn_hi"))
        x_lo_ready, attn_lo_ready = sem("x_lo"), sem("attn_lo")
        set_up, half_ready = sem("set_up"), sem("half_ready")
        var_ready, xn_ready, bo_added = sem("var_ready"), sem("xn_ready"), sem("bo_added")
        score_full, shifted, exped = sem("score_full"), sem("shifted"), sem("exped")
        pv_full, normed = sem("pv_full"), sem("normed")
        dve_step, prep_step, rstd_ready = sem("dve_step"), sem("prep_step"), sem("rstd_ready")

        TILE_USES = ["act"] * (1 + QUADS) + ["dve", "act"]
        LAST_TILE_USES = ["act"] * (1 + QUADS + 1) + ["dve"]
        Q_USES = ["dve"] * KB
        PRE = ["act"] * KB + ["dve"] * KB + ["dve"] * B + ["act"] * TPC + Q_USES
        FIRST = ["act"] * (1 + QUADS + 1) + TILE_USES + LAST_TILE_USES + Q_USES
        BODY = TILE_USES * (TPC - 1) + LAST_TILE_USES + Q_USES
        LAST_USES = ["act"] * (1 + QUADS) + ["dve"]
        LAST = LAST_USES * (TPC + 1) + ["act", "dve"]
        ring = Ring(PRE + FIRST, BODY)
        PRE_K, PRE_V, PRE_T, PRE_Q = KB, 2 * KB, 2 * KB + B, 2 * KB + B + TPC
        DVE_STEPS, DVE_HEAD = 6 * TPC, 2

        def plan(n, first, last):
            out, pos = [], 0

            def take(count=1):
                nonlocal pos
                pos += count
                return pos - count

            for t in range(TPC + 2 if last else TPC):
                step = {}
                if not first or t >= 2:
                    step["OT"] = take()
                if (not first or t >= 1) and t <= TPC:
                    step["PT"] = take(QUADS)
                before_queries = t == TPC - 1 and not last
                if before_queries:
                    step["T"] = take()
                if "OT" in step:
                    step["O"] = take()
                if before_queries:
                    step["Q"] = take(KB)
                elif not last:
                    step["T"] = take()
                out.append(step)
            assert pos == len(FIRST if first else LAST if last else BODY)
            return out

        class Uses:

            def __init__(self, n, first, last):
                self.first, self.n = first, 0 if first else n - 1
                self.seq = FIRST if first else LAST if last else BODY

            def full(self, pos):
                return len(PRE) + pos + 1 if self.first else ring.full(self.n, pos)

            def emptied(self, pos):
                return ring.prefix_emptied(len(PRE) + pos) if self.first else ring.emptied(self.n, self.seq, pos)

            def reuse(self, pos):
                return ring.prefix_emptied(len(PRE) + pos - 2) if self.first else ring.reuse(self.n, self.seq, pos)

        def all_chunks(eng, body):
            body(0, 0, True, False)
            with eng.Fori(0, CHUNKS // 2 - 1) as i:
                body(2 * i + 1, 1, False, False)
                body(2 * i + 2, 0, False, False)
            body(CHUNKS - 1, 1, False, True)

        def batch(n):
            return n // CPB

        with ExitStack() as early:
            def esb(name, shape, dt=F32):
                return early.enter_context(nc.sbuf_tensor("c_" + name, shape, dt))

            wk, wv, wq, wo = (esb(x, [P, KB, D]) for x in ("wk", "wv", "wq", "wo"))
            bv = esb("bv", [P, D])
            ctx_t, ctxT = esb("ctx", [P, B, D]), esb("ctxT", [P, KB, B * KEYS])

            with nc.Block() as block:
                @block.sync
                def _(sp):
                    sp.dma_start(ctx_t[:], io["ctx"].rearrange("(b p) f -> p b f", p=P)).then_inc(ld_ctx, 16)
                    for tile, name, s in ((wk, "wk1", ld_wk), (wv, "wv1", ld_wv), (wq, "wq1", ld_wq), (wo, "wo1", ld_wo)):
                        sp.dma_start(tile[:], io[name].rearrange("(k p) n -> p k n", p=P)).then_inc(s, 16)
                        if tile is wk:
                            sp.dma_start(bias[:], io["qk_bias"]).then_inc(ld_small, 16)
                            sp.dma_start(bv[:], io["bv"].partition_broadcast(P)).then_inc(ld_small, 16)
                            sp.dma_start(bo[:], io["bo"].partition_broadcast(P)).then_inc(ld_small, 16)

                @block.scalar
                def _(act):
                    for k in range(KB):
                        act.wait_ge(bank_full, ring.prefix_full(k))
                        nc.scalar.copy(ctxT[:, k, :], bank[k % 2][:, 0:B * KEYS]).then_inc(freed["act"], 1)
                    act.wait_ge(ld_small, 48)
                    act.wait_ge(set_up, 4)
                    for g in range(QUADS):
                        act.wait_ge(bank_full, ring.prefix_full(PRE_K + g))
                        for h in range(4):
                            part = slice(h * DH1, (h + 1) * DH1)
                            last = nc.scalar.activation(keys_hi[part, :, g, h * KEYS:(h + 1) * KEYS],
                                                        bank[(PRE_K + g) % 2][part, 0:B * KEYS].rearrange("p (b k) -> p b k", b=B),
                                                        ACT.Identity, bias=bias[part, 1, g:g + 1])
                        last.then_inc(early_hi, 1)
                    act.wait_ge(ld_wq, 16)
                    nc.scalar.copy(wq_hi[:], wq[:]).then_inc(early_hi, 1)
                    act.wait_ge(ld_wo, 16)
                    nc.scalar.copy(wo_hi[:], wo[:]).then_inc(early_hi, 1)

                @block.vector
                def _(dve):
                    nc.vector.memset(vals[:, :, :, DH1:VW1], 1.0).then_inc(set_up, 1)
                    nc.vector.memset(keys_hi[:].bitcast(F32), 0.0).then_inc(set_up, 1)
                    nc.vector.memset(keys_lo[:].bitcast(F32), 0.0).then_inc(set_up, 1)
                    nc.vector.memset(tiny[:], 1e-9 * DH1 ** 0.5).then_inc(set_up, 1)
                    dve.wait_ge(set_up, 4)
                    dve.wait_ge(ld_small, 48)
                    for g in range(QUADS):
                        dve.wait_ge(early_hi, g + 1)
                        for h in range(4):
                            part = slice(h * DH1, (h + 1) * DH1)
                            at = (part, slice(None), g, slice(h * KEYS, (h + 1) * KEYS))
                            last = nc.vector.scalar_tensor_tensor(keys_lo[at], bank[(PRE_K + g) % 2][part, 0:B * KEYS].rearrange("p (b k) -> p b k", b=B),
                                                                  bias[part, 1, g:g + 1], keys_hi[at], ALU.add, ALU.subtract)
                        last.then_inc(freed["dve"], 1)
                    for b in range(B):
                        dve.wait_ge(bank_full, ring.prefix_full(PRE_V + b))
                        nc.vector.tensor_tensor(vals[:, b, :, 0:DH1], bank[(PRE_V + b) % 2][:].rearrange("p (h d) -> p h d", d=DH1),
                                                bv[:].rearrange("p (h d) -> p h d", d=DH1), ALU.add).then_inc(freed["dve"], 1)
                    for i, (lo, full, hi) in enumerate(((wq_lo, wq, wq_hi), (wo_lo, wo, wo_hi))):
                        dve.wait_ge(early_hi, QUADS + i + 1)
                        nc.vector.tensor_tensor(lo[:], full[:], hi[:], ALU.subtract).then_inc(set_up, 1)

                @block.tensor
                def _(pe):
                    def begin(u):
                        if u >= 2:
                            who, count = ring.prefix_emptied(u - 2)
                            pe.wait_ge(freed[who], count)
                        return bank[u % 2]

                    pe.wait_ge(ld_ctx, 16)
                    for k in range(KB):
                        out = begin(k)
                        for b in range(B):
                            last = nc.tensor.transpose(out[:, b * KEYS:(b + 1) * KEYS], ctx_t[:, b, k * P:(k + 1) * P], ident[:])
                        last.then_inc(bank_full, 1)
                    pe.wait_ge(freed["act"], KB)
                    pe.wait_ge(ld_wk, 16)
                    for m in range(KB):
                        out = begin(PRE_K + m)
                        for k in range(KB):
                            last = nc.tensor.matmul(out[:, 0:B * KEYS], wk[:, k, m * P:(m + 1) * P], ctxT[:, k, :], start=(k == 0), stop=(k == KB - 1))
                        last.then_inc(bank_full, 1)
                    pe.wait_ge(ld_wv, 16)
                    for b in range(B):
                        out = begin(PRE_V + b)
                        for k in range(KB):
                            last = nc.tensor.matmul(out[:], ctxT[:, k, b * KEYS:(b + 1) * KEYS], wv[:, k, :], start=(k == 0), stop=(k == KB - 1))
                        last.then_inc(bank_full, 1)

        masks = sb("masks", [P, 2, TPC, KEYS], U8)
        xn = sb("xn", [P, 2, D])
        x_full, attn_full = sb("x_full", [P, KB, P]), sb("attn_full", [P, KB, P])
        x_hi, x_lo = (sb("x_" + x, [P, KB, CHUNK], F32R) for x in ("hi_parts", "lo_parts"))
        q_hi, q_lo = (sb("q_" + x, [P, KB, CHUNK], F32R) for x in ("hi_parts", "lo_parts"))
        attn_hi, attn_lo = (sb("attn_" + x, [P, KB, P], F32R) for x in ("hi_parts", "lo_parts"))
        stats, mv = sb("stats", [P, 2, 6]), sb("mv", [P, 2, 2])
        var, rstd, minus_half = sb("var", [P, 2]), sb("rstd", [P, 2]), sb("minus_half", [P, 1])
        top = sb("top", [P, H1])
        held = sb("held", [P, 1])
        probs = sb("probs", [P, 2, H1, KEYS])
        probsT = sb("probsT", [P, H1, P])
        recip = sb("recip", [P, 2, HALF_HEADS])
        attn = sb("attn", [P, D])

        with nc.Block() as block:
            @block.sync
            def _(sp):
                def body(n, j, first, last):
                    if not first:
                        sp.wait_ge(mask_used, 2 * TPC * (n - 1) + 1)
                    c = n % CPB
                    sp.dma_start(masks[:, j], io["mask"][bass.ds(c * CHUNK, CHUNK), :].rearrange("(t p) k -> p t k", p=P)).then_inc(ld_mask, 16)

                all_chunks(sp, body)

            @block.gpsimd
            def _(pool):
                nc.gpsimd.memset(minus_half[:], -0.5).then_inc(half_ready, 1)
                pool.wait_ge(half_ready, 1)
                pool.wait_ge(ld_small, 48)

                def deviation(tile, j):
                    pool.wait_ge(var_ready, tile + 1)
                    nc.gpsimd.tensor_tensor(rstd[:, j:j + 1], var[:, j:j + 1], minus_half[:], ALU.pow).then_inc(rstd_ready, 1)

                def add_bias(tile):
                    pool.wait_ge(xn_ready, tile + 1)
                    rows = xres[:, tile, 0:D]
                    nc.gpsimd.tensor_tensor(rows, rows, bo[:], ALU.add).then_inc(bo_added, 1)

                def x_low(tile, t):
                    pool.wait_ge(x_hi_ready, tile + 1)
                    at = (slice(None), slice(None), slice(t * P, (t + 1) * P))
                    nc.gpsimd.tensor_tensor(x_lo[at], x_full[:], x_hi[at], ALU.subtract).then_inc(x_lo_ready, 1)

                def attn_low(tile):
                    pool.wait_ge(attn_hi_ready, tile + 1)
                    nc.gpsimd.tensor_tensor(attn_lo[:], attn_full[:], attn_hi[:], ALU.subtract).then_inc(attn_lo_ready, 1)

                for t in range(TPC):
                    deviation(t, t % 2)
                    add_bias(t)
                    x_low(t, t)

                def body(n, j, first, last):
                    for t, s in enumerate(plan(n, first, last)):
                        tile = n * TPC + t
                        if not last:
                            deviation(tile + TPC, t % 2)
                        if "OT" in s:
                            attn_low(tile - 2)
                        if not last:
                            add_bias(tile + TPC)
                            x_low(tile + TPC, t)

                all_chunks(pool, body)

            @block.scalar
            def _(act):
                def copy(out, full, pos):
                    act.wait_ge(bank_full, full)
                    nc.scalar.copy(out, bank[pos % 2][:]).then_inc(freed["act"], 1)

                def x_tile(tile, t, full, pos, emptied):
                    if not (isinstance(tile, int) and tile < 1):
                        act.wait_ge(x_lo_ready, tile)
                    copy(x_full[:].rearrange("p k c -> p (k c)"), full, pos)
                    act.wait_ge(freed["act"], emptied)
                    nc.scalar.copy(x_hi[:, :, t * P:(t + 1) * P], x_full[:]).then_inc(x_hi_ready, 1)

                def queries(full, at):
                    for m in range(KB):
                        act.wait_ge(bank_full, full(at + m))
                        nc.scalar.activation(q_hi[:, m, :], bank[(at + m) % 2][:], ACT.Identity, bias=bias[:, 0, m:m + 1]).then_inc(q_hi_ready, 1)

                for t in range(TPC):
                    x_tile(t, t, ring.prefix_full(PRE_T + t), PRE_T + t, ring.prefix_emptied(PRE_T + t)[1])
                queries(ring.prefix_full, PRE_Q)

                def body(n, j, first, last):
                    u = Uses(n, first, last)

                    def turned_probs(s, g):
                        pos = s["PT"] + g
                        copy(probsT[:, 4 * g:4 * g + 4, :].rearrange("p h t -> p (h t)"), u.full(pos), pos)

                    def exponentials(tile, t, half):
                        act.wait_ge(shifted, 2 * tile + half + 1)
                        part = probs[:, t % 2, half * HALF_HEADS:(half + 1) * HALF_HEADS, :]
                        nc.scalar.activation(part, part, ACT.Exp, scale=DH1 ** -0.5).then_inc(exped, 1)

                    for t, s in enumerate(plan(n, first, last)):
                        tile = n * TPC + t
                        if "OT" in s:
                            if not first or t > 2:
                                act.wait_ge(attn_lo_ready, tile - 2)
                            copy(attn_full[:].rearrange("p k t -> p (k t)"), u.full(s["OT"]), s["OT"])
                        if "PT" in s:
                            turned_probs(s, 0)
                        if "OT" in s:
                            act.wait_ge(freed["act"], u.emptied(s["OT"])[1])
                            nc.scalar.copy(attn_hi[:], attn_full[:]).then_inc(attn_hi_ready, 1)
                        if "PT" in s:
                            for g in range(1, QUADS):
                                turned_probs(s, g)
                        if t < TPC:
                            exponentials(tile, t, 0)
                        if "T" in s:
                            x_tile(tile + TPC, t, u.full(s["T"]), s["T"], u.emptied(s["T"])[1])
                        if t < TPC:
                            exponentials(tile, t, 1)
                        if "Q" in s:
                            queries(u.full, s["Q"])

                all_chunks(act, body)

            @block.vector
            def _(dve):
                ch = Chain(dve, prep_step)

                def norm_stats(tile, j, first=False):
                    if not first:
                        dve.wait_ge(xn_ready, tile - 1)
                    ch.step(nc.vector.bn_stats(stats[:, j, :], xres[:, tile, 0:D]))
                    ch.wait()
                    nc.vector.memset(held[:], 0.0)
                    ch.step(nc.vector.bn_aggr(mv[:, j, :], stats[:, j, :]))
                    ch.wait()
                    nc.vector.tensor_scalar(var[:, j:j + 1], mv[:, j, 1:2], LN_EPS, None, ALU.add).then_inc(var_ready, 1)

                def norm_row(tile, j, first=False):
                    dve.wait_ge(rstd_ready, tile + 1)
                    if not first:
                        dve.wait_ge(x_hi_ready, tile - 1)
                    nc.vector.tensor_scalar(xn[:, j, :], xres[:, tile, 0:D], mv[:, j, 0:1], rstd[:, j:j + 1],
                                            ALU.subtract, ALU.mult).then_inc(xn_ready, 1)

                def queries(n, at):
                    for m in range(KB):
                        dve.wait_ge(q_hi_ready, n * KB + m + 1)
                        nc.vector.scalar_tensor_tensor(q_lo[:, m, :], bank[(at + m) % 2][:], bias[:, 0, m:m + 1], q_hi[:, m, :],
                                                       ALU.add, ALU.subtract).then_inc(freed["dve"], 1)

                for t in range(TPC):
                    norm_stats(t, t % 2, t < 2)
                    norm_row(t, t % 2, t < 2)
                queries(0, PRE_Q)
                ch = Chain(dve, dve_step)

                def shift(tile, j, t, half):
                    part = slice(half * HALF_HEADS, (half + 1) * HALF_HEADS)
                    shape = [P, HALF_HEADS, KEYS]
                    dve.wait_ge(score_full, 2 * tile + half + 1)
                    nc.vector.memset(held[:], 0.0)
                    ch.step(nc.vector.copy_predicated(score_ps[:, part, :], masks[:, j, t, :].unsqueeze(1).to_broadcast(shape),
                                                      tiny[:].unsqueeze(2).to_broadcast(shape)))
                    ch.wait()
                    nc.vector.tensor_reduce(top[:, part], score_ps[:, part, :], AX.X, ALU.max).then_inc(mask_used, 1)
                    dve.wait_ge(mask_used, 2 * tile + half + 1)
                    nc.vector.tensor_tensor(probs[:, t % 2, part, :], score_ps[:, part, :], top[:, part].unsqueeze(2).to_broadcast(shape),
                                            ALU.subtract).then_inc(shifted, 1)

                def normalise(tile):
                    for half in range(2):
                        got = pv_ps[half][:, 0:HALF_HEADS * VW1].rearrange("p (h d) -> p h d", d=VW1)
                        dve.wait_ge(pv_full, 2 * tile + half + 1)
                        ch.step(nc.vector.reciprocal(recip[:, half, :], got[:, :, DH1]))
                        ch.wait()
                        nc.vector.tensor_tensor(attn[:, half * D // 2:(half + 1) * D // 2].rearrange("p (h d) -> p h d", d=DH1),
                                                got[:, :, 0:DH1], recip[:, half, :].unsqueeze(2).to_broadcast([P, HALF_HEADS, DH1]),
                                                ALU.mult).then_inc(normed, 1)

                def add_out(u, pos, tile):
                    dve.wait_ge(bank_full, u.full(pos))
                    dve.wait_ge(bo_added, tile + 1)
                    row = xres[:, tile, 0:D]
                    nc.vector.tensor_tensor(row, bank[pos % 2][:], row, ALU.add).then_inc(freed["dve"], 1)

                def body(n, j, first, last):
                    u = Uses(n, first, last)
                    ch.base, ch.k = (0, 0) if first else (n * DVE_STEPS - DVE_HEAD, 0)
                    dve.wait_ge(ld_mask, 16 * (n + 1))
                    for t, s in enumerate(plan(n, first, last)):
                        tile = n * TPC + t
                        if not last:
                            norm_stats(tile + TPC, t % 2)
                        if t < TPC:
                            shift(tile, j, t, 0)
                        if not last:
                            norm_row(tile + TPC, t % 2)
                        if t < TPC:
                            shift(tile, j, t, 1)
                        if "PT" in s:
                            normalise(tile - 1)
                        if "O" in s:
                            add_out(u, s["O"], tile - 2)
                        if "Q" in s:
                            queries(n + 1, s["Q"])
                    assert last or ch.k == DVE_STEPS - (DVE_HEAD if first else 0), ch.k

                all_chunks(dve, body)

            @block.tensor
            def _(pe):
                def begin(reuse, pos):
                    pe.wait_ge(freed[reuse[0]], reuse[1])
                    return bank[pos % 2]

                def parts(out, hi, lo, w_hi, w_lo, first=True, last=True):
                    nc.tensor.matmul(out, hi, w_hi, start=first, stop=False)
                    nc.tensor.matmul(out, hi, w_lo, start=False, stop=False)
                    return nc.tensor.matmul(out, lo, w_hi, start=False, stop=last)

                def turn_x(out, j):
                    for k in range(KB):
                        last = nc.tensor.transpose(out[:, k * P:(k + 1) * P], xn[:, j, k * P:(k + 1) * P], ident[:])
                    last.then_inc(bank_full, 1)

                def project(out, m):
                    cols = slice(m * P, (m + 1) * P)
                    for k in range(KB):
                        last = parts(out[:], wq_hi[:, k, cols], wq_lo[:, k, cols], x_hi[:, k, :], x_lo[:, k, :], k == 0, k == KB - 1)
                    last.then_inc(bank_full, 1)

                for t in range(TPC):
                    pe.wait_ge(xn_ready, t + 1)
                    turn_x(begin(ring.prefix_emptied(PRE_T + t - 2), PRE_T + t), t % 2)
                pe.wait_ge(x_lo_ready, TPC)
                for m in range(KB):
                    project(begin(ring.prefix_emptied(PRE_Q + m - 2), PRE_Q + m), m)
                pe.wait_ge(freed["dve"], PRE.count("dve"))

                def scores(n, tile, t, half):
                    if not (isinstance(tile, int) and tile == 0):
                        pe.wait_ge(shifted, 2 * tile - 1 + half)
                    at = slice(t * P, (t + 1) * P)
                    for g in range(2 * half, 2 * half + 2):
                        last = parts(score_ps[:, 4 * g:4 * g + 4, :].rearrange("p h k -> p (h k)"), q_hi[:, g, at], q_lo[:, g, at],
                                     keys_hi[:, batch(n), g, :], keys_lo[:, batch(n), g, :])
                    last.then_inc(score_full, 1)

                def turn_probs(u, s, tile, t, g):
                    pe.wait_ge(exped, 2 * tile + g // 2 + 1)
                    pos = s["PT"] + g
                    out = begin(u.reuse(pos), pos)
                    for h in range(4):
                        last = nc.tensor.transpose(out[:, h * P:(h + 1) * P], probs[:, t % 2, 4 * g + h, :], ident[:])
                    last.then_inc(bank_full, 1)

                def turn_attn(u, s, tile):
                    pe.wait_ge(normed, 2 * (tile + 1))
                    out = begin(u.reuse(s["OT"]), s["OT"])
                    for k in range(KB):
                        last = nc.tensor.transpose(out[:, k * P:(k + 1) * P], attn[:, k * P:(k + 1) * P], ident[:])
                    last.then_inc(bank_full, 1)

                def output(u, s, tile):
                    pe.wait_ge(attn_lo_ready, tile + 1)
                    out = begin(u.reuse(s["O"]), s["O"])
                    for k in range(KB):
                        last = parts(out[:], attn_hi[:, k, :], attn_lo[:, k, :], wo_hi[:, k, :], wo_lo[:, k, :], k == 0, k == KB - 1)
                    last.then_inc(bank_full, 1)

                def weigh(u, s, tile, b):
                    for half in range(2):
                        who, count = u.emptied(s["PT"] + 2 * half + 1)
                        pe.wait_ge(freed[who], count)
                        if not (isinstance(tile, int) and tile == 0):
                            pe.wait_ge(normed, 2 * (tile - 1) + half + 1)
                        for h in range(HALF_HEADS):
                            last = nc.tensor.matmul(pv_ps[half][:, h * VW1:(h + 1) * VW1], probsT[:, half * HALF_HEADS + h, :],
                                                    vals[:, b, half * HALF_HEADS + h, :], start=True, stop=True)
                        last.then_inc(pv_full, 1)

                def queries_done(n):
                    return (PRE + FIRST).count("dve") + BODY.count("dve") * (n - 1)

                def body(n, j, first, last):
                    u = Uses(n, first, last)
                    for t, s in enumerate(plan(n, first, last)):
                        tile = n * TPC + t
                        if t and t < TPC:
                            scores(n, tile, t, 0)
                        if "OT" in s:
                            turn_attn(u, s, tile - 2)
                        if "PT" in s:
                            turn_probs(u, s, tile - 1, t - 1, 0)
                            turn_probs(u, s, tile - 1, t - 1, 1)
                        if not t:
                            if not first:
                                pe.wait_ge(freed["dve"], queries_done(n))
                            scores(n, tile, t, 0)
                        if t < TPC:
                            scores(n, tile, t, 1)
                        if "PT" in s:
                            turn_probs(u, s, tile - 1, t - 1, 2)
                            turn_probs(u, s, tile - 1, t - 1, 3)
                            weigh(u, s, tile - 1, batch(n) if t else batch(n - 1))
                        for what in ("T", "O") if "Q" in s else ("O", "T"):
                            if what == "T" and "T" in s:
                                pe.wait_ge(xn_ready, tile + TPC + 1)
                                turn_x(begin(u.reuse(s["T"]), s["T"]), t % 2)
                            elif what == "O" and "O" in s:
                                output(u, s, tile - 2)
                        if "Q" in s:
                            pe.wait_ge(x_lo_ready, TPC * (n + 2))
                            for m in range(KB):
                                project(begin(u.reuse(s["Q"] + m), s["Q"] + m), m)
                all_chunks(pe, body)


EXPERTS = 8
SLOT_TILES = TILES + EXPERTS
MAP_ROWS = EXPERTS * TILES + EXPERTS
MAP = MAP_ROWS * P


def expert_stage(nc, io, xres, ident):
    G = 8
    LAG = 5
    with ExitStack() as stage:
        def sb(name, shape, dt=F32):
            return stage.enter_context(nc.sbuf_tensor("d_" + name, shape, dt))

        def sem(name):
            return stage.enter_context(nc.semaphore("d_" + name))

        we = sb("we", [P, EXPERTS, KB, D])
        token_of = sb("token_of", [P, SLOT_TILES], U32)
        tile_expert = sb("tile_expert", [1, SLOT_TILES], U32)
        ld_we, ld_be = sem("ld_we"), sem("ld_be")
        rows_out = sem("rows_out")

        with ExitStack() as early:
            def esb(name, shape, dt=F32):
                return early.enter_context(nc.sbuf_tensor("d_" + name, shape, dt))

            def epb(name, shape, dt=F32):
                return early.enter_context(nc.psum_tensor("d_" + name, shape, dt))

            wg, wg_hi, wg_lo = esb("wg", [P, KB, D]), esb("wg_hi", [P, KB, D], F32R), esb("wg_lo", [P, KB, D], F32R)
            bg, bg_parts, ones_r = esb("bg", [P, D]), esb("bg_parts", [P, D], F32R), esb("ones_r", [P, P], F32R)
            upper_f, upper, ones = esb("upper_f", [P, P]), esb("upper", [P, P], BF16), esb("ones", [P, P], BF16)
            ones_f = esb("ones_f", [P, P])
            token_id = esb("token_id", [P, TPC])
            numbers = esb("numbers", [P, TPC, EXPERTS])
            base_f, base = esb("base_f", [P, TPC, EXPERTS]), esb("base", [P, TPC, EXPERTS], BF16)
            nobody = esb("nobody", [P, MAP_ROWS])
            slot_at = esb("slot_at", [SLOT_TILES, 1])
            stats, mv = esb("stats", [P, TPC, 6]), esb("mv", [P, TPC, 2])
            minus_half, minus_one, shifted = esb("minus_half", [P, TPC]), esb("minus_one", [P, TPC]), esb("shifted", [P, 2, TPC])
            xn = esb("xn", [P, TPC, D])
            x_hi, x_lo = esb("x_hi", [P, 2, KB, CHUNK], F32R), esb("x_lo", [P, 2, KB, CHUNK], F32R)
            exped = esb("exped", [P, D])
            best, where = esb("best", [P, TPC, 8]), esb("where", [P, TPC, 8], U32)
            minus_best, total = esb("minus_best", [P, TPC]), esb("total", [P, TPC])
            held = esb("held", [P, 1])
            pool_held = esb("early_pool_held", [P, 3])
            expert_i, expert = esb("expert_i", [P, TPC], U32), esb("expert", [P, TPC])
            onehot = esb("onehot", [P, TPC, EXPERTS], BF16)
            earlier = esb("earlier", [P, TPC + 1, EXPERTS], BF16)
            rank = esb("rank", [P, TPC, EXPERTS])
            slot, slot_u, token = esb("slot", [P, TPC]), esb("slot_u", [P, 2, TPC], U32), esb("token", [P, 2, TPC])
            counts, padded, padded_i, end = esb("counts", [P, EXPERTS]), esb("padded", [P, EXPERTS]), esb("padded_i", [P, EXPERTS], I32), esb("end", [P, EXPERTS])
            passed, start_of = esb("passed", [SLOT_TILES, EXPERTS - 1]), esb("start_of", [SLOT_TILES, EXPERTS - 1])
            expert_of, start_at = esb("expert_of", [SLOT_TILES, 1]), esb("start_at", [SLOT_TILES, 1])
            map_row, map_row_u = esb("map_row", [SLOT_TILES, 1]), esb("map_row_u", [SLOT_TILES, 1], U32)
            owner = esb("owner", [SLOT_TILES, P])
            bank = [epb(f"bank{i}", [P, CHUNK]) for i in range(2)]
            logit_ps = epb("logit", [P, TPC, D])
            rank_ps = epb("rank_ps", [P, TPC * EXPERTS])
            owner_ps = epb("owner_ps", [P, 2, P])
            ld_small, ld_wg = sem("ld_small"), sem("ld_wg")
            half_ready, pad_set, wg_split = sem("half_ready"), sem("pad_set"), sem("wg_split")
            var_ready, rstd_ready, xn_ready = sem("var_ready"), sem("rstd_ready"), sem("xn_ready")
            turned, hi_ready, lo_ready = sem("turned"), sem("hi_ready"), sem("lo_ready")
            logit_full, best_ready, summed, row_ready = (sem(x) for x in ("logit_full", "best_ready", "summed", "row_ready"))
            map_cleared, hot_ready, ranked, slots_ready = (sem(x) for x in ("map_cleared", "hot_ready", "ranked", "slots_ready"))
            scattered = [sem("scattered0"), sem("scattered1")]
            early_held, rows_found, owner_loaded, owner_turned = sem("early_held"), sem("rows_found"), sem("owner_loaded"), sem("owner_turned")
            gate_step, place_step, last_step = sem("gate_step"), sem("place_step"), sem("last_step")
            HALF = P // 2
            LD_SMALL, PADS, NORM_STEPS, STEPS, PLACE_STEPS = 7 * 16, 8, 2 * TPC + 1, 4 * TPC + 8, 3

            def pairs(eng, body):
                body(0, 0, True, False)
                body(1, 1, False, False)
                with eng.Fori(1, CHUNKS // 2 - 1) as i:
                    body(2 * i, 0, False, False)
                    body(2 * i + 1, 1, False, False)
                body(CHUNKS - 2, 0, False, False)
                body(CHUNKS - 1, 1, False, True)

            def more(n):
                return not isinstance(n, int) or n + 2 < CHUNKS

            with nc.Block() as block:
                @block.sync
                def _(sp):
                    sp.dma_start(wg[:], io["wg"].rearrange("(k p) n -> p k n", p=P)).then_inc(ld_wg, 16)
                    for tile, name in ((nobody, "nobody"), (upper_f, "upper"), (token_id, "token_id"), (numbers, "numbers"),
                                       (base_f, "map_base"), (slot_at, "slot_at")):
                        sp.dma_start(tile[:], io[name]).then_inc(ld_small, 16)
                    sp.dma_start(bg[:], io["bg"].partition_broadcast(P)).then_inc(ld_small, 16)
                    sp.wait_ge(ld_small, LD_SMALL)
                    sp.dma_start(io["owner"].rearrange("(p j) o -> p (j o)", p=P), nobody[:]).then_inc(map_cleared, 16)
                    for e in range(EXPERTS):
                        sp.dma_start(we[:, e], io["we"][e].rearrange("(k p) n -> p k n", p=P)).then_inc(ld_we, 16)
                    with sp.Fori(0, CHUNKS) as n:
                        sp.wait_ge(row_ready, n + 1)
                        sp.dma_start(io["rows"][bass.ds(n * CHUNK, CHUNK), :].rearrange("(t p) f -> p t f", p=P),
                                     xres[:, bass.ds(n * TPC, TPC), :]).then_inc(rows_out, 16)
                    sp.wait_ge(rows_out, 16 * CHUNKS)

                @block.gpsimd
                def _(pool):
                    nc.gpsimd.memset(minus_half[:], -0.5).then_inc(half_ready, 1)
                    nc.gpsimd.memset(minus_one[:], -1.0).then_inc(half_ready, 1)
                    nc.gpsimd.memset(pool_held[:], 0.0).then_inc(early_held, 1)
                    pool.wait_ge(half_ready, 2)
                    pool.wait_ge(early_held, 1)

                    def spread(n, j):
                        pool.wait_ge(var_ready, n + 1)
                        at = bass.ds(n * TPC, TPC)
                        rstd = xres[:, at, COL_RSTD]
                        nc.gpsimd.tensor_tensor(rstd, rstd, minus_half[:], ALU.pow).then_inc(half_ready, 1)
                        pool.wait_ge(half_ready, 2 * n + 3)
                        nc.gpsimd.tensor_tensor(shifted[:, j], xres[:, at, COL_MEAN], rstd, ALU.mult).then_inc(half_ready, 1)
                        pool.wait_ge(half_ready, 2 * n + 4)
                        nc.gpsimd.tensor_tensor(shifted[:, j], shifted[:, j], minus_one[:], ALU.mult).then_inc(rstd_ready, 1)

                    def scatter(n, j, first):
                        pool.wait_ge(slots_ready, n + 1)
                        if not first:
                            pool.wait_ge(scattered[1 - j], 16 * TPC * ((n - 1) // 2 + 1))
                        pool.wait_ge(early_held, n + 1)
                        nc.gpsimd.tensor_tensor(pool_held[:, 2:3], pool_held[:, 0:1], pool_held[:, 1:2], ALU.add).then_inc(early_held, 1)
                        for t in range(TPC):
                            nc.gpsimd.indirect_dma_start(out=io["owner"], out_offset=bass.IndirectOffsetOnAxis(ap=slot_u[:, j, t:t + 1], axis=0),
                                                         in_=token[:, j, t:t + 1], in_offset=None).then_inc(scattered[j], 16)

                    def body(n, j, first, last):
                        if more(n):
                            spread(n + 2, j)
                        if first:
                            pool.wait_ge(map_cleared, 16)
                        scatter(n, j, first)

                    spread(0, 0)
                    spread(1, 1)
                    pairs(pool, body)
                    for j in range(2):
                        pool.wait_ge(scattered[j], 16 * TILES // 2)
                    pool.wait_ge(rows_found, 1)
                    nc.gpsimd.indirect_dma_start(out=owner[:], out_offset=None, in_=io["owner"].rearrange("(j p) o -> j (p o)", p=P),
                                                 in_offset=bass.IndirectOffsetOnAxis(ap=map_row_u[:], axis=0)).then_inc(owner_loaded, 16)
                    pool.wait_ge(owner_loaded, 16)

                @block.scalar
                def _(act):
                    def norm_rows(n, j):
                        act.wait_ge(rstd_ready, n + 1)
                        for t in range(TPC):
                            at = n * TPC + t
                            nc.scalar.activation(xn[:, t, :], xres[:, at, 0:D], ACT.Identity, bias=shifted[:, j, t:t + 1],
                                                 scale=xres[:, at, COL_RSTD:COL_RSTD + 1]).then_inc(xn_ready, 1)

                    def take_hi(n, j, k):
                        act.wait_ge(turned, KB * n + k + 1)
                        nc.scalar.copy(x_hi[:, j, k, :], bank[k % 2][:]).then_inc(hi_ready, 1)

                    act.wait_ge(ld_wg, 16)
                    nc.scalar.copy(wg_hi[:], wg[:]).then_inc(wg_split, 1)
                    norm_rows(0, 0)
                    for k in range(KB):
                        take_hi(0, 0, k)

                    def body(n, j, first, last):
                        for t in range(TPC):
                            tile = n * TPC + t
                            if t == 0 and not last:
                                act.wait_ge(turned, KB * (n + 1))
                                norm_rows(n + 1, 1 - j)
                            if t == 2 and not last:
                                for k in range(KB):
                                    take_hi(n + 1, 1 - j, k)
                            act.wait_ge(best_ready, tile + 1)
                            if not first or t:
                                act.wait_ge(summed, tile)
                            nc.scalar.activation(exped[:], logit_ps[:, t, :], ACT.Exp, bias=minus_best[:, t:t + 1],
                                                 accum_out=total[:, t:t + 1]).then_inc(summed, 1)

                    pairs(act, body)

                @block.vector
                def _(dve):
                    ch = Chain(dve, gate_step)
                    ch.step(nc.vector.memset(ones_f[:], 1.0))
                    nc.vector.memset(ones[:], 1.0).then_inc(pad_set, 1)
                    nc.vector.memset(earlier[:], 0.0).then_inc(pad_set, 1)
                    nc.vector.memset(xres[:, :, COL_RSTD + 1:ROW], 0.0).then_inc(pad_set, 1)

                    def norm_stats(n):
                        for t in range(TPC):
                            ch.step(nc.vector.bn_stats(stats[:, t, :], xres[:, n * TPC + t, 0:D]))
                        ch.wait()
                        nc.vector.memset(held[:], 0.0)
                        for t in range(TPC):
                            ch.step(nc.vector.bn_aggr(mv[:, t, :], stats[:, t, :]))
                        ch.wait()
                        ch.step(nc.vector.tensor_copy(xres[:, bass.ds(n * TPC, TPC), COL_MEAN:COL_RSTD + 1], mv[:]))
                        ch.wait()
                        variance = xres[:, bass.ds(n * TPC, TPC), COL_RSTD]
                        nc.vector.tensor_scalar(variance, variance, LN_EPS, None, ALU.add).then_inc(var_ready, 1)

                    def take_lo(n, j, k):
                        dve.wait_ge(hi_ready, KB * n + k + 1)
                        nc.vector.tensor_tensor(x_lo[:, j, k, :], bank[k % 2][:], x_hi[:, j, k, :], ALU.subtract).then_inc(lo_ready, 1)

                    norm_stats(0)
                    norm_stats(1)
                    dve.wait_ge(wg_split, 1)
                    nc.vector.tensor_tensor(wg_lo[:], wg[:], wg_hi[:], ALU.subtract).then_inc(wg_split, 1)
                    for k in range(KB):
                        take_lo(0, 0, k)
                    dve.wait_ge(ld_small, LD_SMALL)
                    ch.wait()
                    nc.vector.tensor_copy(ones_r[:], ones_f[:]).then_inc(pad_set, 1)
                    ch.step(nc.vector.tensor_copy(bg_parts[:], bg[:]))
                    ch.wait()
                    ch.step(nc.vector.tensor_tensor(bg[:], bg[:], bg_parts[:], ALU.subtract))
                    ch.wait()
                    nc.vector.tensor_scalar(bg_parts[0:HALF], bg_parts[0:HALF], 1.0 / HALF, None, ALU.mult).then_inc(pad_set, 1)
                    nc.vector.tensor_scalar(bg_parts[HALF:P], bg[HALF:P], 1.0 / HALF, None, ALU.mult).then_inc(pad_set, 1)
                    nc.vector.tensor_copy(upper[:], upper_f[:]).then_inc(pad_set, 1)
                    nc.vector.tensor_copy(base[:], base_f[:]).then_inc(pad_set, 1)
                    ch.step(nc.vector.tensor_scalar(token[:, 1, :], token_id[:], -float(CHUNK), None, ALU.add))
                    start = ch.k

                    def places(n, j):
                        pl = Chain(dve, place_step, PLACE_STEPS * n)
                        dve.wait_ge(early_held, n + 1)
                        pl.step(nc.vector.tensor_scalar(token[:, j, :], token[:, 1 - j, :], float(CHUNK), None, ALU.add))
                        dve.wait_ge(ranked, n + 1)
                        pl.step(nc.vector.tensor_tensor(rank[:], rank_ps[:].rearrange("p (t e) -> p t e", e=EXPERTS), onehot[:], ALU.mult))
                        pl.wait()
                        pl.step(nc.vector.tensor_reduce(slot[:], rank[:], AX.X, ALU.add))
                        pl.wait()
                        nc.vector.tensor_copy(slot_u[:, j, :], slot[:]).then_inc(slots_ready, 1)
                        assert pl.k == PLACE_STEPS

                    def body(n, j, first, last):
                        ch.base, ch.k = start + STEPS * n - (NORM_STEPS if last else 0), 0
                        for t in range(TPC):
                            tile = n * TPC + t
                            if t == 2 and not first:
                                places(n - 1, 1 - j)
                            if t == 2 and not last:
                                for k in range(KB):
                                    take_lo(n + 1, 1 - j, k)
                            dve.wait_ge(logit_full, tile + 1)
                            nc.vector.memset(held[:], 0.0)
                            ch.step(nc.vector.max(best[:, t, :], logit_ps[:, t, :]))
                            ch.wait()
                            ch.step(nc.vector.tensor_scalar(minus_best[:, t:t + 1], best[:, t, 0:1], -1.0, None, ALU.mult))
                            nc.vector.max_index(where[:, t, :], best[:, t, :], logit_ps[:, t, :]).then_inc(best_ready, 1)
                            if t == 1 and more(n):
                                norm_stats(n + 2)
                        dve.wait_ge(best_ready, TPC * (n + 1))
                        ch.step(nc.vector.tensor_scalar(expert_i[:], where[:, :, 0], EXPERTS - 1, None, ALU.bitwise_and))
                        ch.wait()
                        ch.step(nc.vector.tensor_copy(expert[:], expert_i[:]))
                        if not first:
                            dve.wait_ge(ranked, n)
                            nc.vector.tensor_copy(earlier[:, 0, :], earlier[:, TPC, :]).then_inc(pad_set, 1)
                            dve.wait_ge(pad_set, PADS + n)
                        ch.wait()
                        ch.step(nc.vector.tensor_tensor(onehot[:], numbers[:], expert[:].unsqueeze(2).to_broadcast([P, TPC, EXPERTS]), ALU.is_equal))
                        for t in range(TPC):
                            ch.wait()
                            add = nc.vector.tensor_tensor(earlier[:, t + 1, :], earlier[:, t, :], onehot[:, t, :], ALU.add)
                            if t < TPC - 1:
                                ch.step(add)
                        add.then_inc(hot_ready, 1)
                        dve.wait_ge(summed, TPC * (n + 1))
                        ch.step(nc.vector.reciprocal(stats[:, :, 0], total[:]))
                        ch.wait()
                        nc.vector.tensor_copy(xres[:, bass.ds(n * TPC, TPC), COL_P], stats[:, :, 0]).then_inc(row_ready, 1)
                        dve.wait_ge(row_ready, n + 1)
                        assert ch.k == STEPS - (0 if more(n) else NORM_STEPS), ch.k

                    pairs(dve, body)
                    places(CHUNKS - 1, 1)

                    ch = Chain(dve, last_step)
                    dve.wait_ge(ranked, CHUNKS + 1)
                    ch.step(nc.vector.tensor_copy(counts[:], owner_ps[:, 1, HALF:HALF + EXPERTS]))
                    ch.wait()
                    ch.step(nc.vector.tensor_scalar(padded[:], counts[:], float(P - 1), None, ALU.add))
                    ch.wait()
                    ch.step(nc.vector.tensor_copy(padded_i[:], padded[:]))
                    ch.wait()
                    ch.step(nc.vector.tensor_scalar(padded_i[:], padded_i[:], 7, 7, ALU.arith_shift_right, ALU.logical_shift_left))
                    ch.wait()
                    ch.step(nc.vector.tensor_copy(padded[:], padded_i[:]))
                    ch.wait()
                    ch.step(nc.vector.tensor_tensor_scan(end[:], ones_f[:, 0:EXPERTS], padded[:], 0.0, ALU.mult, ALU.add))
                    ch.wait()
                    ends = end[0:SLOT_TILES, 0:EXPERTS - 1]
                    ch.step(nc.vector.tensor_scalar(passed[:], ends, slot_at[:], None, ALU.is_le))
                    ch.wait()
                    ch.step(nc.vector.tensor_reduce(expert_of[:], passed[:], AX.X, ALU.add))
                    ch.step(nc.vector.tensor_tensor(start_of[:], passed[:], ends, ALU.mult))
                    ch.wait()
                    ch.step(nc.vector.tensor_reduce(start_at[:], start_of[:], AX.X, ALU.max))
                    ch.wait()
                    ch.step(nc.vector.tensor_tensor(start_at[:], slot_at[:], start_at[:], ALU.subtract))
                    ch.step(nc.vector.tensor_scalar(map_row[:], expert_of[:], float(TILES), None, ALU.mult))
                    ch.wait()
                    ch.step(nc.vector.scalar_tensor_tensor(map_row[:], start_at[:], 1.0 / P, map_row[:], ALU.mult, ALU.add))
                    ch.wait()
                    nc.vector.tensor_copy(map_row_u[:], map_row[:]).then_inc(rows_found, 1)
                    dve.wait_ge(owner_turned, 2)
                    ch.step(nc.vector.tensor_copy(tile_expert[:], owner_ps[0:1, 1, 0:SLOT_TILES]))
                    ch.step(nc.vector.tensor_copy(token_of[:], owner_ps[:, 0, 0:SLOT_TILES]))

                @block.tensor
                def _(pe):
                    def turn(n, k, first=False):
                        if not first or k >= 2:
                            pe.wait_ge(lo_ready, KB * n + k - 1)
                        for t in range(TPC):
                            last = nc.tensor.transpose(bank[k % 2][:, t * P:(t + 1) * P], xn[:, t, k * P:(k + 1) * P], ident[:])
                        last.then_inc(turned, 1)

                    pe.wait_ge(xn_ready, TPC)
                    for k in range(KB):
                        turn(0, k, True)
                    pe.wait_ge(wg_split, 2)
                    pe.wait_ge(pad_set, PADS)

                    def rank_rows(n):
                        pe.wait_ge(hot_ready, n + 1)
                        hot = onehot[:].rearrange("p t e -> p (t e)")
                        nc.tensor.matmul(rank_ps[:], upper[:], hot, start=True, stop=False)
                        nc.tensor.matmul(rank_ps[:], ones[:], earlier[:, 0:TPC, :].rearrange("p t e -> p (t e)"), start=False, stop=False)
                        nc.tensor.matmul(rank_ps[:], ones[:], base[:].rearrange("p t e -> p (t e)"), start=False, stop=True).then_inc(ranked, 1)

                    def body(n, j, first, last):
                        pe.wait_ge(lo_ready, KB * (n + 1))
                        for t in range(TPC):
                            tile = n * TPC + t
                            if not first:
                                pe.wait_ge(summed, tile - 3)
                            out = logit_ps[:, t, :]
                            nc.tensor.matmul(out, ones_r[:], bg_parts[:], start=True, stop=False)
                            for k in range(KB):
                                hi, lo = (x[:, j, k, t * P:(t + 1) * P] for x in (x_hi, x_lo))
                                nc.tensor.matmul(out, hi, wg_hi[:, k, :], start=False, stop=False)
                                nc.tensor.matmul(out, hi, wg_lo[:, k, :], start=False, stop=False)
                                ins = nc.tensor.matmul(out, lo, wg_hi[:, k, :], start=False, stop=(k == KB - 1))
                            ins.then_inc(logit_full, 1)
                            if t == 1 and not last:
                                pe.wait_ge(xn_ready, TPC * (n + 2))
                                for k in range(KB):
                                    turn(n + 1, k)
                            if t == 0 and not first:
                                rank_rows(n - 1)

                    pairs(pe, body)
                    rank_rows(CHUNKS - 1)
                    nc.tensor.matmul(owner_ps[:, 1, HALF:HALF + EXPERTS], ones[:], earlier[:, TPC, :], start=True, stop=True).then_inc(ranked, 1)
                    pe.wait_ge(rows_found, 1)
                    nc.tensor.transpose(owner_ps[0:1, 1, 0:SLOT_TILES], expert_of[:], ident[0:SLOT_TILES, 0:SLOT_TILES]).then_inc(owner_turned, 1)
                    pe.wait_ge(owner_loaded, 16)
                    nc.tensor.transpose(owner_ps[:, 0, 0:SLOT_TILES], owner[:], ident[0:SLOT_TILES, 0:SLOT_TILES]).then_inc(owner_turned, 1)

        with ExitStack() as late:
            def lsb(name, shape, dt=F32):
                return late.enter_context(nc.sbuf_tensor("d_" + name, shape, dt))

            held = lsb("pool_held", [P, 3])
            be = lsb("be", [P, EXPERTS, D])
            got = [lsb(f"got{i}", [P, ROW]) for i in range(G)]
            token = [lsb(f"token{i}", [P, 1], U32) for i in range(G)]
            xn = lsb("slot_xn", [P, 2, D])
            xT = lsb("slot_xT", [P, 2, KB, P])
            y = [lsb(f"y{i}", [P, D]) for i in range(G)]
            turn_ps = late.enter_context(nc.psum_tensor("d_turn", [P, 2, D], F32))
            y_ps = late.enter_context(nc.psum_tensor("d_y", [P, 2, D], F32))
            got_clear, token_ready, held_set = sem("got_clear"), sem("token_ready"), sem("held_set")
            gathered = [sem(f"gathered{i}") for i in range(G)]
            stored = [sem(f"stored{i}") for i in range(G)]
            xn_ready, turned, xT_ready, y_full, y_used, y_ready = (sem("slot_" + x) for x in ("xn", "turned", "xT", "y_full", "y_used", "y_ready"))
            y_step = sem("y_step")
            ROUNDS = SLOT_TILES // G

            def rounds(eng, body):
                for u in range(G):
                    body(u, 0, u, True, False)
                with eng.Fori(1, ROUNDS - 1) as i:
                    for u in range(G):
                        body(G * i + u, i, u, False, False)
                for u in range(G):
                    body(SLOT_TILES - G + u, ROUNDS - 1, u, False, True)

            with nc.Block() as block:
                @block.sync
                def _(sp):
                    sp.dma_start(be[:].rearrange("p e n -> p (e n)"), io["be"].partition_broadcast(P)).then_inc(ld_be, 16)

                @block.gpsimd
                def _(pool):
                    nc.gpsimd.memset(held[:], 0.0).then_inc(held_set, 1)

                    def hold(before):
                        pool.wait_ge(held_set, 1 + before)
                        nc.gpsimd.tensor_tensor(held[:, 2:3], held[:, 0:1], held[:, 1:2], ALU.add).then_inc(held_set, 1)

                    def gather(i, u, before):
                        pool.wait_ge(token_ready, G * i + u + 1)
                        hold(before)
                        nc.gpsimd.indirect_dma_start(out=got[u][:], out_offset=None, in_=io["rows"],
                                                     in_offset=bass.IndirectOffsetOnAxis(ap=token[u][:], axis=0),
                                                     bounds_check=TOK - 1, oob_is_err=False).then_inc(gathered[u], 16)

                    def scatter(j, u, before):
                        pool.wait_ge(y_ready, j + 1)
                        hold(before)
                        nc.gpsimd.indirect_dma_start(out=io["out"], out_offset=bass.IndirectOffsetOnAxis(ap=token[u][:], axis=0),
                                                     in_=y[u][:], in_offset=None, bounds_check=TOK - 1,
                                                     oob_is_err=False).then_inc(stored[u], 16)

                    for u in range(G):
                        pool.wait_ge(got_clear, u + 1)
                        gather(0, u, u)

                    def body(j, i, u, first, last):
                        more = SLOT_TILES - G if last and u >= LAG else 0 if first and u < LAG else j - LAG
                        if not (first and u < 2):
                            scatter(j - 2, (u - 2) % G, G + j - 2 + more)
                        if u >= LAG and not last:
                            gather(i + 1, u - LAG, G + j - 1 + more)
                        elif u < LAG and not first:
                            gather(i, u - LAG + G, G + j - 1 + more)

                    rounds(pool, body)
                    for j in (SLOT_TILES - 2, SLOT_TILES - 1):
                        scatter(j, j % G, SLOT_TILES + j)
                    for u in range(G):
                        pool.wait_ge(stored[u], 16 * ROUNDS)

                @block.scalar
                def _(act):
                    def body(j, i, u, first, last):
                        act.wait_ge(turned, j + 1)
                        if not first or u >= 2:
                            act.wait_ge(y_full, j - 1)
                        nc.scalar.copy(xT[:, u % 2].rearrange("p k t -> p (k t)"), turn_ps[:, u % 2, :]).then_inc(xT_ready, 1)

                    rounds(act, body)

                @block.vector
                def _(dve):
                    ch = Chain(dve, y_step)
                    for u in range(G):
                        nc.vector.memset(got[u][:], 0.0).then_inc(got_clear, 1)
                        nc.vector.tensor_copy(token[u][:], token_of[:, u:u + 1]).then_inc(token_ready, 1)
                    dve.wait_ge(ld_be, 16)

                    def norm(j, i, u, first):
                        dve.wait_ge(gathered[u], 16 * (i + 1))
                        if not first or u >= 2:
                            dve.wait_ge(turned, j - 1)
                        nc.vector.tensor_scalar(xn[:, u % 2, :], got[u][:, 0:D], got[u][:, COL_MEAN:COL_MEAN + 1],
                                                got[u][:, COL_RSTD:COL_RSTD + 1], ALU.subtract, ALU.mult).then_inc(xn_ready, 1)

                    def finish(j, u):
                        expert = dve.value_load(tile_expert[0:1, bass.ds(j, 1)], min_val=0, max_val=EXPERTS - 1)
                        dve.wait_ge(y_full, j + 1)
                        nc.vector.tensor_tensor(y[u][:], y_ps[:, u % 2, :], be[:, expert, :], ALU.add).then_inc(y_used, 1)
                        dve.wait_ge(y_used, j + 1)
                        ch.base, ch.k = j, 0
                        ch.step(nc.vector.tensor_scalar(y[u][:], y[u][:], 0.0, got[u][:, COL_P:COL_P + 1], ALU.max, ALU.mult))
                        ch.wait()
                        nc.vector.tensor_tensor(y[u][:], y[u][:], got[u][:, 0:D], ALU.add).then_inc(y_ready, 1)

                    def next_token(j, i, u):
                        dve.wait_ge(stored[u], 16 * (i + 1))
                        nc.vector.tensor_copy(token[u][:], token_of[:, bass.ds(j + G, 1)]).then_inc(token_ready, 1)

                    def body(j, i, u, first, last):
                        norm(j, i, u, first)
                        if not (first and u < 2):
                            finish(j - 2, (u - 2) % G)
                        if u >= LAG and not last:
                            next_token(j - LAG, i, u - LAG)
                        elif u < LAG and not first:
                            next_token(j - LAG, i - 1, u - LAG + G)

                    rounds(dve, body)
                    finish(SLOT_TILES - 2, G - 2)
                    finish(SLOT_TILES - 1, G - 1)

                @block.tensor
                def _(pe):
                    pe.wait_ge(ld_we, 16 * EXPERTS)

                    def turn(j, i, u, first):
                        pe.wait_ge(xn_ready, j + 1)
                        if not first or u >= 2:
                            pe.wait_ge(xT_ready, j - 1)
                        for k in range(KB):
                            last = nc.tensor.transpose(turn_ps[:, u % 2, k * P:(k + 1) * P], xn[:, u % 2, k * P:(k + 1) * P], ident[:])
                        last.then_inc(turned, 1)

                    def product(j, par):
                        expert = pe.value_load(tile_expert[0:1, bass.ds(j, 1)], min_val=0, max_val=EXPERTS - 1)
                        pe.wait_ge(xT_ready, j + 1)
                        if not (isinstance(j, int) and j < 2):
                            pe.wait_ge(y_used, j - 1)
                        for k in range(KB):
                            last = nc.tensor.matmul(y_ps[:, par, :], xT[:, par, k, :], we[:, expert, k, :], start=(k == 0), stop=(k == KB - 1))
                        last.then_inc(y_full, 1)

                    def body(j, i, u, first, last):
                        turn(j, i, u, first)
                        if not (first and u == 0):
                            product(j - 1, (u - 1) % 2)

                    rounds(pe, body)
                    product(SLOT_TILES - 1, (SLOT_TILES - 1) % 2)


def build_program(nc, io):
    with ExitStack() as whole:
        xres = whole.enter_context(nc.sbuf_tensor("xres", [P, TILES, ROW], F32))
        ident = whole.enter_context(nc.sbuf_tensor("ident", [P, P], F32))
        with ExitStack() as first_two:
            seen = Seen(nc, first_two)
            rope_attention_stage(nc, io, xres, ident, seen)
            quantised_ffn_stage(nc, io, xres, ident, seen)
        masked_attention_stage(nc, io, xres, ident)
        expert_stage(nc, io, xres, ident)


def shape_constants():
    import numpy as np

    freq = np.float32(1) / (10000.0 ** (np.arange(0, DH0, 2) / DH0)).astype(np.float32)
    angle = np.arange(S, dtype=np.float32)[:, None] * freq[None, :]
    cos = np.repeat(np.cos(angle), 2, axis=1).T
    sin = np.repeat(np.sin(angle), 2, axis=1).T * np.tile(np.array([-1, 1], np.float32), DH0 // 2)[:, None]
    rot = np.stack([np.tile(cos, (2, 1)), np.tile(sin, (2, 1))], axis=1)
    at = np.arange(P)
    causal = np.ones((P, 2, KEYS), np.float32)
    causal[:, 0, :] = at[:, None] <= at[None, :]
    return {
        "ident": np.eye(P, dtype=np.float32),
        "rot": np.ascontiguousarray(rot, np.float32),
        "causal": causal,
        "upper": (at[:, None] < at[None, :]).astype(np.float32),
        "token_id": (P * np.arange(TPC, dtype=np.float32)[None, :] + at[:, None].astype(np.float32)),
        "numbers": np.broadcast_to(np.arange(EXPERTS, dtype=np.float32), (P, TPC, EXPERTS)),
        "map_base": (at[:, None, None] == 0) * np.broadcast_to(TOK * np.arange(EXPERTS, dtype=np.float32), (P, TPC, EXPERTS)).astype(np.float32),
        "slot_at": (P * np.arange(SLOT_TILES, dtype=np.float32))[:, None],
        "nobody": np.full((P, MAP_ROWS), TOK, np.float32),
    }


def kernel(x, ctx_1024, mask_BxS2_bf0, mask_1x1xSxS2_bk0, L0_xattn_Wq, L0_xattn_Wk, L0_xattn_Wv, L0_xattn_Wo, L0_xattn_ln_g,
           L0_xattn_ln_b, L0_ffn_clip_x, L0_ffn_clip_down, L0_ffn_w_gate, L0_ffn_w_up, L0_ffn_w_down, L1_xattn_Wq, L1_xattn_bq,
           L1_xattn_Wk, L1_xattn_bk, L1_xattn_Wv, L1_xattn_bv, L1_xattn_Wo, L1_xattn_bo, L1_ffn_Wg, L1_ffn_bg, L1_ffn_We,
           L1_ffn_be):
    import numpy as np
    import concourse.bacc as bacc
    from concourse.bass_utils import run_bass_kernel_spmd

    def columns(v):
        return np.asarray(v).reshape(KB, P).T

    def row(v):
        return np.asarray(v).reshape(1, -1)

    laid_out = {
        "x": np.asarray(x).reshape(TOK, D),
        "ctx": np.asarray(ctx_1024).reshape(B * KEYS, D),
        "pad": np.asarray(mask_BxS2_bf0).T,
        "mask": np.asarray(mask_1x1xSxS2_bk0).reshape(S, KEYS),
        "ln_g": columns(L0_xattn_ln_g), "ln_b": columns(L0_xattn_ln_b),
        "wq0": L0_xattn_Wq, "wk0": L0_xattn_Wk, "wv0": L0_xattn_Wv, "wo0": L0_xattn_Wo,
        "clip": np.concatenate([row(L0_ffn_clip_x), row(L0_ffn_clip_down)], axis=1),
        "w_gate": L0_ffn_w_gate, "w_up": L0_ffn_w_up, "w_down": L0_ffn_w_down,
        "wq1": np.asarray(L1_xattn_Wq).T, "wk1": np.asarray(L1_xattn_Wk).T,
        "wv1": np.asarray(L1_xattn_Wv).T, "wo1": np.asarray(L1_xattn_Wo).T,
        "qk_bias": np.stack([columns(L1_xattn_bq), columns(L1_xattn_bk)], axis=1),
        "bv": row(L1_xattn_bv), "bo": row(L1_xattn_bo),
        "wg": L1_ffn_Wg, "bg": row(L1_ffn_bg), "we": L1_ffn_We, "be": row(L1_ffn_be),
        **shape_constants(),
    }
    nc = bacc.Bacc("TRN2", target_bir_lowering=False, num_devices=1)
    arrays, io = {}, {}
    for name, value in laid_out.items():
        a = np.ascontiguousarray(value)
        arrays[f"in_{name}"] = a
        io[name] = nc.dram_tensor(f"in_{name}", a.shape, mybir.dt.from_np(a.dtype), kind="ExternalInput").ap()
    io["hidden"] = nc.dram_tensor("hidden", [CHUNKS, P, IT * CHUNK], F32).ap()
    io["rows"] = nc.dram_tensor("rows", [TOK, ROW], F32).ap()
    io["owner"] = nc.dram_tensor("owner", [MAP, 1], F32).ap()
    io["out"] = nc.dram_tensor("out", [TOK, D], F32, kind="ExternalOutput").ap()
    build_program(nc, io)
    got = run_bass_kernel_spmd(nc, [arrays], core_ids=[0])
    return got.results[0]["out"].reshape(B, S, D)
```

```python
import concourse.bass as bass
from concourse import mybir
from contextlib import ExitStack

F32 = mybir.dt.float32
F32R = mybir.dt.float32r
BF16 = mybir.dt.bfloat16
I32 = mybir.dt.int32
U32 = mybir.dt.uint32
U8 = mybir.dt.uint8
ALU = mybir.AluOpType
ACT = mybir.ActivationFunctionType
AX = mybir.AxisListType

P = 128
B, S, D = 2, 2048, 512
KEYS = 128
TOK = B * S
TILES = TOK // P
CHUNK = 512
TPC = CHUNK // P
CHUNKS = TOK // CHUNK
KB = D // P
LN_EPS = 1e-5
ROW = D + 4
COL_P, COL_MEAN, COL_RSTD, COL_SHIFT = D, D + 1, D + 2, D + 3

H0, DH0 = 16, 64
HD0 = H0 * DH0
GROK = 30.0
ROPE_CHUNK = 256
ROPE_TILES = ROPE_CHUNK // P
ROPE_CHUNKS = TOK // ROPE_CHUNK
ROPE_CPB = ROPE_CHUNKS // B
UNITS = H0 // 4
BLOCKS = HD0 // P
INNER = 1408


def next_offset(nc):
    return -(-nc.sbuf_base // 32) * 32


class Chain:

    def __init__(self, eng, sem, base=0):
        self.eng, self.sem, self.base, self.k = eng, sem, base, 0

    def step(self, ins):
        ins.then_inc(self.sem, 1)
        self.k += 1

    def wait(self):
        self.eng.wait_ge(self.sem, self.base + self.k)


class Ring:

    def __init__(self, prefix, body):
        self.prefix, self.body = prefix, body
        assert len(prefix) % 2 == 0 and len(body) % 2 == 0 and prefix[-2:] == body[-2:]

    def full(self, n, pos):
        return len(self.prefix) + len(self.body) * n + pos + 1

    def emptied(self, n, seq, pos):
        who = seq[pos]
        return who, self.prefix.count(who) + self.body.count(who) * n + seq[:pos + 1].count(who)

    def reuse(self, n, seq, pos):
        if pos >= 2:
            return self.emptied(n, seq, pos - 2)
        last = self.prefix[-2:]
        who = last[pos]
        return who, self.prefix.count(who) + self.body.count(who) * n - last[pos + 1:].count(who)

    def prefix_full(self, pos):
        return pos + 1

    def prefix_emptied(self, pos):
        who = self.prefix[pos]
        return who, self.prefix[:pos + 1].count(who)


class Seen:

    def __init__(self, nc, stage):
        self.stats = stage.enter_context(nc.sbuf_tensor("seen_stats", [P, TILES, 6], F32))
        self.top = stage.enter_context(nc.sbuf_tensor("seen_top", [P, TILES], F32))
        self.low = stage.enter_context(nc.sbuf_tensor("seen_low", [P, TILES], F32))


class Ahead:

    def __init__(self, nc, whole):
        self.gate = nc.alloc_sbuf_tensor_at("gate_ahead", [P, INNER // P, D], F32, offset=next_offset(nc))
        self.ld_gate = whole.enter_context(nc.semaphore("ld_gate_ahead"))


def rope_attention_stage(nc, io, xres, ident, seen, ahead):
    SWAP = [i ^ 1 for i in range(32)]
    VW = DH0 + 1
    NT, NC, CPBA = ROPE_TILES, ROPE_CHUNKS, ROPE_CPB
    with ExitStack() as stage:
        def sb(name, shape, dt=F32):
            return stage.enter_context(nc.sbuf_tensor("a_" + name, shape, dt))

        def pb(name, shape, dt=F32):
            return stage.enter_context(nc.psum_tensor("a_" + name, shape, dt))

        def sem(name):
            return stage.enter_context(nc.semaphore("a_" + name))

        wq_hi, wq_lo = (sb("wq_" + x, [P, KB, HD0], F32R) for x in ("hi", "lo"))
        keysT = sb("keysT", [P, BLOCKS, B * KEYS])
        vals = sb("vals", [P, B, H0, VW])
        gain = sb("gain", [P, KB])
        shift = sb("shift", [P, KB])
        pad_u8 = sb("pad_u8", [P, B], U8)
        pad_bias = sb("pad_bias", [P, B])
        causal = sb("causal", [P, 2, KEYS])
        rot = sb("rot", [P, 2, ROPE_CHUNK])
        wo_hi, wo_lo = (sb("wo_" + x, [P, BLOCKS, D], F32R) for x in ("hi", "lo"))
        q_bias, q_bias_swapped = sb("q_bias", [P, BLOCKS]), sb("q_bias_swapped", [P, BLOCKS])
        stats = sb("stats", [P, NT, 6])
        mv = sb("mv", [P, NT, 2])
        var = sb("var", [P, NT])
        rstd = sb("rstd", [P, NT])
        minus_half = sb("minus_half", [P, NT])
        swapped = sb("swapped", [P, 2, ROPE_CHUNK])
        recip = sb("recip", [P, NT, 4])
        held = sb("held", [P, 1])

        score_ps = pb("score_ps", [P, 2, 4, ROPE_CHUNK])
        bank = [pb(f"bank{i}", [P, 2, ROPE_CHUNK]) for i in range(2)]
        pv_ps = [pb(f"pv_ps{i}", [P, D]) for i in range(NT)]

        ld_small, ld_ctx, ld_wk, ld_wv = sem("ld_small"), sem("ld_ctx"), sem("ld_wk"), sem("ld_wv")
        ld_wq, ld_wo, ld_x = sem("ld_wq"), sem("ld_wo"), sem("ld_x")
        ld_rot, rot_used = sem("ld_rot"), sem("rot_used")
        bank_full = sem("bank_full")
        freed = {"dve": sem("freed_by_dve"), "act": sem("freed_by_act")}
        var_ready, rstd_ready, xn_ready = sem("var_ready"), sem("rstd_ready"), sem("xn_ready")
        half_ready = sem("half_ready")
        weight_hi, weight_lo, bias_full = sem("weight_hi"), sem("weight_lo"), sem("bias_full")
        hi_ready, lo_ready = sem("hi_ready"), sem("lo_ready")
        q_ready, score_full, capped, exped = sem("q_ready"), sem("score_full"), sem("capped"), sem("exped")
        masked, pv_full, normed = sem("masked"), sem("pv_full"), sem("normed")
        dve_step = sem("dve_step")

        PRE = ["act"] * KB + ["dve"] * BLOCKS + ["act"] * (2 * B) + ["act"] * 2 + ["dve"] * 2
        BODY = ["dve"] * 2 + ["act"] * 4 + ["dve", "act"] * 2 + ["dve"] * 2
        LAST = ["dve"] * 2 + ["act"] * 4 + ["dve"] * 2
        AT_Q2, AT_Q3, AT_X = 0, 1, 2
        ring = Ring(PRE, BODY)
        PREP_STEPS = 1 + 2 * B + 1 + 3 * BLOCKS + 2 + 2 * NT
        VAR0 = 1
        PRE_K, PRE_V = KB, KB + BLOCKS
        PRE_T0, PRE_Q0 = PRE_V + 2 * B, PRE_V + 2 * B + 2

        def places(last):
            if last:
                return {"attn": [2, 3, 4, 5], "out": [6, 7]}
            return {"attn": [4, 5, 7, 9], "next": [6, 8], "out": [10, 11]}

        def splits(n, last):
            return 2 + 6 * n, 2 + 6 * n + (0 if last else 2)

        def chunks(eng, body):
            with eng.Fori(0, CPBA - 1) as c:
                body(c, c, 0, False)
            body(CPBA - 1, CPBA - 1, 0, False)
            with eng.Fori(0, CPBA - 1) as c:
                body(c + CPBA, c, 1, False)
            body(NC - 1, CPBA - 1, 1, True)

        def norm_stats(dve, ch, n, before):
            dve.wait_ge(xn_ready, before)
            for t in range(NT):
                ch.step(nc.vector.bn_stats(stats[:, t, :], xres[:, n * NT + t, 0:D]))
            ch.wait()
            nc.vector.memset(held[:], 0.0)
            for t in range(NT):
                ch.step(nc.vector.bn_aggr(mv[:, t, :], stats[:, t, :]))
            ch.wait()
            nc.vector.tensor_scalar(var[:], mv[:, :, 1], 1.0 + LN_EPS, LN_EPS * LN_EPS,
                                    ALU.mult, ALU.add).then_inc(var_ready, 1)

        def deviation(pool, n):
            pool.wait_ge(var_ready, VAR0 + 1 + n)
            nc.gpsimd.tensor_tensor(rstd[:], var[:], minus_half[:], ALU.pow).then_inc(rstd_ready, 1)

        with ExitStack() as early:
            def esb(name, shape):
                return early.enter_context(nc.sbuf_tensor("a_" + name, shape, F32))

            wk_or_wo = esb("wk_or_wo", [P, KB * HD0])
            wk, wo = wk_or_wo[:].rearrange("p (k n) -> p k n", k=KB), wk_or_wo[:].rearrange("p (k n) -> p k n", k=BLOCKS)
            wv, wq = esb("wv", [P, KB, HD0]), esb("wq", [P, KB, HD0])
            ctx_t, ctxT = esb("ctx", [P, B, D]), esb("ctxT", [P, KB, B * KEYS])
            turned = ctx_t[:, 0, 0:B * KEYS]

            with nc.Block() as block:
                @block.sync
                def _(sp):
                    sp.dma_start(ctx_t[:], io["ctx"].rearrange("(b p) f -> p b f", p=P)).then_inc(ld_ctx, 16)
                    sp.dma_start(ident[:], io["ident"]).then_inc(ld_small, 16)
                    sp.dma_start(gain[:], io["ln_g"]).then_inc(ld_small, 16)
                    sp.dma_start(shift[:], io["ln_b"]).then_inc(ld_small, 16)
                    sp.dma_start(pad_u8[:], io["pad"]).then_inc(ld_small, 16)
                    sp.dma_start(causal[:], io["causal"]).then_inc(ld_small, 16)
                    sp.dma_start(rot[:], io["rot"][:, :, 0:ROPE_CHUNK]).then_inc(ld_small, 16)
                    sp.dma_start(wk, io["wk0"].rearrange("(k p) n -> p k n", p=P)).then_inc(ld_wk, 16)
                    sp.dma_start(wq[:], io["wq0"].rearrange("(k p) n -> p k n", p=P)).then_inc(ld_wq, 16)
                    sp.dma_start(wv[:], io["wv0"].rearrange("(k p) n -> p k n", p=P)).then_inc(ld_wv, 16)

                    def load_x(c, loaded):
                        sp.dma_start(xres[:, c * TPC:(c + 1) * TPC, 0:D],
                                     io["x"][c * CHUNK:(c + 1) * CHUNK, :].rearrange("(t p) f -> p t f", p=P)).then_inc(loaded, 16)

                    for c in range(CHUNKS // 2, CHUNKS):
                        load_x(c, ld_x)
                    sp.wait_ge(bank_full, ring.prefix_full(PRE_V - 1))
                    sp.dma_start(wo, io["wo0"].rearrange("(k p) n -> p k n", p=P)).then_inc(ld_wo, 16)
                    load_x(0, ld_ctx)
                    for c in range(1, CHUNKS // 2):
                        load_x(c, ld_x)

                @block.gpsimd
                def _(pool):
                    nc.gpsimd.memset(minus_half[:], -0.5).then_inc(half_ready, 1)
                    pool.wait_ge(half_ready, 1)
                    pool.wait_ge(var_ready, 1)
                    nc.gpsimd.tensor_tensor(rstd[:, 0:B], var[:, 0:B], minus_half[:, 0:B], ALU.pow).then_inc(rstd_ready, 1)
                    deviation(pool, 0)

                @block.scalar
                def _(act):
                    act.wait_ge(ld_small, 96)
                    for k in range(KB):
                        act.wait_ge(bank_full, ring.prefix_full(k))
                        nc.scalar.activation(ctxT[:, k, :], bank[k % 2][:, 0, :], ACT.Identity,
                                             bias=shift[:, k:k + 1], scale=gain[:, k:k + 1]).then_inc(freed["act"], 1)
                    act.wait_ge(ld_wq, 16)
                    for k in range(KB):
                        nc.scalar.activation(wq_hi[:, k, :], wq[:, k, :], ACT.Copy, scale=gain[:, k:k + 1]).then_inc(weight_hi, 1)
                    for u in range(2 * B):
                        if u == B:
                            act.wait_ge(ld_wo, 16)
                            nc.scalar.copy(wo_hi[:], wo).then_inc(weight_hi, 1)
                        b, half = u // 2, u % 2
                        act.wait_ge(bank_full, ring.prefix_full(PRE_V + u))
                        nc.scalar.copy(vals[:, b, half * 8:(half + 1) * 8, 0:DH0],
                                       bank[(PRE_V + u) % 2][:].rearrange("p a c -> p (a c)").rearrange("p (h d) -> p h d", d=DH0)
                                       ).then_inc(freed["act"], 1)

                @block.vector
                def _(dve):
                    ch = Chain(dve, dve_step)
                    ch.step(nc.vector.memset(vals[:, :, :, DH0:VW], 1.0))
                    dve.wait_ge(ld_ctx, 16)
                    for b in range(B):
                        ch.step(nc.vector.bn_stats(stats[:, b, :], ctx_t[:, b, :]))
                    ch.wait()
                    for b in range(B):
                        ch.step(nc.vector.bn_aggr(mv[:, b, :], stats[:, b, :]))
                    ch.wait()
                    nc.vector.tensor_scalar(var[:, 0:B], mv[:, 0:B, 1], LN_EPS, None, ALU.add).then_inc(var_ready, 1)
                    dve.wait_ge(rstd_ready, 1)
                    for b in range(B):
                        last = nc.vector.tensor_scalar(ctx_t[:, b, :], ctx_t[:, b, :], mv[:, b, 0:1],
                                                       rstd[:, b:b + 1], ALU.subtract, ALU.mult)
                    last.then_inc(xn_ready, 1)
                    dve.wait_ge(ld_small, 96)
                    ch.step(nc.vector.tensor_scalar(pad_bias[:], pad_u8[:], -1e30, None, ALU.mult))
                    cos_k = rot[:, 0, 0:KEYS].unsqueeze(1).to_broadcast([P, B, KEYS])
                    sin_k = rot[:, 1, 0:KEYS].unsqueeze(1).to_broadcast([P, B, KEYS])
                    by_batch = lambda x: x.rearrange("p (b k) -> p b k", b=B)
                    for m in range(BLOCKS):
                        dve.wait_ge(bank_full, ring.prefix_full(PRE_K + m))
                        src = bank[(PRE_K + m) % 2][:, 0, :]
                        sw = swapped[:, 0, :]
                        ch.wait()
                        ch.step(nc.vector.stream_shuffle(sw, src, SWAP))
                        nc.vector.tensor_tensor(by_batch(turned), by_batch(src), cos_k, ALU.mult).then_inc(freed["dve"], 1)
                        ch.wait()
                        ch.step(nc.vector.tensor_tensor(by_batch(sw), by_batch(sw), sin_k, ALU.mult))
                        ch.wait()
                        ch.step(nc.vector.tensor_tensor(keysT[:, m, :], turned, sw, ALU.add))
                    dve.wait_ge(bias_full, 1)
                    ch.step(nc.vector.tensor_copy(q_bias[:], score_ps[:, 0, 0, 0:BLOCKS]))
                    ch.wait()
                    ch.step(nc.vector.stream_shuffle(q_bias_swapped[:], q_bias[:], SWAP))
                    for k in range(KB):
                        dve.wait_ge(weight_hi, k + 1)
                        nc.vector.scalar_tensor_tensor(wq_lo[:, k, :], wq[:, k, :], gain[:, k:k + 1], wq_hi[:, k, :],
                                                       ALU.mult, ALU.subtract).then_inc(weight_lo, 1)
                    dve.wait_ge(ld_ctx, 32)
                    norm_stats(dve, ch, 0, 1)
                    dve.wait_ge(weight_hi, KB + 1)
                    nc.vector.tensor_tensor(wo_lo[:], wo, wo_hi[:], ALU.subtract).then_inc(weight_lo, 1)
                    assert ch.k == PREP_STEPS, ch.k

                @block.tensor
                def _(pe):
                    pe.wait_ge(ld_small, 96)
                    pe.wait_ge(xn_ready, 1)

                    def begin(u):
                        if u >= 2:
                            who, count = ring.prefix_emptied(u - 2)
                            pe.wait_ge(freed[who], count)
                        return bank[u % 2]

                    for k in range(KB):
                        out = begin(k)
                        for b in range(B):
                            last = nc.tensor.transpose(out[:, 0, b * KEYS:(b + 1) * KEYS], ctx_t[:, b, k * P:(k + 1) * P], ident[:])
                        last.then_inc(bank_full, 1)
                    pe.wait_ge(freed["act"], KB)
                    pe.wait_ge(ld_wk, 16)
                    for m in range(BLOCKS):
                        out = begin(PRE_K + m)
                        for k in range(KB):
                            last = nc.tensor.matmul(out[:, 0, :], wk[:, k, m * P:(m + 1) * P], ctxT[:, k, :],
                                                    start=(k == 0), stop=(k == KB - 1))
                        last.then_inc(bank_full, 1)
                    pe.wait_ge(ld_wq, 16)
                    for m in range(BLOCKS):
                        for k in range(KB):
                            last = nc.tensor.matmul(score_ps[:, 0, 0, m:m + 1], wq[:, k, m * P:(m + 1) * P], shift[:, k:k + 1],
                                                    start=(k == 0), stop=(k == KB - 1))
                    last.then_inc(bias_full, 1)
                    pe.wait_ge(ld_wv, 16)
                    for u in range(2 * B):
                        b, half = u // 2, u % 2
                        out = begin(PRE_V + u)
                        for k in range(KB):
                            last = nc.tensor.matmul(out[:].rearrange("p a c -> p (a c)"), ctxT[:, k, b * KEYS:(b + 1) * KEYS],
                                                    wv[:, k, half * D:(half + 1) * D], start=(k == 0), stop=(k == KB - 1))
                        last.then_inc(bank_full, 1)

        xn = sb("xn", [P, NT, D])
        x_hi, x_lo = (sb("x_" + x, [P, KB, ROPE_CHUNK], F32R) for x in ("hi_parts", "lo_parts"))
        probs = sb("probs", [P, 2, 4, ROPE_CHUNK])
        q = sb("q", [P, BLOCKS, ROPE_CHUNK])
        attn = sb("attn", [P, NT, HD0])
        attn_hi, attn_lo = (sb("attn_" + x, [P, BLOCKS, ROPE_CHUNK], F32R) for x in ("hi_parts", "lo_parts"))
        full = sb("full", [P, 2, 2, ROPE_CHUNK])
        DVE_STEPS = 2 * NT + 4 - 1 + UNITS * NT + 3 * NT
        with nc.Block() as block:
            @block.sync
            def _(sp):
                def load_rot(n, c):
                    sp.wait_ge(rot_used, n)
                    sp.dma_start(rot[:], io["rot"][:, :, bass.ds(c * ROPE_CHUNK, ROPE_CHUNK)]).then_inc(ld_rot, 16)
                with sp.Fori(1, CPBA) as c:
                    load_rot(c, c)
                with sp.Fori(0, CPBA) as c:
                    load_rot(c + CPBA, c)
                sp.wait_ge(bank_full, ring.full(NC - 1, AT_Q3))
                sp.dma_start(ahead.gate[:], io["w_gate"].rearrange("(i p) f -> p i f", p=P)).then_inc(ahead.ld_gate, 16)

            @block.gpsimd
            def _(pool):
                def low_parts(i, j, lo, hi, pair):
                    pool.wait_ge(hi_ready, i + 1)
                    at = slice(2 * pair, 2 * pair + 2)
                    nc.gpsimd.tensor_tensor(lo[:, at, :], full[:, j], hi[:, at, :], ALU.subtract).then_inc(lo_ready, 1)

                for k in range(2):
                    low_parts(k, k, x_lo, x_hi, k)

                def body(n, c, b, last):
                    x_at, attn_at = splits(n, last)
                    if not last:
                        deviation(pool, n + 1)
                        for k in range(2):
                            low_parts(x_at + k, k, x_lo, x_hi, k)
                    for g in range(UNITS):
                        low_parts(attn_at + g, g % 2, attn_lo, attn_hi, g)

                chunks(pool, body)

            @block.scalar
            def _(act):
                def split(i, j, filled, emptied, pos, hi, pair):
                    if not isinstance(i, int) or i >= 2:
                        act.wait_ge(lo_ready, i - 1)
                    act.wait_ge(bank_full, filled)
                    nc.scalar.copy(full[:, j], bank[pos % 2][:]).then_inc(freed["act"], 1)
                    act.wait_ge(freed["act"], emptied)
                    nc.scalar.copy(hi[:, 2 * pair:2 * pair + 2, :], full[:, j]).then_inc(hi_ready, 1)

                for k in range(2):
                    pos = PRE_T0 + k
                    split(k, k, ring.prefix_full(pos), ring.prefix_emptied(pos)[1], pos, x_hi, k)

                def body(n, c, b, last):
                    seq, at = LAST if last else BODY, places(last)["attn"]
                    x_at, attn_at = splits(n, last)

                    def split_attn(g):
                        split(attn_at + g, g % 2, ring.full(n, at[g]), ring.emptied(n, seq, at[g])[1], at[g], attn_hi, g)

                    for p in range(UNITS):
                        unit = n * UNITS + p
                        buf = probs[:, p % 2]
                        act.wait_ge(score_full, unit + 1)
                        if p >= 2:
                            act.wait_ge(pv_full, NT * (unit - 1))
                        nc.scalar.activation(buf, score_ps[:, p % 2], ACT.Tanh, scale=1.0 / (DH0 ** 0.5 * GROK)).then_inc(capped, 1)
                        act.wait_ge(capped, unit + 1)
                        nc.scalar.activation(buf, buf, ACT.Exp, bias=pad_bias[:, b:b + 1], scale=GROK).then_inc(exped, 1)
                        if p == 2 and not last:
                            for k in range(2):
                                pos = AT_X + k
                                split(x_at + k, k, ring.full(n, pos), ring.emptied(n, seq, pos)[1], pos, x_hi, k)
                        if p >= 2:
                            split_attn(p - 2)
                    for g in range(2, UNITS):
                        split_attn(g)

                chunks(act, body)

            @block.vector
            def _(dve):
                ch = Chain(dve, dve_step)
                ch.base = PREP_STEPS

                def norm_rows(n):
                    dve.wait_ge(rstd_ready, VAR0 + 1 + n)
                    for t in range(NT):
                        nc.vector.tensor_scalar(xn[:, t, :], xres[:, n * NT + t, 0:D], mv[:, t, 0:1], rstd[:, t:t + 1],
                                                ALU.subtract, ALU.mult).then_inc(xn_ready, 1)

                def rotate(n, g, full, emptied, pos, before):
                    src = bank[pos % 2]
                    dve.wait_ge(bank_full, full)
                    if before is not None:
                        dve.wait_ge(q_ready, before)
                    blocks = range(2 * g, 2 * g + 2)
                    for i, m in enumerate(blocks):
                        nc.vector.scalar_tensor_tensor(q[:, m, :], src[:, i, :], q_bias[:, m:m + 1], rot[:, 0, :], ALU.add, ALU.mult)
                    nc.vector.stream_shuffle(swapped[:], src[:], SWAP).then_inc(freed["dve"], 1)
                    dve.wait_ge(freed["dve"], emptied)
                    for i, m in enumerate(blocks):
                        turned = nc.vector.scalar_tensor_tensor(swapped[:, i, :], swapped[:, i, :], q_bias_swapped[:, m:m + 1],
                                                                rot[:, 1, :], ALU.add, ALU.mult)
                    if g == UNITS - 1:
                        turned.then_inc(rot_used, 1)
                        dve.wait_ge(rot_used, n + 1)
                    else:
                        ch.step(turned)
                        ch.wait()
                    unit = q[:, 2 * g:2 * g + 2, :]
                    nc.vector.tensor_tensor(unit, unit, swapped[:], ALU.add).then_inc(q_ready, 1)

                def mask(n, c, p):
                    dve.wait_ge(exped, n * UNITS + p + 1)
                    first = probs[:, p % 2, :, 0:P]
                    kind = (c + CPBA - 1) // CPBA
                    nc.vector.tensor_tensor(first, first, causal[:, bass.ds(kind, 1), :].to_broadcast([P, 4, KEYS]),
                                            ALU.mult).then_inc(masked, 1)

                def normalise(n, p):
                    for t in range(NT):
                        got = pv_ps[t][:, 0:4 * VW].rearrange("p (h d) -> p h d", d=VW)
                        dve.wait_ge(pv_full, NT * (n * UNITS + p) + t + 1)
                        ch.step(nc.vector.reciprocal(recip[:, t, :], got[:, :, DH0]))
                        ch.wait()
                        out = attn[:, t, p * 4 * DH0:(p + 1) * 4 * DH0].rearrange("p (h d) -> p h d", d=DH0)
                        nc.vector.tensor_tensor(out, got[:, :, 0:DH0], recip[:, t, :].unsqueeze(2).to_broadcast([P, 4, DH0]),
                                                ALU.mult).then_inc(normed, 1)

                norm_rows(0)
                dve.wait_ge(ld_x, 16 * (CHUNKS - 1))
                for g in range(2):
                    rotate(0, g, ring.prefix_full(PRE_Q0 + g), ring.prefix_emptied(PRE_Q0 + g)[1], PRE_Q0 + g, g or None)
                start = ch.base + ch.k

                def body(n, c, b, last):
                    seq, at = LAST if last else BODY, places(last)
                    ch.base, ch.k = start + n * DVE_STEPS, 0

                    def queries(m, g, pos):
                        rotate(m, g, ring.full(n, pos), ring.emptied(n, seq, pos)[1], pos, m * UNITS + g)

                    for p in range(UNITS):
                        mask(n, c, p)
                        if p >= 1:
                            normalise(n, p - 1)
                        if p == 0 and not last:
                            norm_stats(dve, ch, n + 1, 1 + NT * (n + 1))
                        if p == 1 and not last:
                            norm_rows(n + 1)
                        if p < 2:
                            queries(n, p + 2, (AT_Q2, AT_Q3)[p])
                        if p == 3 and not last:
                            dve.wait_ge(ld_rot, 16 * (n + 1))
                            queries(n + 1, 0, at["next"][0])
                    normalise(n, UNITS - 1)
                    if not last:
                        queries(n + 1, 1, at["next"][1])
                    for t in range(NT):
                        pos = at["out"][t]
                        dve.wait_ge(bank_full, ring.full(n, pos))
                        tile = n * NT + t
                        row = xres[:, tile, 0:D]
                        nc.vector.tensor_tensor(row, bank[pos % 2][:].rearrange("p a c -> p (a c)"), row, ALU.add).then_inc(freed["dve"], 1)
                        dve.wait_ge(freed["dve"], ring.emptied(n, seq, pos)[1])
                        ch.step(nc.vector.bn_stats(seen.stats[:, tile, :], row))
                        ch.step(nc.vector.tensor_reduce(seen.top[:, bass.ds(tile, 1)], row, AX.X, ALU.max))
                        ch.step(nc.vector.tensor_reduce(seen.low[:, bass.ds(tile, 1)], row, AX.X, ALU.min))
                    if not last:
                        assert ch.k == DVE_STEPS, (ch.k, DVE_STEPS)

                chunks(dve, body)

            @block.tensor
            def _(pe):
                def begin_prefix(u):
                    who, count = ring.prefix_emptied(u - 2)
                    pe.wait_ge(freed[who], count)
                    return bank[u % 2]

                def begin(n, seq, pos):
                    who, count = ring.reuse(n, seq, pos)
                    pe.wait_ge(freed[who], count)
                    return bank[pos % 2]

                def parts(out, hi, lo, w_hi, w_lo, first, last):
                    nc.tensor.matmul(out, hi, w_hi, start=first, stop=False)
                    nc.tensor.matmul(out, hi, w_lo, start=False, stop=False)
                    return nc.tensor.matmul(out, lo, w_hi, start=False, stop=last)

                def turn(out, rows, first_block):
                    for i in range(2):
                        at = slice((first_block + i) * P, (first_block + i + 1) * P)
                        for t in range(NT):
                            last = nc.tensor.transpose(out[:, i, t * P:(t + 1) * P], rows[:, t, at], ident[:])
                    last.then_inc(bank_full, 1)

                def project(out, g):
                    products = [(w, x, k) for k in range(KB) for w, x in ((wq_hi, x_hi), (wq_hi, x_lo), (wq_lo, x_hi))]
                    for j, (w, x, k) in enumerate(products):
                        for i in range(2):
                            cols = slice((2 * g + i) * P, (2 * g + i + 1) * P)
                            last = nc.tensor.matmul(out[:, i, :], w[:, k, cols], x[:, k, :], start=(j == 0 and i == 0), stop=(j == len(products) - 1 and i == 1))
                    last.then_inc(bank_full, 1)

                def place(h):
                    return h % 2 * 2 + h // 2

                def scores(n, b, p):
                    unit = n * UNITS + p
                    pe.wait_ge(q_ready, unit + 1)
                    if p >= 2:
                        pe.wait_ge(capped, unit - 1)
                    for h in range(4):
                        rows, m = slice(h % 2 * DH0, (h % 2 + 1) * DH0), 2 * p + h // 2
                        last = nc.tensor.matmul(score_ps[:, p % 2, place(h), :], keysT[rows, m, b * KEYS:(b + 1) * KEYS], q[rows, m, :],
                                                start=True, stop=True)
                    last.then_inc(score_full, 1)

                def weigh(n, b, p):
                    unit = n * UNITS + p
                    pe.wait_ge(masked, unit + 1)
                    for t in range(NT):
                        if p >= 1:
                            pe.wait_ge(normed, NT * (unit - 1) + t + 1)
                        for h in range(4):
                            last = nc.tensor.matmul(pv_ps[t][:, h * VW:(h + 1) * VW], probs[:, p % 2, place(h), t * P:(t + 1) * P],
                                                    vals[:, b, 4 * p + h, :], start=True, stop=True)
                        last.then_inc(pv_full, 1)

                pe.wait_ge(xn_ready, 1 + NT)
                for k in range(2):
                    turn(begin_prefix(PRE_T0 + k), xn, 2 * k)
                pe.wait_ge(weight_lo, KB + 1)
                pe.wait_ge(lo_ready, 2)
                for g in range(2):
                    project(begin_prefix(PRE_Q0 + g), g)
                scores(0, 0, 0)

                def body(n, c, b, last):
                    seq, at = LAST if last else BODY, places(last)

                    def turn_attn(g):
                        pe.wait_ge(normed, NT * (n * UNITS + g + 1))
                        turn(begin(n, seq, at["attn"][g]), attn, 2 * g)

                    for p in range(UNITS):
                        if p >= 1:
                            scores(n, b, p)
                            weigh(n, b, p - 1)
                        if p < 2:
                            pos = (AT_Q2, AT_Q3)[p]
                            project(begin(n, seq, pos), p + 2)
                        if p == 2 and not last:
                            pe.wait_ge(xn_ready, 1 + NT * (n + 2))
                            for k in range(2):
                                turn(begin(n, seq, AT_X + k), xn, 2 * k)
                        if p >= 2:
                            turn_attn(p - 2)
                        if p == 3 and not last:
                            pe.wait_ge(lo_ready, splits(n, last)[0] + 2)
                            project(begin(n, seq, at["next"][0]), 0)
                    weigh(n, b, UNITS - 1)
                    turn_attn(2)
                    if not last:
                        project(begin(n, seq, at["next"][1]), 1)
                    turn_attn(3)
                    if not last:
                        scores(n + 1, (n + 1) // CPBA if isinstance(n, int) else b, 0)
                    for t in range(NT):
                        out = begin(n, seq, at["out"][t])
                        for k in range(BLOCKS):
                            if t == 0 and k % 2 == 0:
                                pe.wait_ge(lo_ready, splits(n, last)[1] + k // 2 + 1)
                            tokens = slice(t * P, (t + 1) * P)
                            ins = parts(out[:].rearrange("p a c -> p (a c)"), attn_hi[:, k, tokens], attn_lo[:, k, tokens],
                                        wo_hi[:, k, :], wo_lo[:, k, :], k == 0, k == BLOCKS - 1)
                        ins.then_inc(bank_full, 1)

                chunks(pe, body)


IT = INNER // P
QMAX = 127.0
MAGIC = 1.5 * 2.0 ** 23


def quantised_ffn_stage(nc, io, xres, ident, seen, ahead):
    with ExitStack() as stage:
        def sb(name, shape, dt=F32):
            return stage.enter_context(nc.sbuf_tensor("b_" + name, shape, dt))

        def sem(name):
            return stage.enter_context(nc.semaphore("b_" + name))

        downT = sb("downT", [P, IT, D], BF16)
        upT = sb("upT", [P, KB, INNER], BF16)
        gateT = sb("gateT", [P, KB, INNER], BF16)
        gate_scale, up_scale, down_scale = sb("gate_scale", [P, IT]), sb("up_scale", [P, IT]), sb("down_scale", [P, KB])
        down_row = sb("down_row", [P, D])
        ident16 = sb("ident16", [P, P], BF16)
        clip = sb("clip", [P, 2])
        sigm = sb("sigm", [P, 2])
        mv = sb("mv", [P, TILES, 2])
        rstd = sb("rstd", [P, TILES])
        peak = sb("peak", [P, 1])
        peak_all = sb("peak_all", [P, 1])
        x_scale = sb("x_scale", [P, 1])
        inv_scale = sb("inv_scale", [P, 1])
        h_peak = sb("h_peak", [P, CHUNKS * IT])
        dve_step = sem("dve_step")
        peak_ready, peak_all_ready = sem("peak_ready"), sem("peak_all_ready")
        tr_full, tr_freed = sem("tr_full"), {"act": sem("tr_freed_by_act"), "dve": sem("tr_freed_by_dve")}

        with ExitStack() as early:
            def esb(name, shape, dt=F32):
                return early.enter_context(nc.sbuf_tensor("b_" + name, shape, dt))

            raw = [ahead.gate, esb("raw_up", [P, IT, D]), esb("raw_down", [P, KB, INNER])]
            ld_small, ld_w = sem("ld_small"), [ahead.ld_gate, sem("ld_up"), sem("ld_down")]
            inv = [esb("inv_gate", [P, IT]), esb("inv_up", [P, IT]), esb("inv_down", [P, KB])]
            scale = [gate_scale, up_scale, down_scale]
            whole = [esb("whole_gate", [P, IT, D], BF16), esb("whole_up", [P, IT, D], BF16), esb("whole_down", [P, KB, INNER], BF16)]
            stats, top, low = seen.stats, seen.top, seen.low
            magic = esb("magic", [P, 1])
            half_minus = esb("half_minus", [P, TILES])
            ones = esb("ones", [P, P])
            diag = esb("diag", [P, KB, P])
            TR_BANKS = 4
            tr_bank = [early.enter_context(nc.psum_tensor(f"b_tr{i}", [P, 4, P], BF16)) for i in range(TR_BANKS)]
            row_ps = early.enter_context(nc.psum_tensor("b_row", [P, D], F32))
            quantised = sem("quantised")
            inv_ready, rounded = sem("inv_ready"), sem("early_rounded")
            var_ready, rstd_ready, half_ready = sem("var_ready"), sem("rstd_ready"), sem("half_ready")
            sig_exp = sem("sig_exp")
            diag_ready, row_full = sem("diag_ready"), sem("row_full")
            uses = [(w, r, range(KB)) for w in range(2) for r in range(IT)]
            uses += [(2, r, range(g, min(g + 4, IT))) for r in range(KB) for g in range(0, IT, 4)]
            rows_before = [0, IT, 2 * IT]

            def user(u):
                w, r, cols = uses[u]
                return "act" if w == 0 or w == 1 and r >= IT // 2 or w == 2 and u % 2 else "dve"

            def uses_of(who, w):
                return [u for u in range(len(uses)) if user(u) == who and uses[u][0] == w]

            GATE_PIECES = (slice(0, IT // 2 + 1), slice(IT // 2 + 1, IT))

            def turned_weight(u):
                w, r, cols = uses[u]
                at = slice(r * P, (r + 1) * P)
                out = downT[:, cols[0]:cols[-1] + 1, at] if w == 2 else (gateT, upT)[w][:, :, at]
                return out, tr_bank[u % TR_BANKS][:, 0:len(cols), :]

            with nc.Block() as block:
                @block.sync
                def _(sp):
                    sp.dma_start(clip[:], io["clip"].partition_broadcast(P)).then_inc(ld_small, 16)
                    sp.dma_start(raw[1][:], io["w_up"].rearrange("(i p) f -> p i f", p=P)).then_inc(ld_w[1], 16)
                    sp.dma_start(raw[2][:], io["w_down"].rearrange("(k p) i -> p k i", p=P)).then_inc(ld_w[2], 16)

                @block.gpsimd
                def _(pool):
                    nc.gpsimd.memset(half_minus[:], -0.5).then_inc(half_ready, 1)
                    pool.wait_ge(half_ready, 1)
                    pool.wait_ge(var_ready, 1)
                    nc.gpsimd.tensor_tensor(rstd[:], rstd[:], half_minus[:], ALU.pow).then_inc(rstd_ready, 1)
                    pool.wait_ge(peak_ready, 1)
                    nc.gpsimd.partition_all_reduce(peak_all[:], peak[:], P, bass.bass_isa.ReduceOp.max).then_inc(peak_all_ready, 1)

                @block.scalar
                def _(act):
                    def round_rows(w, rows, scales):
                        act.wait_ge(inv_ready, scales)
                        for r in range(raw[w].shape[1])[rows]:
                            nc.scalar.activation(raw[w][:, r, :], raw[w][:, r, :], ACT.Identity, bias=magic[:],
                                                 scale=inv[w][:, r:r + 1]).then_inc(rounded, 1)

                    def take_turned(w):
                        for u in uses_of("act", w):
                            act.wait_ge(tr_full, u + 1)
                            nc.scalar.copy(*turned_weight(u)).then_inc(tr_freed["act"], 1)

                    act.wait_ge(ld_small, 16)
                    nc.scalar.activation(sigm[:], clip[:], ACT.Exp, scale=-1.0).then_inc(sig_exp, 1)
                    round_rows(0, GATE_PIECES[0], 1)
                    round_rows(0, GATE_PIECES[1], 2)
                    take_turned(0)
                    round_rows(1, slice(None), 3)
                    round_rows(2, slice(None), 4)
                    take_turned(1)
                    take_turned(2)

                @block.vector
                def _(dve):
                    ch = Chain(dve, dve_step)
                    nc.vector.tensor_copy(ident16[:], ident[:]).then_inc(quantised, 1)
                    nc.vector.memset(magic[:], MAGIC)
                    ch.step(nc.vector.memset(ones[:], 1.0))
                    for t in range(TILES):
                        ch.step(nc.vector.bn_aggr(mv[:, t, :], stats[:, t, :]))
                    ch.wait()
                    nc.vector.tensor_scalar(rstd[:], mv[:, :, 1], LN_EPS, None, ALU.add).then_inc(var_ready, 1)
                    ch.step(nc.vector.tensor_tensor(top[:], top[:], mv[:, :, 0], ALU.subtract))
                    ch.step(nc.vector.tensor_tensor(low[:], mv[:, :, 0], low[:], ALU.subtract))
                    ch.wait()
                    ch.step(nc.vector.tensor_tensor(top[:], top[:], low[:], ALU.max))

                    def row_scales(w, loaded, rows=slice(None)):
                        dve.wait_ge(*loaded)
                        ch.step(nc.vector.tensor_reduce(inv[w][:, rows], raw[w][:, rows], AX.X, ALU.max, apply_absolute_value=True))
                        ch.wait()
                        ch.step(nc.vector.tensor_scalar(scale[w][:, rows], inv[w][:, rows], 1.0 / QMAX, None, ALU.mult))
                        ch.wait()
                        nc.vector.reciprocal(inv[w][:, rows], scale[w][:, rows]).then_inc(inv_ready, 1)

                    def whole_rows(w):
                        for r in range(raw[w].shape[1]):
                            dve.wait_ge(rounded, rows_before[w] + r + 1)
                            nc.vector.tensor_scalar(whole[w][:, r, :], raw[w][:, r, :], MAGIC, QMAX, ALU.subtract, ALU.min).then_inc(quantised, 1)

                    def take_turned(w):
                        for u in uses_of("dve", w):
                            dve.wait_ge(tr_full, u + 1)
                            nc.vector.tensor_copy(*turned_weight(u)).then_inc(tr_freed["dve"], 1)

                    for piece in GATE_PIECES:
                        row_scales(0, (ld_w[0], 16), piece)
                    dve.wait_ge(rstd_ready, 1)
                    ch.wait()
                    ch.step(nc.vector.tensor_tensor(top[:], top[:], rstd[:], ALU.mult))
                    ch.wait()
                    nc.vector.tensor_reduce(peak[:], top[:], AX.X, ALU.max).then_inc(peak_ready, 1)
                    dve.wait_ge(sig_exp, 1)
                    ch.step(nc.vector.tensor_scalar(clip[:], sigm[:], 1.0, None, ALU.add))
                    ch.wait()
                    ch.step(nc.vector.reciprocal(sigm[:], clip[:]))

                    whole_rows(0)
                    row_scales(1, (ld_w[1], 16))
                    row_scales(2, (ld_w[2], 16))
                    for k in range(KB):
                        nc.vector.tensor_scalar(diag[:, k, :], ident[:], down_scale[:, k:k + 1], None, ALU.mult).then_inc(diag_ready, 1)
                    whole_rows(1)
                    take_turned(1)
                    dve.wait_ge(peak_all_ready, 1)
                    ch.wait()
                    ch.step(nc.vector.tensor_scalar(x_scale[:], peak_all[:], sigm[:, 0:1], 1.0 / QMAX, ALU.mult, ALU.mult))
                    ch.wait()
                    ch.step(nc.vector.reciprocal(inv_scale[:], x_scale[:]))
                    ch.step(nc.vector.tensor_scalar(gate_scale[:], gate_scale[:], x_scale[:], None, ALU.mult))
                    ch.step(nc.vector.tensor_scalar(up_scale[:], up_scale[:], x_scale[:], None, ALU.mult))
                    ch.wait()
                    ch.step(nc.vector.tensor_scalar(rstd[:], rstd[:], inv_scale[:], None, ALU.mult))
                    whole_rows(2)
                    take_turned(2)
                    dve.wait_ge(row_full, 1)
                    ch.step(nc.vector.tensor_copy(down_row[:], row_ps[:]))

                @block.tensor
                def _(pe):
                    for u, (w, r, cols) in enumerate(uses):
                        pe.wait_ge(quantised, 1 + rows_before[w] + r + 1)
                        if u >= TR_BANKS:
                            who = user(u - TR_BANKS)
                            pe.wait_ge(tr_freed[who], sum(user(v) == who for v in range(u - TR_BANKS + 1)))
                        for j, c in enumerate(cols):
                            last = nc.tensor.transpose(tr_bank[u % TR_BANKS][:, j, :], whole[w][:, r, c * P:(c + 1) * P], ident16[:])
                        last.then_inc(tr_full, 1)
                    pe.wait_ge(diag_ready, KB)
                    for k in range(KB):
                        last = nc.tensor.matmul(row_ps[:, k * P:(k + 1) * P], ones[:], diag[:, k, :], start=True, stop=True)
                    last.then_inc(row_full, 1)

        hidden = sb("hidden", [P, 2, IT, CHUNK])
        spilled = [sem("spilled0"), sem("spilled1")]
        with ExitStack() as mid:
            def msb(name, shape, dt=F32):
                return mid.enter_context(nc.sbuf_tensor("b_" + name, shape, dt))

            scaled = msb("scaled", [P, 2, D])
            whole_x = msb("whole_x", [P, TPC, D], BF16)
            xT = msb("xT", [P, 2, KB, CHUNK], BF16)
            silu = msb("silu", [P, 2, CHUNK])
            scratch = msb("scratch", [P, 6])
            bank = [mid.enter_context(nc.psum_tensor(f"b_bank{i}", [P, CHUNK], BF16)) for i in range(2)]
            gate_ps = mid.enter_context(nc.psum_tensor("b_gate", [P, 2, CHUNK], F32))
            up_ps = mid.enter_context(nc.psum_tensor("b_up", [P, 2, CHUNK], F32))
            x_full, x_freed, x_quant = sem("x_full"), sem("x_freed"), sem("x_quant")
            gate_full, up_full = sem("gate_full"), sem("up_full")
            gate_used, up_used = sem("gate_used"), sem("up_used")
            dve_q = sem("dve_q")
            h_seen = sem("h_seen")
            Q_STEPS = 2 * TPC

            def all_chunks(eng, body):
                with eng.Fori(0, CHUNKS // 2 - 1) as i:
                    for j in range(2):
                        body(2 * i + j, j, False)
                body(CHUNKS - 2, 0, False)
                body(CHUNKS - 1, 1, True)

            with nc.Block() as block:
                @block.sync
                def _(sp):
                    with sp.Fori(0, CHUNKS // 2 - 1) as i:
                        for j in range(2):
                            n = 2 * i + j
                            sp.wait_ge(up_used, 2 + IT * (n + 1))
                            sp.dma_start(io["hidden"][bass.ds(n, 1)].rearrange("o p f -> (o p) f"),
                                         hidden[:, j].rearrange("p i t -> p (i t)")).then_inc(spilled[j], 16)
                    for j in range(2):
                        sp.wait_ge(spilled[j], 16 * (CHUNKS // 2))

                @block.scalar
                def _(act):
                    nc.scalar.copy(scratch[:, 0:1], clip[:, 0:1]).then_inc(gate_used, 1)
                    nc.scalar.copy(scratch[:, 1:2], clip[:, 0:1]).then_inc(gate_used, 1)
                    for k in range(KB):
                        act.wait_ge(x_full, k + 1)
                        nc.scalar.copy(xT[:, 0, k, :], bank[k % 2][:]).then_inc(x_freed, 1)

                    def body(n, j, last):
                        for i in range(IT):
                            k = n * IT + i
                            b = (j * IT + i) % 2
                            act.wait_ge(gate_full, k + 1)
                            act.wait_ge(up_used, k + 1)
                            nc.scalar.activation(silu[:, b, :], gate_ps[:, b, :], ACT.Silu, scale=gate_scale[:, i:i + 1]).then_inc(gate_used, 1)
                            if i >= 7 and not last:
                                act.wait_ge(x_full, KB * (n + 1) + i - 6)
                                nc.scalar.copy(xT[:, 1 - j, i - 7, :], bank[(i - 7) % 2][:]).then_inc(x_freed, 1)

                    all_chunks(act, body)

                @block.vector
                def _(dve):
                    ch = Chain(dve, dve_q)
                    nc.vector.memset(scratch[:, 2:3], 0.0).then_inc(up_used, 1)
                    nc.vector.memset(scratch[:, 3:4], 0.0).then_inc(up_used, 1)
                    nc.vector.memset(scratch[:, 4:5], 0.0).then_inc(spilled[0], 16)
                    nc.vector.memset(scratch[:, 5:6], 0.0).then_inc(spilled[1], 16)

                    def quantise(n, t, done):
                        buf = scaled[:, t % 2, :]
                        if done is not None:
                            dve.wait_ge(x_quant, done)
                        at = n * TPC + t
                        ch.step(nc.vector.tensor_scalar(buf, xres[:, at, 0:D], mv[:, at, 0:1], rstd[:, bass.ds(at, 1)], ALU.subtract, ALU.mult))
                        ch.wait()
                        ch.step(nc.vector.tensor_scalar(buf, buf, MAGIC, MAGIC + QMAX, ALU.add, ALU.min))
                        ch.wait()
                        nc.vector.tensor_scalar(whole_x[:, t, :], buf, MAGIC - QMAX - 1.0, MAGIC, ALU.max, ALU.subtract).then_inc(x_quant, 1)

                    for t in range(TPC):
                        quantise(0, t, t - 1 if t >= 2 else None)

                    def body(n, j, last):
                        ch.base, ch.k = Q_STEPS * (n + 1), 0

                        def greatest(i):
                            dve.wait_ge(up_used, n * IT + i + 3)
                            nc.vector.tensor_reduce(h_peak[:, bass.ds(n * IT + i, 1)], hidden[:, j, i, :], AX.X, ALU.max,
                                                    apply_absolute_value=True).then_inc(h_seen, 1)

                        dve.wait_ge(spilled[j], 16 * ((n + 2 - j) // 2) if isinstance(n, int) else 8 * (n + 2 - j))
                        for i in range(IT):
                            k = n * IT + i
                            b = (j * IT + i) % 2
                            dve.wait_ge(up_full, k + 1)
                            dve.wait_ge(gate_used, k + 3)
                            nc.vector.scalar_tensor_tensor(hidden[:, j, i, :], up_ps[:, b, :], up_scale[:, i:i + 1], silu[:, b, :],
                                                           ALU.mult, ALU.mult).then_inc(up_used, 1)
                            if i >= 1:
                                greatest(i - 1)
                            if i < TPC and not last:
                                quantise(n + 1, i, TPC * (n + 1) + i - 1)
                        greatest(IT - 1)

                    all_chunks(dve, body)

                @block.tensor
                def _(pe):
                    def turn(n, k, count):
                        if count is not None:
                            pe.wait_ge(x_freed, count)
                        for t in range(TPC):
                            last = nc.tensor.transpose(bank[k % 2][:, t * P:(t + 1) * P], whole_x[:, t, k * P:(k + 1) * P], ident16[:])
                        last.then_inc(x_full, 1)

                    pe.wait_ge(x_quant, TPC)
                    for k in range(KB):
                        turn(0, k, k - 1 if k >= 2 else None)

                    def body(n, j, last):
                        pe.wait_ge(x_freed, KB * (n + 1))
                        for i in range(IT):
                            b = (j * IT + i) % 2
                            for ps, w, full, used in ((gate_ps, gateT, gate_full, gate_used), (up_ps, upT, up_full, up_used)):
                                pe.wait_ge(used, n * IT + i + 1)
                                for k in range(KB):
                                    ins = nc.tensor.matmul(ps[:, b, :], w[:, k, i * P:(i + 1) * P], xT[:, j, k, :],
                                                           start=(k == 0), stop=(k == KB - 1))
                                ins.then_inc(full, 1)
                            if i == 6 and not last:
                                pe.wait_ge(x_quant, TPC * (n + 2))
                            if i >= 6 and i < 6 + KB and not last:
                                turn(n + 1, i - 6, KB * (n + 1) + i - 7)

                    all_chunks(pe, body)

        with ExitStack() as late:
            def lsb(name, shape, dt=F32):
                return late.enter_context(nc.sbuf_tensor("b_" + name, shape, dt))

            whole_h = lsb("whole_h", [P, 2, IT, CHUNK], BF16)
            h_scale, h_inv = lsb("h_scale", [P, 1]), lsb("h_inv", [P, 1])
            minus_magic = lsb("minus_magic", [P, 1])
            delta = lsb("delta", [P, 2, D])
            out_ps = late.enter_context(nc.psum_tensor("b_out", [P, TPC, D], F32))
            rounded, whole_ready = sem("rounded"), sem("whole_ready")
            out_full, out_freed, added = sem("out_full"), sem("out_freed"), sem("added")
            reloaded = [sem("reloaded0"), sem("reloaded1")]
            h_step = sem("h_step")
            magic_set = sem("magic_set")
            LOOPS = CHUNKS // 2 - 1
            PIECES = (slice(0, IT // 2), slice(IT // 2, IT))

            def order(eng, body):
                body(0, 0, CHUNKS - 2, None, True)
                body(1, 1, CHUNKS - 1, 0, True)
                with eng.Fori(0, LOOPS - 1) as i:
                    body(2 * i + 2, 0, 2 * i, i, True)
                    body(2 * i + 3, 1, 2 * i + 1, i + 1, True)
                body(CHUNKS - 2, 0, CHUNKS - 4, LOOPS - 1, True)
                body(CHUNKS - 1, 1, CHUNKS - 3, None, False)

            with nc.Block() as block:
                @block.sync
                def _(sp):
                    with sp.Fori(0, LOOPS) as i:
                        for j in range(2):
                            sp.wait_ge(whole_ready, len(PIECES) * (2 * i + j + 1))
                            sp.dma_start(hidden[:, j].rearrange("p i t -> p (i t)"),
                                         io["hidden"][bass.ds(2 * i + j, 1)].rearrange("o p f -> (o p) f")).then_inc(reloaded[j], 16)

                @block.gpsimd
                def _(pool):
                    pool.wait_ge(peak_ready, 2)
                    nc.gpsimd.partition_all_reduce(peak_all[:], peak[:], P, bass.bass_isa.ReduceOp.max).then_inc(peak_all_ready, 1)

                    def body(q, j, n, load, more):
                        for t in range(TPC):
                            pool.wait_ge(out_freed, q * TPC + t + 1)
                            row = xres[:, n * TPC + t, 0:D]
                            nc.gpsimd.tensor_tensor(row, row, delta[:, t % 2, :], ALU.add).then_inc(added, 1)

                    order(pool, body)

                @block.scalar
                def _(act):
                    act.wait_ge(magic_set, 1)

                    def body(q, j, n, load, more):
                        if not isinstance(q, int) or q >= 2:
                            act.wait_ge(out_full, TPC * (q - 1))
                        for i, piece in enumerate(PIECES):
                            act.wait_ge(rounded, len(PIECES) * q + i + 1)
                            nc.scalar.activation(whole_h[:, j, piece], hidden[:, j, piece], ACT.Identity, bias=minus_magic[:]).then_inc(whole_ready, 1)

                    order(act, body)

                @block.vector
                def _(dve):
                    ch = Chain(dve, h_step)
                    nc.vector.memset(minus_magic[:], -MAGIC).then_inc(magic_set, 1)
                    dve.wait_ge(h_seen, CHUNKS * IT)
                    nc.vector.tensor_reduce(peak[:], h_peak[:], AX.X, ALU.max).then_inc(peak_ready, 1)
                    dve.wait_ge(peak_all_ready, 2)
                    ch.step(nc.vector.tensor_scalar(h_scale[:], peak_all[:], sigm[:, 1:2], 1.0 / QMAX, ALU.mult, ALU.mult))
                    ch.wait()
                    ch.step(nc.vector.reciprocal(h_inv[:], h_scale[:]))
                    ch.step(nc.vector.tensor_scalar(down_row[:], down_row[:], h_scale[:], None, ALU.mult))
                    ch.wait()

                    def round_piece(j, piece):
                        values = hidden[:, j, piece]
                        ch.step(nc.vector.tensor_scalar(values, values, h_inv[:], QMAX, ALU.mult, ALU.min))
                        ch.wait()
                        nc.vector.tensor_scalar(values, values, -QMAX - 1.0, MAGIC, ALU.max, ALU.add).then_inc(rounded, 1)

                    def scale_out(q, t):
                        dve.wait_ge(out_full, q * TPC + t + 1)
                        if not isinstance(q, int) or q or t >= 2:
                            dve.wait_ge(added, q * TPC + t - 1)
                        nc.vector.tensor_tensor(delta[:, t % 2, :], out_ps[:, t, :], down_row[:], ALU.mult).then_inc(out_freed, 1)

                    for piece in PIECES:
                        round_piece(0, piece)
                    base = ch.k

                    def body(q, j, n, load, more):
                        ch.base, ch.k = len(PIECES) * q + base, 0
                        if more:
                            if load is not None:
                                dve.wait_ge(reloaded[1 - j], 16 * (load + 1))
                            round_piece(1 - j, PIECES[0])
                        if not isinstance(q, int) or q:
                            scale_out(q - 1, TPC - 1)
                        if more:
                            round_piece(1 - j, PIECES[1])
                        for t in range(TPC - 1):
                            scale_out(q, t)

                    order(dve, body)
                    scale_out(CHUNKS - 1, TPC - 1)

                @block.tensor
                def _(pe):
                    def body(q, j, n, load, more):
                        for t in range(TPC):
                            if not isinstance(q, int) or q:
                                pe.wait_ge(out_freed, (q - 1) * TPC + t + 1)
                            for i in range(IT):
                                if t == 0 and i in (PIECES[0].start, PIECES[1].start):
                                    pe.wait_ge(whole_ready, len(PIECES) * q + (2 if i else 1))
                                ins = nc.tensor.matmul(out_ps[:, t, :], whole_h[:, j, i, t * P:(t + 1) * P], downT[:, i, :],
                                                       start=(i == 0), stop=(i == IT - 1))
                            ins.then_inc(out_full, 1)

                    order(pe, body)


H1, DH1 = 16, 32
VW1 = DH1 + 1
QUADS = H1 // 4
HALF_HEADS = H1 // 2
MASK_TILES = 2
MASK_CHUNK = MASK_TILES * P
MASK_CHUNKS = TOK // MASK_CHUNK
MASK_CPB = MASK_CHUNKS // B


def masked_attention_stage(nc, io, xres, ident, seen):
    NT, NC = MASK_TILES, MASK_CHUNKS
    with ExitStack() as stage:
        def sb(name, shape, dt=F32):
            return stage.enter_context(nc.sbuf_tensor("c_" + name, shape, dt))

        def pb(name, shape, dt=F32):
            return stage.enter_context(nc.psum_tensor("c_" + name, shape, dt))

        def sem(name):
            return stage.enter_context(nc.semaphore("c_" + name))

        keys_hi, keys_lo = (sb("keys_" + x, [P, B, QUADS, 4 * KEYS], F32R) for x in ("hi", "lo"))
        vals = sb("vals", [P, B, H1, VW1])
        bias = sb("bias", [P, 2, KB])
        tiny = sb("tiny", [P, 1])
        bo = sb("bo", [P, D])
        wq_hi, wq_lo = (sb("wq_" + x, [P, KB, D], F32R) for x in ("hi", "lo"))
        wo_hi, wo_lo = (sb("wo_" + x, [P, KB, D], F32R) for x in ("hi", "lo"))

        score_ps = pb("score", [P, H1, KEYS])
        bank = [pb(f"bank{i}", [P, CHUNK]) for i in range(2)]
        pv_ps = [pb(f"pv{i}", [P, CHUNK]) for i in range(2)]

        ld_ctx, ld_small, ld_wk, ld_wv, ld_wq, ld_wo = (sem("ld_" + x) for x in ("ctx", "small", "wk", "wv", "wq", "wo"))
        ld_mask, mask_used = sem("ld_mask"), sem("mask_used")
        bank_full = sem("bank_full")
        freed = {"dve": sem("freed_by_dve"), "act": sem("freed_by_act")}
        early_hi, x_hi_ready, q_hi_ready, attn_hi_ready = (sem(x) for x in ("early_hi", "x_hi", "q_hi", "attn_hi"))
        x_lo_ready, attn_lo_ready = sem("x_lo"), sem("attn_lo")
        set_up, half_ready = sem("set_up"), sem("half_ready")
        var_ready, xn_ready, bo_added = sem("var_ready"), sem("xn_ready"), sem("bo_added")
        score_full, shifted, exped = sem("score_full"), sem("shifted"), sem("exped")
        pv_full, normed = sem("pv_full"), sem("normed")
        dve_step, out_added, rstd_ready = sem("dve_step"), sem("out_added"), sem("rstd_ready")

        EMPTIED_BY = {"OT": "act", "PT": "act", "Q": "dve", "T": "act", "O": "act"}

        def left(n, k=1):
            return not isinstance(n, int) or n + k < NC

        def steps(n):
            out = []
            for t in range(NT if left(n) else NT + 2):
                g = n * NT + t if isinstance(n, int) else None
                probs_left = (g is None or g >= 1) and t <= NT
                out_left = g is None or g >= 2
                here = {"PT": probs_left, "OT": out_left, "Q": left(n), "T": left(n, 2), "O": out_left}
                step = [what for what in ("PT", "PT", "OT", "PT", "Q", "PT", "Q", "T", "O") if here[what]]
                out.append(step)
            return out

        def users(n):
            return [EMPTIED_BY[what] for step in steps(n) for what in step]

        def plan(n):
            pos = len(users(n - 1)) if not left(n) else 0
            out = []
            for step in steps(n):
                at = {}
                for what in step:
                    at.setdefault(what, []).append(pos)
                    pos += 1
                out.append(at)
            return out

        PRE = ["act"] * KB + ["dve"] * KB + ["dve"] * B + ["act"] * NT + ["dve"] * KB + ["act"] * NT
        PRE_K, PRE_V, PRE_T, PRE_Q, PRE_T1 = KB, 2 * KB, 2 * KB + B, 2 * KB + B + NT, 3 * KB + B + NT
        FIRST, SECOND, BODY, LAST = users(0), users(1), users(None), users(NC - 2) + users(NC - 1)
        ring = Ring(PRE + FIRST + SECOND, BODY)
        DVE_STEPS, DVE_HEAD = 6 * NT, 2

        class Uses:

            def __init__(self, n):
                self.start = None if not isinstance(n, int) or n >= 2 else len(PRE) + n * len(FIRST)
                self.n, self.seq = (n - 2, BODY) if left(n, 2) else (NC - 4, LAST)

            def full(self, pos):
                return ring.full(self.n, pos) if self.start is None else self.start + pos + 1

            def emptied(self, pos):
                return ring.emptied(self.n, self.seq, pos) if self.start is None else ring.prefix_emptied(self.start + pos)

            def reuse(self, pos):
                return ring.reuse(self.n, self.seq, pos) if self.start is None else ring.prefix_emptied(self.start + pos - 2)

        def all_chunks(eng, body):
            body(0, 0)
            body(1, 1)
            with eng.Fori(1, NC // 2 - 1) as i:
                body(2 * i, 0)
                body(2 * i + 1, 1)
            body(NC - 2, 0)
            body(NC - 1, 1)

        def batch(n):
            return n // MASK_CPB

        with ExitStack() as early:
            def esb(name, shape, dt=F32):
                return early.enter_context(nc.sbuf_tensor("c_" + name, shape, dt))

            wk, wv, wq, wo = (esb(x, [P, KB, D]) for x in ("wk", "wv", "wq", "wo"))
            bv = esb("bv", [P, D])
            WQ, WO = "wq", "wo"
            EARLY_HI = [0, 1, WQ, 2, WO, 3]
            assert B == 2 and QUADS == 4
            ctx_t, ctxT = esb("ctx", [P, B, D]), esb("ctxT", [P, KB, B * KEYS])

            with nc.Block() as block:
                @block.sync
                def _(sp):
                    sp.dma_start(ctx_t[:], io["ctx"].rearrange("(b p) f -> p b f", p=P)).then_inc(ld_ctx, 16)
                    for tile, name, s in ((wk, "wk1", ld_wk), (wv, "wv1", ld_wv), (wq, "wq1", ld_wq), (wo, "wo1", ld_wo)):
                        sp.dma_start(tile[:], io[name].rearrange("(k p) n -> p k n", p=P)).then_inc(s, 16)
                        if tile is wk:
                            sp.dma_start(bias[:], io["qk_bias"]).then_inc(ld_small, 16)
                            sp.dma_start(bv[:], io["bv"].partition_broadcast(P)).then_inc(ld_small, 16)
                            sp.dma_start(bo[:], io["bo"].partition_broadcast(P)).then_inc(ld_small, 16)

                @block.scalar
                def _(act):
                    for k in range(KB):
                        act.wait_ge(bank_full, ring.prefix_full(k))
                        nc.scalar.copy(ctxT[:, k, :], bank[k % 2][:, 0:B * KEYS]).then_inc(freed["act"], 1)
                    act.wait_ge(ld_small, 48)
                    act.wait_ge(set_up, 4)
                    for what in EARLY_HI:
                        if what in (WQ, WO):
                            loaded, hi, full = (ld_wq, wq_hi, wq) if what == WQ else (ld_wo, wo_hi, wo)
                            act.wait_ge(loaded, 16)
                            nc.scalar.copy(hi[:], full[:]).then_inc(early_hi, 1)
                            continue
                        g = what
                        act.wait_ge(bank_full, ring.prefix_full(PRE_K + g))
                        for h in range(4):
                            part = slice(h * DH1, (h + 1) * DH1)
                            last = nc.scalar.activation(keys_hi[part, :, g, h * KEYS:(h + 1) * KEYS],
                                                        bank[(PRE_K + g) % 2][part, 0:B * KEYS].rearrange("p (b k) -> p b k", b=B),
                                                        ACT.Identity, bias=bias[part, 1, g:g + 1])
                        last.then_inc(early_hi, 1)

                @block.vector
                def _(dve):
                    nc.vector.memset(vals[:, :, :, DH1:VW1], 1.0).then_inc(set_up, 1)
                    nc.vector.memset(keys_hi[:].bitcast(F32), 0.0).then_inc(set_up, 1)
                    nc.vector.memset(keys_lo[:].bitcast(F32), 0.0).then_inc(set_up, 1)
                    nc.vector.memset(tiny[:], 1e-9 * DH1 ** 0.5).then_inc(set_up, 1)
                    dve.wait_ge(set_up, 4)
                    dve.wait_ge(ld_small, 48)
                    for g in range(QUADS):
                        dve.wait_ge(early_hi, EARLY_HI.index(g) + 1)
                        for h in range(4):
                            part = slice(h * DH1, (h + 1) * DH1)
                            at = (part, slice(None), g, slice(h * KEYS, (h + 1) * KEYS))
                            last = nc.vector.scalar_tensor_tensor(keys_lo[at], bank[(PRE_K + g) % 2][part, 0:B * KEYS].rearrange("p (b k) -> p b k", b=B),
                                                                  bias[part, 1, g:g + 1], keys_hi[at], ALU.add, ALU.subtract)
                        last.then_inc(freed["dve"], 1)
                    for b, (what, lo, full, hi) in enumerate(((WQ, wq_lo, wq, wq_hi), (WO, wo_lo, wo, wo_hi))):
                        dve.wait_ge(early_hi, EARLY_HI.index(what) + 1)
                        nc.vector.tensor_tensor(lo[:], full[:], hi[:], ALU.subtract).then_inc(set_up, 1)
                        dve.wait_ge(bank_full, ring.prefix_full(PRE_V + b))
                        nc.vector.tensor_tensor(vals[:, b, :, 0:DH1], bank[(PRE_V + b) % 2][:].rearrange("p (h d) -> p h d", d=DH1),
                                                bv[:].rearrange("p (h d) -> p h d", d=DH1), ALU.add).then_inc(freed["dve"], 1)

                @block.tensor
                def _(pe):
                    def begin(u):
                        if u >= 2:
                            who, count = ring.prefix_emptied(u - 2)
                            pe.wait_ge(freed[who], count)
                        return bank[u % 2]

                    pe.wait_ge(ld_ctx, 16)
                    for k in range(KB):
                        out = begin(k)
                        for b in range(B):
                            last = nc.tensor.transpose(out[:, b * KEYS:(b + 1) * KEYS], ctx_t[:, b, k * P:(k + 1) * P], ident[:])
                        last.then_inc(bank_full, 1)
                    pe.wait_ge(freed["act"], KB)
                    pe.wait_ge(ld_wk, 16)
                    for m in range(KB):
                        out = begin(PRE_K + m)
                        for k in range(KB):
                            last = nc.tensor.matmul(out[:, 0:B * KEYS], wk[:, k, m * P:(m + 1) * P], ctxT[:, k, :], start=(k == 0), stop=(k == KB - 1))
                        last.then_inc(bank_full, 1)
                    pe.wait_ge(ld_wv, 16)
                    for b in range(B):
                        out = begin(PRE_V + b)
                        for k in range(KB):
                            last = nc.tensor.matmul(out[:], ctxT[:, k, b * KEYS:(b + 1) * KEYS], wv[:, k, :], start=(k == 0), stop=(k == KB - 1))
                        last.then_inc(bank_full, 1)

        masks = sb("masks", [P, 2, NT, KEYS], U8)
        xn = sb("xn", [P, 2, D])
        x_full, attn_full = sb("x_full", [P, KB, P]), sb("attn_full", [P, KB, P])
        x_hi, x_lo = (sb("x_" + x, [P, 2, KB, MASK_CHUNK], F32R) for x in ("hi_parts", "lo_parts"))
        q_hi, q_lo = (sb("q_" + x, [P, 2, KB, MASK_CHUNK], F32R) for x in ("hi_parts", "lo_parts"))
        attn_hi, attn_lo = (sb("attn_" + x, [P, KB, P], F32R) for x in ("hi_parts", "lo_parts"))
        stats, mv = sb("stats", [P, 2, 6]), sb("mv", [P, 2, 2])
        var, rstd, minus_half = sb("var", [P, 2]), sb("rstd", [P, 2]), sb("minus_half", [P, 1])
        top = sb("top", [P, H1])
        held = sb("held", [P, 1])
        probs = sb("probs", [P, 2, H1, KEYS])
        probsT = sb("probsT", [P, H1, P])
        recip = sb("recip", [P, 2, HALF_HEADS])
        attn = sb("attn", [P, D])

        with nc.Block() as block:
            @block.sync
            def _(sp):
                def body(n, j):
                    if not isinstance(n, int) or n >= 1:
                        sp.wait_ge(mask_used, 2 * NT * (n - 1) + 1)
                    c = n % MASK_CPB
                    sp.dma_start(masks[:, j], io["mask"][bass.ds(c * MASK_CHUNK, MASK_CHUNK), :].rearrange("(t p) k -> p t k", p=P)).then_inc(ld_mask, 16)

                all_chunks(sp, body)

            @block.gpsimd
            def _(pool):
                nc.gpsimd.memset(minus_half[:], -0.5).then_inc(half_ready, 1)
                pool.wait_ge(half_ready, 1)
                pool.wait_ge(ld_small, 48)

                def deviation(tile, t):
                    pool.wait_ge(var_ready, tile + 1)
                    nc.gpsimd.tensor_tensor(rstd[:, t:t + 1], var[:, t:t + 1], minus_half[:], ALU.pow).then_inc(rstd_ready, 1)

                def add_bias(tile):
                    pool.wait_ge(xn_ready, tile + 1)
                    rows = xres[:, tile, 0:D]
                    nc.gpsimd.tensor_tensor(rows, rows, bo[:], ALU.add).then_inc(bo_added, 1)

                def x_low(tile, j, t):
                    pool.wait_ge(x_hi_ready, tile + 1)
                    at = (slice(None), j, slice(None), slice(t * P, (t + 1) * P))
                    nc.gpsimd.tensor_tensor(x_lo[at], x_full[:], x_hi[at], ALU.subtract).then_inc(x_lo_ready, 1)

                def add_out(u, pos, tile):
                    pool.wait_ge(freed["act"], u.emptied(pos)[1])
                    pool.wait_ge(bo_added, tile + 1)
                    rows = xres[:, tile, 0:D]
                    nc.gpsimd.tensor_tensor(rows, rows, attn_full[:].rearrange("p k t -> p (k t)"), ALU.add).then_inc(out_added, 1)

                def attn_low(tile):
                    pool.wait_ge(attn_hi_ready, tile + 1)
                    nc.gpsimd.tensor_tensor(attn_lo[:], attn_full[:], attn_hi[:], ALU.subtract).then_inc(attn_lo_ready, 1)

                for t in range(NT):
                    deviation(t, t)
                for t in range(NT):
                    x_low(t, 0, t)
                for t in range(NT):
                    deviation(NT + t, t)
                for t in range(2 * NT):
                    add_bias(t)
                for t in range(NT):
                    x_low(NT + t, 1, t)

                def body(n, j):
                    u = Uses(n)
                    for t, s in enumerate(plan(n)):
                        tile = n * NT + t
                        if "T" in s:
                            deviation(tile + 2 * NT, t)
                        if "OT" in s:
                            attn_low(tile - 2)
                        if "T" in s:
                            add_bias(tile + 2 * NT)
                            x_low(tile + 2 * NT, j, t)
                        if "O" in s:
                            add_out(u, s["O"][0], tile - 2)

                all_chunks(pool, body)

            @block.scalar
            def _(act):
                def copy(out, full, pos):
                    act.wait_ge(bank_full, full)
                    nc.scalar.copy(out, bank[pos % 2][:]).then_inc(freed["act"], 1)

                def x_tile(tile, j, t, full, pos, emptied):
                    if not (isinstance(tile, int) and tile < 1):
                        act.wait_ge(x_lo_ready, tile)
                    copy(x_full[:].rearrange("p k c -> p (k c)"), full, pos)
                    act.wait_ge(freed["act"], emptied)
                    nc.scalar.copy(x_hi[:, j, :, t * P:(t + 1) * P], x_full[:]).then_inc(x_hi_ready, 1)

                def queries(j, m, full, pos):
                    act.wait_ge(bank_full, full)
                    nc.scalar.activation(q_hi[:, j, m, :], bank[pos % 2][:, 0:MASK_CHUNK], ACT.Identity, bias=bias[:, 0, m:m + 1]).then_inc(q_hi_ready, 1)

                for t in range(NT):
                    x_tile(t, 0, t, ring.prefix_full(PRE_T + t), PRE_T + t, ring.prefix_emptied(PRE_T + t)[1])
                for m in range(KB):
                    queries(0, m, ring.prefix_full(PRE_Q + m), PRE_Q + m)
                for t in range(NT):
                    x_tile(NT + t, 1, t, ring.prefix_full(PRE_T1 + t), PRE_T1 + t, ring.prefix_emptied(PRE_T1 + t)[1])

                def body(n, j):
                    u = Uses(n)

                    def turned_probs(s, g):
                        pos = s["PT"][g]
                        copy(probsT[:, 4 * g:4 * g + 4, :].rearrange("p h t -> p (h t)"), u.full(pos), pos)

                    def exponentials(tile, t, half):
                        act.wait_ge(shifted, 2 * tile + half + 1)
                        part = probs[:, t % 2, half * HALF_HEADS:(half + 1) * HALF_HEADS, :]
                        nc.scalar.activation(part, part, ACT.Exp, scale=DH1 ** -0.5).then_inc(exped, 1)

                    for t, s in enumerate(plan(n)):
                        tile = n * NT + t
                        if "PT" in s:
                            turned_probs(s, 0)
                            turned_probs(s, 1)
                        if "OT" in s:
                            pos = s["OT"][0]
                            if not (isinstance(tile, int) and tile < 3):
                                act.wait_ge(out_added, tile - 2)
                            copy(attn_full[:].rearrange("p k t -> p (k t)"), u.full(pos), pos)
                            act.wait_ge(freed["act"], u.emptied(pos)[1])
                            nc.scalar.copy(attn_hi[:], attn_full[:]).then_inc(attn_hi_ready, 1)
                        if t < NT:
                            exponentials(tile, t, 0)
                        if "PT" in s:
                            turned_probs(s, 2)
                        if "Q" in s:
                            queries(1 - j, 2 * t, u.full(s["Q"][0]), s["Q"][0])
                        if t < NT:
                            exponentials(tile, t, 1)
                        if "PT" in s:
                            turned_probs(s, 3)
                        if "Q" in s:
                            queries(1 - j, 2 * t + 1, u.full(s["Q"][1]), s["Q"][1])
                        if "T" in s:
                            pos = s["T"][0]
                            x_tile(tile + 2 * NT, j, t, u.full(pos), pos, u.emptied(pos)[1])
                        if "O" in s:
                            pos = s["O"][0]
                            act.wait_ge(attn_lo_ready, tile - 1)
                            copy(attn_full[:].rearrange("p k t -> p (k t)"), u.full(pos), pos)

                all_chunks(act, body)

            @block.vector
            def _(dve):
                ch = Chain(dve, dve_step)

                def norm_stats(tile, t, first=False):
                    if not first:
                        dve.wait_ge(xn_ready, tile - 1)
                    ch.step(nc.vector.bn_stats(stats[:, t, :], xres[:, tile, 0:D]))
                    ch.wait()
                    nc.vector.memset(held[:], 0.0)
                    ch.step(nc.vector.bn_aggr(mv[:, t, :], stats[:, t, :]))
                    ch.wait()
                    nc.vector.tensor_scalar(var[:, t:t + 1], mv[:, t, 1:2], LN_EPS, None, ALU.add).then_inc(var_ready, 1)

                def norm_row(tile, t, first=False):
                    dve.wait_ge(rstd_ready, tile + 1)
                    if not first:
                        dve.wait_ge(x_hi_ready, tile - 1)
                    nc.vector.tensor_scalar(xn[:, t, :], xres[:, tile, 0:D], mv[:, t, 0:1], rstd[:, t:t + 1],
                                            ALU.subtract, ALU.mult).then_inc(xn_ready, 1)

                def queries(n, j, m, pos):
                    dve.wait_ge(q_hi_ready, n * KB + m + 1)
                    nc.vector.scalar_tensor_tensor(q_lo[:, j, m, :], bank[pos % 2][:, 0:MASK_CHUNK], bias[:, 0, m:m + 1], q_hi[:, j, m, :],
                                                   ALU.add, ALU.subtract).then_inc(freed["dve"], 1)

                def shift(tile, j, t, half):
                    part = slice(half * HALF_HEADS, (half + 1) * HALF_HEADS)
                    shape = [P, HALF_HEADS, KEYS]
                    dve.wait_ge(score_full, 2 * tile + half + 1)
                    nc.vector.memset(held[:], 0.0)
                    ch.step(nc.vector.copy_predicated(score_ps[:, part, :], masks[:, j, t, :].unsqueeze(1).to_broadcast(shape),
                                                      tiny[:].unsqueeze(2).to_broadcast(shape)))
                    ch.wait()
                    nc.vector.tensor_reduce(top[:, part], score_ps[:, part, :], AX.X, ALU.max).then_inc(mask_used, 1)
                    dve.wait_ge(mask_used, 2 * tile + half + 1)
                    nc.vector.tensor_tensor(probs[:, t, part, :], score_ps[:, part, :], top[:, part].unsqueeze(2).to_broadcast(shape),
                                            ALU.subtract).then_inc(shifted, 1)

                def normalise(tile, half):
                    got = pv_ps[half][:, 0:HALF_HEADS * VW1].rearrange("p (h d) -> p h d", d=VW1)
                    dve.wait_ge(pv_full, 2 * tile + half + 1)
                    ch.step(nc.vector.reciprocal(recip[:, half, :], got[:, :, DH1]))
                    ch.wait()
                    nc.vector.tensor_tensor(attn[:, half * D // 2:(half + 1) * D // 2].rearrange("p (h d) -> p h d", d=DH1),
                                            got[:, :, 0:DH1], recip[:, half, :].unsqueeze(2).to_broadcast([P, HALF_HEADS, DH1]),
                                            ALU.mult).then_inc(normed, 1)

                def row_stats(tile):
                    dve.wait_ge(out_added, tile + 1)
                    nc.vector.bn_stats(seen.stats[:, tile, :], xres[:, tile, 0:D])

                for tile in range(2 * NT):
                    norm_stats(tile, tile % 2, tile < 2)
                    norm_row(tile, tile % 2, tile < 2)
                for m in range(KB):
                    queries(0, 0, m, PRE_Q + m)
                dve.wait_ge(ld_mask, 16)
                shift(0, 0, 0, 0)
                head = ch.k

                def body(n, j):
                    if left(n) and not (isinstance(n, int) and n == 0):
                        ch.base, ch.k = n * DVE_STEPS - DVE_HEAD + head, 0
                    for t, s in enumerate(plan(n)):
                        tile = n * NT + t
                        if "T" in s:
                            norm_stats(tile + 2 * NT, t)
                        if t < NT:
                            shift(tile, j, t, 1)
                        if "PT" in s:
                            normalise(tile - 1, 0)
                        if not isinstance(tile, int) or tile >= 3:
                            row_stats(tile - 3)
                        if "Q" in s:
                            queries(n + 1, 1 - j, 2 * t, s["Q"][0])
                        if "T" in s:
                            norm_row(tile + 2 * NT, t)
                        if "Q" in s:
                            queries(n + 1, 1 - j, 2 * t + 1, s["Q"][1])
                        if t < NT - 1:
                            shift(tile + 1, j, t + 1, 0)
                        elif left(n):
                            dve.wait_ge(ld_mask, 16 * (n + 2))
                            shift(tile + 1, 1 - j, 0, 0)
                        if "PT" in s:
                            normalise(tile - 1, 1)
                    assert not left(n, 2) or ch.k == DVE_STEPS - (DVE_HEAD - head if isinstance(n, int) and n == 0 else 0), ch.k

                all_chunks(dve, body)
                row_stats(TILES - 1)

            @block.tensor
            def _(pe):
                def begin(reuse, pos):
                    pe.wait_ge(freed[reuse[0]], reuse[1])
                    return bank[pos % 2]

                def parts(out, hi, lo, w_hi, w_lo, first=True, last=True):
                    nc.tensor.matmul(out, hi, w_hi, start=first, stop=False)
                    nc.tensor.matmul(out, hi, w_lo, start=False, stop=False)
                    return nc.tensor.matmul(out, lo, w_hi, start=False, stop=last)

                def turn_x(out, t):
                    for k in range(KB):
                        last = nc.tensor.transpose(out[:, k * P:(k + 1) * P], xn[:, t, k * P:(k + 1) * P], ident[:])
                    last.then_inc(bank_full, 1)

                def project(out, j, m):
                    cols = slice(m * P, (m + 1) * P)
                    for k in range(KB):
                        last = parts(out[:, 0:MASK_CHUNK], wq_hi[:, k, cols], wq_lo[:, k, cols], x_hi[:, j, k, :], x_lo[:, j, k, :], k == 0, k == KB - 1)
                    last.then_inc(bank_full, 1)

                def scores(b, tile, j, t, g):
                    if g % 2 == 0 and not (isinstance(tile, int) and tile == 0):
                        pe.wait_ge(shifted, 2 * tile - 1 + g // 2)
                    at = slice(t * P, (t + 1) * P)
                    last = parts(score_ps[:, 4 * g:4 * g + 4, :].rearrange("p h k -> p (h k)"), q_hi[:, j, g, at], q_lo[:, j, g, at],
                                 keys_hi[:, b, g, :], keys_lo[:, b, g, :])
                    if g % 2:
                        last.then_inc(score_full, 1)

                for t in range(NT):
                    pe.wait_ge(xn_ready, t + 1)
                    turn_x(begin(ring.prefix_emptied(PRE_T + t - 2), PRE_T + t), t)
                pe.wait_ge(x_lo_ready, NT)
                for m in range(KB):
                    project(begin(ring.prefix_emptied(PRE_Q + m - 2), PRE_Q + m), 0, m)
                for t in range(NT):
                    pe.wait_ge(xn_ready, NT + t + 1)
                    turn_x(begin(ring.prefix_emptied(PRE_T1 + t - 2), PRE_T1 + t), t)
                pe.wait_ge(freed["dve"], PRE.count("dve"))
                for g in range(2):
                    scores(0, 0, 0, 0, g)

                def turn_probs(u, s, tile, t, g):
                    pe.wait_ge(exped, 2 * tile + g // 2 + 1)
                    pos = s["PT"][g]
                    out = begin(u.reuse(pos), pos)
                    for h in range(4):
                        last = nc.tensor.transpose(out[:, h * P:(h + 1) * P], probs[:, t % 2, 4 * g + h, :], ident[:])
                    last.then_inc(bank_full, 1)

                def turn_attn(u, pos, tile):
                    pe.wait_ge(normed, 2 * (tile + 1))
                    out = begin(u.reuse(pos), pos)
                    for k in range(KB):
                        last = nc.tensor.transpose(out[:, k * P:(k + 1) * P], attn[:, k * P:(k + 1) * P], ident[:])
                    last.then_inc(bank_full, 1)

                def output(u, pos, tile):
                    pe.wait_ge(attn_lo_ready, tile + 1)
                    out = begin(u.reuse(pos), pos)
                    for k in range(KB):
                        last = parts(out[:], attn_hi[:, k, :], attn_lo[:, k, :], wo_hi[:, k, :], wo_lo[:, k, :], k == 0, k == KB - 1)
                    last.then_inc(bank_full, 1)

                def weigh(u, s, tile, b, half):
                    who, count = u.emptied(s["PT"][2 * half + 1])
                    pe.wait_ge(freed[who], count)
                    if not (isinstance(tile, int) and tile == 0):
                        pe.wait_ge(normed, 2 * (tile - 1) + half + 1)
                    for h in range(HALF_HEADS):
                        last = nc.tensor.matmul(pv_ps[half][:, h * VW1:(h + 1) * VW1], probsT[:, half * HALF_HEADS + h, :],
                                                vals[:, b, half * HALF_HEADS + h, :], start=True, stop=True)
                    last.then_inc(pv_full, 1)

                def body(n, j):
                    u = Uses(n)
                    for t, s in enumerate(plan(n)):
                        tile = n * NT + t
                        b_before = batch(n) if t else batch(n - 1)
                        if t == 0:
                            pe.wait_ge(freed["dve"], PRE.count("dve") + KB * n)
                        for g in range(2):
                            if "PT" in s:
                                turn_probs(u, s, tile - 1, t - 1, g)
                            if t < NT:
                                scores(batch(n), tile, j, t, 2 + g)
                        if "OT" in s:
                            turn_attn(u, s["OT"][0], tile - 2)
                        if "PT" in s:
                            weigh(u, s, tile - 1, b_before, 0)
                            turn_probs(u, s, tile - 1, t - 1, 2)
                        if "Q" in s:
                            pe.wait_ge(x_lo_ready, NT * (n + 2))
                            project(begin(u.reuse(s["Q"][0]), s["Q"][0]), 1 - j, 2 * t)
                        if "PT" in s:
                            turn_probs(u, s, tile - 1, t - 1, 3)
                        if t < NT - 1:
                            for g in range(2):
                                scores(batch(n), tile + 1, j, t + 1, g)
                        elif left(n):
                            pe.wait_ge(freed["dve"], PRE.count("dve") + KB * n + KB // 2)
                            for g in range(2):
                                scores(batch(n + 1), tile + 1, 1 - j, 0, g)
                        if "Q" in s:
                            project(begin(u.reuse(s["Q"][1]), s["Q"][1]), 1 - j, 2 * t + 1)
                        if "PT" in s:
                            weigh(u, s, tile - 1, b_before, 1)
                        if "T" in s:
                            pe.wait_ge(xn_ready, tile + 2 * NT + 1)
                            turn_x(begin(u.reuse(s["T"][0]), s["T"][0]), t)
                        if "O" in s:
                            output(u, s["O"][0], tile - 2)

                all_chunks(pe, body)


EXPERTS = 8
SLOT_TILES = TILES + EXPERTS
MAP_ROWS = EXPERTS * TILES + EXPERTS
MAP = MAP_ROWS * P


def expert_stage(nc, io, xres, x_offset, ident, seen):
    G = 8
    LAG = 5
    assert EXPERTS == CHUNKS and TPC == KB
    with ExitStack() as stage:
        def sb(name, shape, dt=F32):
            return stage.enter_context(nc.sbuf_tensor("d_" + name, shape, dt))

        def sem(name):
            return stage.enter_context(nc.semaphore("d_" + name))

        we_offset = next_offset(nc)
        we = sb("we", [P, EXPERTS, KB, D])
        token_of = sb("token_of", [P, SLOT_TILES], U32)
        tile_expert = sb("tile_expert", [1, SLOT_TILES], U32)
        ld_we, ld_be = sem("ld_we"), sem("ld_be")
        rows_out = sem("rows_out")
        we_hi = nc.alloc_sbuf_tensor_at("d_we_hi", [P, EXPERTS, KB, ROW], F32R, offset=x_offset)[:, :, :, 0:D]
        we_lo = nc.alloc_sbuf_tensor_at("d_we_lo", [P, EXPERTS, KB, D], F32R, offset=we_offset)
        we_hi_ready, we_lo_ready = sem("we_hi"), sem("we_lo")
        place_step = sem("place_step")
        PLACE_STEPS, LAST_STEPS = 3, 15

        with ExitStack() as early:
            def esb(name, shape, dt=F32):
                return early.enter_context(nc.sbuf_tensor("d_" + name, shape, dt))

            def epb(name, shape, dt=F32):
                return early.enter_context(nc.psum_tensor("d_" + name, shape, dt))

            wg, wg_hi, wg_lo = esb("wg", [P, KB, D]), esb("wg_hi", [P, KB, D], F32R), esb("wg_lo", [P, KB, D], F32R)
            bg, bg_parts, ones_r = esb("bg", [P, D]), esb("bg_parts", [P, D], F32R), esb("ones_r", [P, P], F32R)
            upper_f, upper, ones = esb("upper_f", [P, P]), esb("upper", [P, P], BF16), esb("ones", [P, P], BF16)
            ones_f = esb("ones_f", [P, P])
            token_id = esb("token_id", [P, TPC])
            numbers = esb("numbers", [P, TPC, EXPERTS])
            base_f, base = esb("base_f", [P, TPC, EXPERTS]), esb("base", [P, TPC, EXPERTS], BF16)
            nobody = esb("nobody", [P, MAP_ROWS])
            slot_at = esb("slot_at", [SLOT_TILES, 1])
            prob, stats, mv = esb("prob", [P, TPC]), esb("stats", [P, TPC, 6]), esb("mv", [P, TPC, 2])
            minus_half, minus_one, shifted = esb("minus_half", [P, TPC]), esb("minus_one", [P, TPC]), esb("shifted", [P, 2, TPC])
            xn = esb("xn", [P, TPC, D])
            x_hi, x_lo = esb("x_hi", [P, 2, KB, CHUNK], F32R), esb("x_lo", [P, 2, KB, CHUNK], F32R)
            exped = esb("exped", [P, D])
            best, where = esb("best", [P, TPC, 8]), esb("where", [P, TPC, 8], U32)
            minus_best, total = esb("minus_best", [P, TPC]), esb("total", [P, TPC])
            held = esb("held", [P, 1])
            pool_held = esb("early_pool_held", [P, 3])
            expert_i, expert = esb("expert_i", [P, TPC], U32), esb("expert", [P, TPC])
            onehot = esb("onehot", [P, TPC, EXPERTS], BF16)
            earlier = esb("earlier", [P, TPC + 1, EXPERTS], BF16)
            rank = esb("rank", [P, TPC, EXPERTS])
            slot, slot_u, token = esb("slot", [P, TPC]), esb("slot_u", [P, 2, TPC], U32), esb("token", [P, 2, TPC])
            counts, padded, padded_i, end = esb("counts", [P, EXPERTS]), esb("padded", [P, EXPERTS]), esb("padded_i", [P, EXPERTS], I32), esb("end", [P, EXPERTS])
            passed, start_of = esb("passed", [SLOT_TILES, EXPERTS - 1]), esb("start_of", [SLOT_TILES, EXPERTS - 1])
            expert_of, start_at = esb("expert_of", [SLOT_TILES, 1]), esb("start_at", [SLOT_TILES, 1])
            map_row, map_row_u = esb("map_row", [SLOT_TILES, 1]), esb("map_row_u", [SLOT_TILES, 1], U32)
            owner = esb("owner", [SLOT_TILES, P])
            bank = [epb(f"bank{i}", [P, CHUNK]) for i in range(2)]
            logit_ps = epb("logit", [P, TPC, D])
            rank_ps = epb("rank_ps", [P, TPC * EXPERTS])
            owner_ps = epb("owner_ps", [P, 2, P])
            ld_small, ld_wg = sem("ld_small"), sem("ld_wg")
            half_ready, pad_set, wg_split = sem("half_ready"), sem("pad_set"), sem("wg_split")
            var_ready, rstd_ready, xn_ready = sem("var_ready"), sem("rstd_ready"), sem("xn_ready")
            turned, hi_ready, lo_ready = sem("turned"), sem("hi_ready"), sem("lo_ready")
            logit_full, best_ready, summed, row_ready = (sem(x) for x in ("logit_full", "best_ready", "summed", "row_ready"))
            map_cleared, hot_ready, ranked, slots_ready = (sem(x) for x in ("map_cleared", "hot_ready", "ranked", "slots_ready"))
            scattered = [sem("scattered0"), sem("scattered1")]
            early_held, rows_found, owner_loaded, owner_turned = sem("early_held"), sem("rows_found"), sem("owner_loaded"), sem("owner_turned")
            gate_step = sem("gate_step")
            HALF = P // 2
            TURNS = ((0, 1), (2,), (3,), ())
            LD_SMALL, PADS, NORM_STEPS, STEPS = 7 * 16, 7, TPC + 2, 3 * TPC + 9

            def pairs(eng, body):
                body(0, 0, True, False)
                body(1, 1, False, False)
                with eng.Fori(1, CHUNKS // 2 - 1) as i:
                    body(2 * i, 0, False, False)
                    body(2 * i + 1, 1, False, False)
                body(CHUNKS - 2, 0, False, False)
                body(CHUNKS - 1, 1, False, True)

            def more(n):
                return not isinstance(n, int) or n + 2 < CHUNKS

            with nc.Block() as block:
                @block.sync
                def _(sp):
                    sp.dma_start(wg[:], io["wg"].rearrange("(k p) n -> p k n", p=P)).then_inc(ld_wg, 16)
                    for tile, name in ((nobody, "nobody"), (upper_f, "upper"), (token_id, "token_id"), (numbers, "numbers"),
                                       (base_f, "map_base"), (slot_at, "slot_at")):
                        sp.dma_start(tile[:], io[name]).then_inc(ld_small, 16)
                    sp.dma_start(bg[:], io["bg"].partition_broadcast(P)).then_inc(ld_small, 16)
                    sp.wait_ge(ld_small, LD_SMALL)
                    sp.dma_start(io["owner"].rearrange("(p j) o -> p (j o)", p=P), nobody[:]).then_inc(map_cleared, 16)
                    for e in range(EXPERTS):
                        sp.dma_start(we[:, e], io["we"][e].rearrange("(k p) n -> p k n", p=P)).then_inc(ld_we, 16)
                    for n in range(CHUNKS):
                        if n >= 1:
                            sp.wait_ge(rows_out, 16 * n)
                        sp.wait_ge(row_ready, n + 1)
                        sp.dma_start(io["rows"][n * CHUNK:(n + 1) * CHUNK, :].rearrange("(t p) f -> p t f", p=P),
                                     xres[:, n * TPC:(n + 1) * TPC, :]).then_inc(rows_out, 16)
                    sp.wait_ge(rows_out, 16 * CHUNKS)

                @block.gpsimd
                def _(pool):
                    nc.gpsimd.memset(minus_half[:], -0.5).then_inc(half_ready, 1)
                    nc.gpsimd.memset(minus_one[:], -1.0).then_inc(half_ready, 1)
                    nc.gpsimd.memset(pool_held[:], 0.0).then_inc(early_held, 1)
                    pool.wait_ge(half_ready, 2)
                    pool.wait_ge(early_held, 1)

                    def spread(n, j):
                        pool.wait_ge(var_ready, n + 1)
                        at = bass.ds(n * TPC, TPC)
                        rstd = xres[:, at, COL_RSTD]
                        nc.gpsimd.tensor_tensor(rstd, rstd, minus_half[:], ALU.pow).then_inc(half_ready, 1)
                        pool.wait_ge(half_ready, 2 * n + 3)
                        nc.gpsimd.tensor_tensor(shifted[:, j], xres[:, at, COL_MEAN], rstd, ALU.mult).then_inc(half_ready, 1)
                        pool.wait_ge(half_ready, 2 * n + 4)
                        nc.gpsimd.tensor_tensor(xres[:, at, COL_SHIFT], shifted[:, j], minus_one[:], ALU.mult).then_inc(rstd_ready, 1)

                    def scatter(n, j, first):
                        pool.wait_ge(slots_ready, n + 1)
                        if first:
                            pool.wait_ge(map_cleared, 16)
                        else:
                            pool.wait_ge(scattered[1 - j], 16 * TPC * ((n - 1) // 2 + 1))
                        pool.wait_ge(early_held, n + 1)
                        nc.gpsimd.tensor_tensor(pool_held[:, 2:3], pool_held[:, 0:1], pool_held[:, 1:2], ALU.add).then_inc(early_held, 1)
                        for t in range(TPC):
                            nc.gpsimd.indirect_dma_start(out=io["owner"], out_offset=bass.IndirectOffsetOnAxis(ap=slot_u[:, j, t:t + 1], axis=0),
                                                         in_=token[:, j, t:t + 1], in_offset=None).then_inc(scattered[j], 16)

                    def body(n, j, first, last):
                        if more(n):
                            spread(n + 2, j)
                        if not first:
                            before = n - 1
                            scatter(before, 1 - j, isinstance(before, int) and before == 0)
                        if not isinstance(n, int) or n >= 2 and not last:
                            e = n - 2
                            pool.wait_ge(we_hi_ready, e + 1)
                            nc.gpsimd.tensor_tensor(we_lo[:, e], we[:, e], we_hi[:, e], ALU.subtract).then_inc(we_lo_ready, 1)

                    spread(0, 0)
                    spread(1, 1)
                    pairs(pool, body)
                    scatter(CHUNKS - 1, 1, False)
                    for j in range(2):
                        pool.wait_ge(scattered[j], 16 * TILES // 2)
                    pool.wait_ge(rows_found, 1)
                    nc.gpsimd.indirect_dma_start(out=owner[:], out_offset=None, in_=io["owner"].rearrange("(j p) o -> j (p o)", p=P),
                                                 in_offset=bass.IndirectOffsetOnAxis(ap=map_row_u[:], axis=0)).then_inc(owner_loaded, 16)
                    pool.wait_ge(owner_loaded, 16)

                @block.scalar
                def _(act):
                    def norm_rows(n, j):
                        act.wait_ge(rstd_ready, n + 1)
                        for t in range(TPC):
                            at = n * TPC + t
                            nc.scalar.activation(xn[:, t, :], xres[:, at, 0:D], ACT.Identity, bias=xres[:, at, COL_SHIFT:COL_SHIFT + 1],
                                                 scale=xres[:, at, COL_RSTD:COL_RSTD + 1]).then_inc(xn_ready, 1)

                    def take_hi(n, j, k):
                        act.wait_ge(turned, KB * n + k + 1)
                        nc.scalar.copy(x_hi[:, j, k, :], bank[k % 2][:]).then_inc(hi_ready, 1)

                    norm_rows(0, 0)
                    act.wait_ge(ld_wg, 16)
                    nc.scalar.copy(wg_hi[:], wg[:]).then_inc(wg_split, 1)
                    for k in range(KB):
                        take_hi(0, 0, k)
                    norm_rows(1, 1)

                    def expert_hi(e):
                        act.wait_ge(rows_out, 16 * (e + 1))
                        nc.scalar.copy(we_hi[:, e], we[:, e]).then_inc(we_hi_ready, 1)

                    def body(n, j, first, last):
                        if isinstance(n, int) and n == 1:
                            act.wait_ge(ld_we, 16 * EXPERTS)
                        for t in range(TPC):
                            tile = n * TPC + t
                            if not last:
                                for k in TURNS[t]:
                                    take_hi(n + 1, 1 - j, k)
                            if t == TPC - 1 and more(n):
                                norm_rows(n + 2, j)
                            act.wait_ge(best_ready, tile + 1)
                            if not first or t:
                                act.wait_ge(summed, tile)
                            nc.scalar.activation(exped[:], logit_ps[:, t, :], ACT.Exp, bias=minus_best[:, t:t + 1],
                                                 accum_out=total[:, t:t + 1]).then_inc(summed, 1)
                        if not first:
                            expert_hi(n - 1)

                    pairs(act, body)
                    expert_hi(EXPERTS - 1)

                @block.vector
                def _(dve):
                    ch = Chain(dve, gate_step)
                    ch.step(nc.vector.memset(ones_f[:], 1.0))
                    nc.vector.memset(ones[:], 1.0).then_inc(pad_set, 1)
                    nc.vector.memset(earlier[:], 0.0).then_inc(pad_set, 1)

                    def norm_stats(n):
                        ch.step(nc.vector.tensor_copy(stats[:], seen.stats[:, bass.ds(n * TPC, TPC), :]))
                        ch.wait()
                        nc.vector.memset(held[:], 0.0)
                        for t in range(TPC):
                            ch.step(nc.vector.bn_aggr(mv[:, t, :], stats[:, t, :]))
                        ch.wait()
                        ch.step(nc.vector.tensor_copy(xres[:, bass.ds(n * TPC, TPC), COL_MEAN:COL_RSTD + 1], mv[:]))
                        ch.wait()
                        variance = xres[:, bass.ds(n * TPC, TPC), COL_RSTD]
                        nc.vector.tensor_scalar(variance, variance, LN_EPS, None, ALU.add).then_inc(var_ready, 1)

                    def take_lo(n, j, k):
                        dve.wait_ge(hi_ready, KB * n + k + 1)
                        nc.vector.tensor_tensor(x_lo[:, j, k, :], bank[k % 2][:], x_hi[:, j, k, :], ALU.subtract).then_inc(lo_ready, 1)

                    norm_stats(0)
                    norm_stats(1)
                    dve.wait_ge(ld_small, LD_SMALL)
                    ch.wait()
                    nc.vector.tensor_copy(ones_r[:], ones_f[:]).then_inc(pad_set, 1)
                    ch.step(nc.vector.tensor_copy(bg_parts[:], bg[:]))
                    ch.wait()
                    ch.step(nc.vector.tensor_tensor(bg[:], bg[:], bg_parts[:], ALU.subtract))
                    ch.wait()
                    nc.vector.tensor_scalar(bg_parts[0:HALF], bg_parts[0:HALF], 1.0 / HALF, None, ALU.mult).then_inc(pad_set, 1)
                    nc.vector.tensor_scalar(bg_parts[HALF:P], bg[HALF:P], 1.0 / HALF, None, ALU.mult).then_inc(pad_set, 1)
                    nc.vector.tensor_copy(upper[:], upper_f[:]).then_inc(pad_set, 1)
                    nc.vector.tensor_copy(base[:], base_f[:]).then_inc(pad_set, 1)
                    ch.step(nc.vector.tensor_scalar(token[:, 1, :], token_id[:], -float(CHUNK), None, ALU.add))
                    for k in range(KB):
                        if k == 2:
                            dve.wait_ge(wg_split, 1)
                            nc.vector.tensor_tensor(wg_lo[:], wg[:], wg_hi[:], ALU.subtract).then_inc(wg_split, 1)
                        take_lo(0, 0, k)
                    start = ch.k

                    def places(n, j):
                        pl = Chain(dve, place_step, PLACE_STEPS * n)
                        dve.wait_ge(early_held, n + 1)
                        pl.step(nc.vector.tensor_scalar(token[:, j, :], token[:, 1 - j, :], float(CHUNK), None, ALU.add))
                        dve.wait_ge(ranked, n + 1)
                        pl.step(nc.vector.tensor_tensor(rank[:], rank_ps[:].rearrange("p (t e) -> p t e", e=EXPERTS), onehot[:], ALU.mult))
                        pl.wait()
                        pl.step(nc.vector.tensor_reduce(slot[:], rank[:], AX.X, ALU.add))
                        pl.wait()
                        nc.vector.tensor_copy(slot_u[:, j, :], slot[:]).then_inc(slots_ready, 1)
                        assert pl.k == PLACE_STEPS

                    def body(n, j, first, last):
                        ch.base, ch.k = start + STEPS * n - (NORM_STEPS if last else 0), 0
                        for t in range(TPC):
                            tile = n * TPC + t
                            dve.wait_ge(logit_full, tile + 1)
                            nc.vector.memset(held[:], 0.0)
                            ch.step(nc.vector.max(best[:, t, :], logit_ps[:, t, :]))
                            ch.wait()
                            ch.step(nc.vector.tensor_scalar(minus_best[:, t:t + 1], best[:, t, 0:1], -1.0, None, ALU.mult))
                            nc.vector.max_index(where[:, t, :], best[:, t, :], logit_ps[:, t, :]).then_inc(best_ready, 1)
                            if not last:
                                for k in TURNS[t]:
                                    take_lo(n + 1, 1 - j, k)
                            if t == 0 and more(n):
                                norm_stats(n + 2)
                            if t == 1 and not first:
                                places(n - 1, 1 - j)
                        dve.wait_ge(best_ready, TPC * (n + 1))
                        ch.step(nc.vector.tensor_scalar(expert_i[:], where[:, :, 0], EXPERTS - 1, None, ALU.bitwise_and))
                        ch.wait()
                        ch.step(nc.vector.tensor_copy(expert[:], expert_i[:]))
                        if not first:
                            dve.wait_ge(ranked, n)
                            nc.vector.tensor_copy(earlier[:, 0, :], earlier[:, TPC, :]).then_inc(pad_set, 1)
                            dve.wait_ge(pad_set, PADS + n)
                        ch.wait()
                        ch.step(nc.vector.tensor_tensor(onehot[:], numbers[:], expert[:].unsqueeze(2).to_broadcast([P, TPC, EXPERTS]), ALU.is_equal))
                        for t in range(TPC):
                            ch.wait()
                            add = nc.vector.tensor_tensor(earlier[:, t + 1, :], earlier[:, t, :], onehot[:, t, :], ALU.add)
                            if t < TPC - 1:
                                ch.step(add)
                        add.then_inc(hot_ready, 1)
                        dve.wait_ge(summed, TPC * (n + 1))
                        ch.step(nc.vector.reciprocal(prob[:], total[:]))
                        ch.wait()
                        nc.vector.tensor_copy(xres[:, bass.ds(n * TPC, TPC), COL_P], prob[:]).then_inc(row_ready, 1)
                        dve.wait_ge(row_ready, n + 1)
                        assert ch.k == STEPS - (0 if more(n) else NORM_STEPS), ch.k

                    pairs(dve, body)
                    places(CHUNKS - 1, 1)

                    ch = Chain(dve, place_step, PLACE_STEPS * CHUNKS)
                    dve.wait_ge(ranked, CHUNKS + 1)
                    ch.step(nc.vector.tensor_copy(counts[:], owner_ps[:, 1, HALF:HALF + EXPERTS]))
                    ch.wait()
                    ch.step(nc.vector.tensor_scalar(padded[:], counts[:], float(P - 1), None, ALU.add))
                    ch.wait()
                    ch.step(nc.vector.tensor_copy(padded_i[:], padded[:]))
                    ch.wait()
                    ch.step(nc.vector.tensor_scalar(padded_i[:], padded_i[:], 7, 7, ALU.arith_shift_right, ALU.logical_shift_left))
                    ch.wait()
                    ch.step(nc.vector.tensor_copy(padded[:], padded_i[:]))
                    ch.wait()
                    ch.step(nc.vector.tensor_tensor_scan(end[:], ones_f[:, 0:EXPERTS], padded[:], 0.0, ALU.mult, ALU.add))
                    ch.wait()
                    ends = end[0:SLOT_TILES, 0:EXPERTS - 1]
                    ch.step(nc.vector.tensor_scalar(passed[:], ends, slot_at[:], None, ALU.is_le))
                    ch.wait()
                    ch.step(nc.vector.tensor_reduce(expert_of[:], passed[:], AX.X, ALU.add))
                    ch.step(nc.vector.tensor_tensor(start_of[:], passed[:], ends, ALU.mult))
                    ch.wait()
                    ch.step(nc.vector.tensor_reduce(start_at[:], start_of[:], AX.X, ALU.max))
                    ch.wait()
                    ch.step(nc.vector.tensor_tensor(start_at[:], slot_at[:], start_at[:], ALU.subtract))
                    ch.step(nc.vector.tensor_scalar(map_row[:], expert_of[:], float(TILES), None, ALU.mult))
                    ch.wait()
                    ch.step(nc.vector.scalar_tensor_tensor(map_row[:], start_at[:], 1.0 / P, map_row[:], ALU.mult, ALU.add))
                    ch.wait()
                    nc.vector.tensor_copy(map_row_u[:], map_row[:]).then_inc(rows_found, 1)
                    for e in range(EXPERTS - 3, EXPERTS):
                        dve.wait_ge(we_hi_ready, e + 1)
                        nc.vector.tensor_tensor(we_lo[:, e], we[:, e], we_hi[:, e], ALU.subtract).then_inc(we_lo_ready, 1)
                    dve.wait_ge(owner_turned, 2)
                    ch.step(nc.vector.tensor_copy(tile_expert[:], owner_ps[0:1, 1, 0:SLOT_TILES]))
                    ch.step(nc.vector.tensor_copy(token_of[:], owner_ps[:, 0, 0:SLOT_TILES]))
                    assert ch.k == LAST_STEPS, ch.k

                @block.tensor
                def _(pe):
                    def turn(n, k, first=False):
                        if not first or k >= 2:
                            pe.wait_ge(lo_ready, KB * n + k - 1)
                        for t in range(TPC):
                            last = nc.tensor.transpose(bank[k % 2][:, t * P:(t + 1) * P], xn[:, t, k * P:(k + 1) * P], ident[:])
                        last.then_inc(turned, 1)

                    pe.wait_ge(xn_ready, TPC)
                    for k in range(KB):
                        turn(0, k, True)
                    pe.wait_ge(wg_split, 2)
                    pe.wait_ge(pad_set, PADS)

                    def rank_rows(n):
                        pe.wait_ge(hot_ready, n + 1)
                        hot = onehot[:].rearrange("p t e -> p (t e)")
                        nc.tensor.matmul(rank_ps[:], upper[:], hot, start=True, stop=False)
                        nc.tensor.matmul(rank_ps[:], ones[:], earlier[:, 0:TPC, :].rearrange("p t e -> p (t e)"), start=False, stop=False)
                        nc.tensor.matmul(rank_ps[:], ones[:], base[:].rearrange("p t e -> p (t e)"), start=False, stop=True).then_inc(ranked, 1)

                    def body(n, j, first, last):
                        pe.wait_ge(lo_ready, KB * (n + 1))
                        for t in range(TPC):
                            tile = n * TPC + t
                            if not first:
                                pe.wait_ge(summed, tile - 3)
                            out = logit_ps[:, t, :]
                            nc.tensor.matmul(out, ones_r[:], bg_parts[:], start=True, stop=False)
                            for k in range(KB):
                                hi, lo = (x[:, j, k, t * P:(t + 1) * P] for x in (x_hi, x_lo))
                                nc.tensor.matmul(out, hi, wg_hi[:, k, :], start=False, stop=False)
                                nc.tensor.matmul(out, hi, wg_lo[:, k, :], start=False, stop=False)
                                ins = nc.tensor.matmul(out, lo, wg_hi[:, k, :], start=False, stop=(k == KB - 1))
                            ins.then_inc(logit_full, 1)
                            if not last:
                                pe.wait_ge(xn_ready, TPC * (n + 2))
                                for k in TURNS[t]:
                                    turn(n + 1, k)
                            if t == 0 and not first:
                                rank_rows(n - 1)

                    pairs(pe, body)
                    rank_rows(CHUNKS - 1)
                    nc.tensor.matmul(owner_ps[:, 1, HALF:HALF + EXPERTS], ones[:], earlier[:, TPC, :], start=True, stop=True).then_inc(ranked, 1)
                    pe.wait_ge(rows_found, 1)
                    nc.tensor.transpose(owner_ps[0:1, 1, 0:SLOT_TILES], expert_of[:], ident[0:SLOT_TILES, 0:SLOT_TILES]).then_inc(owner_turned, 1)
                    pe.wait_ge(owner_loaded, 16)
                    nc.tensor.transpose(owner_ps[:, 0, 0:SLOT_TILES], owner[:], ident[0:SLOT_TILES, 0:SLOT_TILES]).then_inc(owner_turned, 1)

        with ExitStack() as late:
            def lsb(name, shape, dt=F32):
                return late.enter_context(nc.sbuf_tensor("d_" + name, shape, dt))

            held = lsb("pool_held", [P, 3])
            be = lsb("be", [P, EXPERTS, D])
            got = [lsb(f"got{i}", [P, ROW]) for i in range(G)]
            token = [lsb(f"token{i}", [P, 1], U32) for i in range(G)]
            xn = lsb("slot_xn", [P, 2, D])
            xT_hi, xT_lo = (lsb("slot_xT_" + x, [P, 2, KB, P], F32R) for x in ("hi", "lo"))
            y = [lsb(f"y{i}", [P, D]) for i in range(G)]
            turn_ps = late.enter_context(nc.psum_tensor("d_turn", [P, 2, D], F32))
            y_ps = late.enter_context(nc.psum_tensor("d_y", [P, 2, D], F32))
            got_clear, token_ready, held_set = sem("got_clear"), sem("token_ready"), sem("held_set")
            gathered = [sem(f"gathered{i}") for i in range(G)]
            stored = [sem(f"stored{i}") for i in range(G)]
            xn_ready, turned, hi_ready, lo_ready, y_full, y_used, y_ready = (sem("slot_" + x) for x in ("xn", "turned", "hi", "lo", "y_full", "y_used", "y_ready"))
            ROUNDS = SLOT_TILES // G

            def rounds(eng, body):
                for u in range(G):
                    body(u, 0, u, True, False)
                with eng.Fori(1, ROUNDS - 1) as i:
                    for u in range(G):
                        body(G * i + u, i, u, False, False)
                for u in range(G):
                    body(SLOT_TILES - G + u, ROUNDS - 1, u, False, True)

            with nc.Block() as block:
                @block.sync
                def _(sp):
                    sp.wait_ge(gathered[3], 16)
                    sp.dma_start(be[:].rearrange("p e n -> p (e n)"), io["be"].partition_broadcast(P)).then_inc(ld_be, 16)

                @block.gpsimd
                def _(pool):
                    nc.gpsimd.memset(held[:], 0.0).then_inc(held_set, 1)

                    def hold(before):
                        pool.wait_ge(held_set, 1 + before)
                        nc.gpsimd.tensor_tensor(held[:, 2:3], held[:, 0:1], held[:, 1:2], ALU.add).then_inc(held_set, 1)

                    def gather(i, u, before):
                        pool.wait_ge(token_ready, G * i + u + 1)
                        hold(before)
                        nc.gpsimd.indirect_dma_start(out=got[u][:], out_offset=None, in_=io["rows"],
                                                     in_offset=bass.IndirectOffsetOnAxis(ap=token[u][:], axis=0),
                                                     bounds_check=TOK - 1, oob_is_err=False).then_inc(gathered[u], 16)

                    def scatter(j, u, before):
                        pool.wait_ge(y_ready, j + 1)
                        hold(before)
                        nc.gpsimd.indirect_dma_start(out=io["out"], out_offset=bass.IndirectOffsetOnAxis(ap=token[u][:], axis=0),
                                                     in_=y[u][:], in_offset=None, bounds_check=TOK - 1,
                                                     oob_is_err=False).then_inc(stored[u], 16)

                    for u in range(G):
                        pool.wait_ge(got_clear, u + 1)
                        gather(0, u, u)

                    def body(j, i, u, first, last):
                        more = SLOT_TILES - G if last and u >= LAG else 0 if first and u < LAG else j - LAG
                        if not (first and u < 2):
                            scatter(j - 2, (u - 2) % G, G + j - 2 + more)
                        if u >= LAG and not last:
                            gather(i + 1, u - LAG, G + j - 1 + more)
                        elif u < LAG and not first:
                            gather(i, u - LAG + G, G + j - 1 + more)

                    rounds(pool, body)
                    for j in (SLOT_TILES - 2, SLOT_TILES - 1):
                        scatter(j, j % G, SLOT_TILES + j)
                    for u in range(G):
                        pool.wait_ge(stored[u], 16 * ROUNDS)

                @block.scalar
                def _(act):
                    def norm(j, i, u, first):
                        act.wait_ge(gathered[u], 16 * (i + 1))
                        if not first or u >= 2:
                            act.wait_ge(turned, j - 1)
                        nc.scalar.activation(xn[:, u % 2, :], got[u][:, 0:D], ACT.Identity, bias=got[u][:, COL_SHIFT:COL_SHIFT + 1],
                                             scale=got[u][:, COL_RSTD:COL_RSTD + 1]).then_inc(xn_ready, 1)

                    def take_hi(j, par):
                        act.wait_ge(turned, j + 1)
                        if not (isinstance(j, int) and j < 2):
                            act.wait_ge(y_full, j - 1)
                        nc.scalar.copy(xT_hi[:, par].rearrange("p k t -> p (k t)"), turn_ps[:, par, :]).then_inc(hi_ready, 1)

                    def body(j, i, u, first, last):
                        norm(j, i, u, first)
                        if not (first and u == 0):
                            take_hi(j - 1, (u - 1) % 2)

                    rounds(act, body)
                    take_hi(SLOT_TILES - 1, (SLOT_TILES - 1) % 2)

                @block.vector
                def _(dve):
                    ch = Chain(dve, place_step)
                    for u in range(G):
                        nc.vector.memset(got[u][:], 0.0).then_inc(got_clear, 1)
                        nc.vector.tensor_copy(token[u][:], token_of[:, u:u + 1]).then_inc(token_ready, 1)
                    def take_lo(j, par):
                        dve.wait_ge(hi_ready, j + 1)
                        if not (isinstance(j, int) and j < 2):
                            dve.wait_ge(y_full, j - 1)
                        nc.vector.tensor_tensor(xT_lo[:, par].rearrange("p k t -> p (k t)"), turn_ps[:, par, :],
                                                xT_hi[:, par].rearrange("p k t -> p (k t)"), ALU.subtract).then_inc(lo_ready, 1)

                    def finish(j, u):
                        expert = dve.value_load(tile_expert[0:1, bass.ds(j, 1)], min_val=0, max_val=EXPERTS - 1)
                        if isinstance(j, int) and j == 0:
                            dve.wait_ge(ld_be, 16)
                        dve.wait_ge(y_full, j + 1)
                        nc.vector.tensor_tensor(y[u][:], y_ps[:, u % 2, :], be[:, expert, :], ALU.add).then_inc(y_used, 1)
                        dve.wait_ge(y_used, j + 1)
                        ch.base, ch.k = PLACE_STEPS * CHUNKS + LAST_STEPS + j, 0
                        ch.step(nc.vector.tensor_scalar(y[u][:], y[u][:], 0.0, got[u][:, COL_P:COL_P + 1], ALU.max, ALU.mult))
                        ch.wait()
                        nc.vector.tensor_tensor(y[u][:], y[u][:], got[u][:, 0:D], ALU.add).then_inc(y_ready, 1)

                    def next_token(j, i, u):
                        dve.wait_ge(stored[u], 16 * (i + 1))
                        nc.vector.tensor_copy(token[u][:], token_of[:, bass.ds(j + G, 1)]).then_inc(token_ready, 1)

                    def body(j, i, u, first, last):
                        if not (first and u == 0):
                            take_lo(j - 1, (u - 1) % 2)
                        if not (first and u < 2):
                            finish(j - 2, (u - 2) % G)
                        if u >= LAG and not last:
                            next_token(j - LAG, i, u - LAG)
                        elif u < LAG and not first:
                            next_token(j - LAG, i - 1, u - LAG + G)

                    rounds(dve, body)
                    take_lo(SLOT_TILES - 1, (SLOT_TILES - 1) % 2)
                    finish(SLOT_TILES - 2, G - 2)
                    finish(SLOT_TILES - 1, G - 1)

                @block.tensor
                def _(pe):
                    def turn(j, i, u, first):
                        pe.wait_ge(xn_ready, j + 1)
                        if not first or u >= 2:
                            pe.wait_ge(lo_ready, j - 1)
                        for k in range(KB):
                            last = nc.tensor.transpose(turn_ps[:, u % 2, k * P:(k + 1) * P], xn[:, u % 2, k * P:(k + 1) * P], ident[:])
                        last.then_inc(turned, 1)

                    def product(j, par):
                        expert = pe.value_load(tile_expert[0:1, bass.ds(j, 1)], min_val=0, max_val=EXPERTS - 1)
                        pe.wait_ge(lo_ready, j + 1)
                        if isinstance(j, int) and j == 0:
                            pe.wait_ge(we_lo_ready, EXPERTS)
                        if not (isinstance(j, int) and j < 2):
                            pe.wait_ge(y_used, j - 1)
                        for k in range(KB):
                            hi, lo = xT_hi[:, par, k, :], xT_lo[:, par, k, :]
                            nc.tensor.matmul(y_ps[:, par, :], hi, we_hi[:, expert, k, :], start=(k == 0), stop=False)
                            nc.tensor.matmul(y_ps[:, par, :], hi, we_lo[:, expert, k, :], start=False, stop=False)
                            last = nc.tensor.matmul(y_ps[:, par, :], lo, we_hi[:, expert, k, :], start=False, stop=(k == KB - 1))
                        last.then_inc(y_full, 1)

                    def body(j, i, u, first, last):
                        turn(j, i, u, first)
                        if not (first and u == 0):
                            product(j - 1, (u - 1) % 2)

                    rounds(pe, body)
                    product(SLOT_TILES - 1, (SLOT_TILES - 1) % 2)


def build_program(nc, io):
    with ExitStack() as whole:
        x_offset = next_offset(nc)
        xres = whole.enter_context(nc.sbuf_tensor("xres", [P, TILES, ROW], F32))
        ident = whole.enter_context(nc.sbuf_tensor("ident", [P, P], F32))
        seen = Seen(nc, whole)
        ahead = Ahead(nc, whole)
        rope_attention_stage(nc, io, xres, ident, seen, ahead)
        quantised_ffn_stage(nc, io, xres, ident, seen, ahead)
        masked_attention_stage(nc, io, xres, ident, seen)
        expert_stage(nc, io, xres, x_offset, ident, seen)


def shape_constants():
    import numpy as np

    freq = np.float32(1) / (10000.0 ** (np.arange(0, DH0, 2) / DH0)).astype(np.float32)
    angle = np.arange(S, dtype=np.float32)[:, None] * freq[None, :]
    cos = np.repeat(np.cos(angle), 2, axis=1).T
    sin = np.repeat(np.sin(angle), 2, axis=1).T * np.tile(np.array([-1, 1], np.float32), DH0 // 2)[:, None]
    rot = np.stack([np.tile(cos, (2, 1)), np.tile(sin, (2, 1))], axis=1)
    at = np.arange(P)
    causal = np.ones((P, 2, KEYS), np.float32)
    causal[:, 0, :] = at[:, None] <= at[None, :]
    return {
        "ident": np.eye(P, dtype=np.float32),
        "rot": np.ascontiguousarray(rot, np.float32),
        "causal": causal,
        "upper": (at[:, None] < at[None, :]).astype(np.float32),
        "token_id": (P * np.arange(TPC, dtype=np.float32)[None, :] + at[:, None].astype(np.float32)),
        "numbers": np.broadcast_to(np.arange(EXPERTS, dtype=np.float32), (P, TPC, EXPERTS)),
        "map_base": (at[:, None, None] == 0) * np.broadcast_to(TOK * np.arange(EXPERTS, dtype=np.float32), (P, TPC, EXPERTS)).astype(np.float32),
        "slot_at": (P * np.arange(SLOT_TILES, dtype=np.float32))[:, None],
        "nobody": np.full((P, MAP_ROWS), TOK, np.float32),
    }


def kernel(x, ctx_1024, mask_BxS2_bf0, mask_1x1xSxS2_bk0, L0_xattn_Wq, L0_xattn_Wk, L0_xattn_Wv, L0_xattn_Wo, L0_xattn_ln_g,
           L0_xattn_ln_b, L0_ffn_clip_x, L0_ffn_clip_down, L0_ffn_w_gate, L0_ffn_w_up, L0_ffn_w_down, L1_xattn_Wq, L1_xattn_bq,
           L1_xattn_Wk, L1_xattn_bk, L1_xattn_Wv, L1_xattn_bv, L1_xattn_Wo, L1_xattn_bo, L1_ffn_Wg, L1_ffn_bg, L1_ffn_We,
           L1_ffn_be):
    import numpy as np
    import concourse.bacc as bacc
    from concourse.bass_utils import run_bass_kernel_spmd

    def columns(v):
        return np.asarray(v).reshape(KB, P).T

    def row(v):
        return np.asarray(v).reshape(1, -1)

    laid_out = {
        "x": np.asarray(x).reshape(TOK, D),
        "ctx": np.asarray(ctx_1024).reshape(B * KEYS, D),
        "pad": np.asarray(mask_BxS2_bf0).T,
        "mask": np.asarray(mask_1x1xSxS2_bk0).reshape(S, KEYS),
        "ln_g": columns(L0_xattn_ln_g), "ln_b": columns(L0_xattn_ln_b),
        "wq0": L0_xattn_Wq, "wk0": L0_xattn_Wk, "wv0": L0_xattn_Wv, "wo0": L0_xattn_Wo,
        "clip": np.concatenate([row(L0_ffn_clip_x), row(L0_ffn_clip_down)], axis=1),
        "w_gate": L0_ffn_w_gate, "w_up": L0_ffn_w_up, "w_down": L0_ffn_w_down,
        "wq1": np.asarray(L1_xattn_Wq).T, "wk1": np.asarray(L1_xattn_Wk).T,
        "wv1": np.asarray(L1_xattn_Wv).T, "wo1": np.asarray(L1_xattn_Wo).T,
        "qk_bias": np.stack([columns(L1_xattn_bq), columns(L1_xattn_bk)], axis=1),
        "bv": row(L1_xattn_bv), "bo": row(L1_xattn_bo),
        "wg": L1_ffn_Wg, "bg": row(L1_ffn_bg), "we": L1_ffn_We, "be": row(L1_ffn_be),
        **shape_constants(),
    }
    nc = bacc.Bacc("TRN2", target_bir_lowering=False, num_devices=1)
    arrays, io = {}, {}
    for name, value in laid_out.items():
        a = np.ascontiguousarray(value)
        arrays[f"in_{name}"] = a
        io[name] = nc.dram_tensor(f"in_{name}", a.shape, mybir.dt.from_np(a.dtype), kind="ExternalInput").ap()
    io["hidden"] = nc.dram_tensor("hidden", [CHUNKS, P, IT * CHUNK], F32).ap()
    io["rows"] = nc.dram_tensor("rows", [TOK, ROW], F32).ap()
    io["owner"] = nc.dram_tensor("owner", [MAP, 1], F32).ap()
    io["out"] = nc.dram_tensor("out", [TOK, D], F32, kind="ExternalOutput").ap()
    build_program(nc, io)
    got = run_bass_kernel_spmd(nc, [arrays], core_ids=[0])
    return got.results[0]["out"].reshape(B, S, D)
```
